# Optimizing a Trainium2 kernel written in Bass

```python
import numpy as np
import jax
import jax.numpy as jnp

def _softmax(x, axis=-1):
    return jax.nn.softmax(x, axis=axis)

def _gelu(x):
    return jax.nn.gelu(x, approximate=True)

def _silu(x):
    return jax.nn.silu(x)

def _sigmoid(x):
    return jax.nn.sigmoid(x)

def _layernorm(x, axis=-1, eps=1e-05):
    m = jnp.mean(x, axis=axis, keepdims=True)
    v = jnp.var(x, axis=axis, keepdims=True)
    return (x - m) / jnp.sqrt(v + eps)

def _scatter_add(tgt, idx, src, axis=0):
    return tgt.at[idx].add(src)

def _segment_sum(src, seg, n):
    return jax.ops.segment_sum(src, seg, n)
kernel_name = 'mk_metaformer_d2_conv_nchw128_r4_c515b0'

def setup_inputs(seed: int=0):
    np.random.seed(seed)
    _w = jnp.asarray

    def _rec_inputs():
        import jax
        import jax.numpy as jnp
        _gk = jax.random.key(seed)
        x = -0.0003598 + 1 * jax.random.normal(jax.random.fold_in(_gk, 1), (4, 32, 28, 28), jnp.float32)
        return x
    x = _rec_inputs()

    def _L0_conv_setup():
        import jax, jax.numpy as jnp
        import numpy as np

        def conv2d(x, w, stride=1, padding=0):
            return jax.lax.conv_general_dilated(x, w, window_strides=(stride, stride), padding=[(padding, padding), (padding, padding)], dimension_numbers=('NCHW', 'OIHW', 'NCHW'))

        def adder2d(x, w, stride=1, padding=0):
            N, Ci, H, W = x.shape
            Co, _, K, _ = w.shape
            xp = jnp.pad(x, ((0, 0), (0, 0), (padding, padding), (padding, padding)))
            Ho = (H + 2 * padding - K) // stride + 1
            Wo = (W + 2 * padding - K) // stride + 1
            acc = jnp.zeros((N, Co, Ho, Wo), x.dtype)
            for kh in range(K):
                for kw in range(K):
                    xs = xp[:, :, kh:kh + Ho * stride:stride, kw:kw + Wo * stride:stride]
                    diff = jnp.abs(xs[:, None] - w[None, :, :, kh, kw, None, None])
                    acc = acc - diff.sum(axis=2)
            return acc

        def batchnorm(x, gamma, beta, mean, var, eps=1e-05):
            inv = gamma / jnp.sqrt(var + eps)
            return x * inv[None, :, None, None] + (beta - mean * inv)[None, :, None, None]
        key = jax.random.key(seed)
        ks = jax.random.split(key, 16)
        N, C, H, W = (4, 32, 28, 28)
        inp = {'x': jax.random.normal(ks[0], (N, C, H, W), jnp.float32), 'w_shift1': jax.random.normal(ks[1], (C, C, 1, 1), jnp.float32) * 0.1, 'w_add1': jax.random.normal(ks[2], (C, C, 1, 1), jnp.float32) * 0.1, 'bn1_gamma': jax.random.uniform(ks[3], (C,), jnp.float32, 0.5, 1.5), 'bn1_beta': jax.random.normal(ks[4], (C,), jnp.float32) * 0.1, 'bn1_mean': jax.random.normal(ks[5], (C,), jnp.float32), 'bn1_var': jax.random.uniform(ks[6], (C,), jnp.float32, 0.5, 1.5), 'w_shift2': jax.random.normal(ks[7], (C, C, 3, 3), jnp.float32) * 0.05, 'w_add2': jax.random.normal(ks[8], (C, C, 3, 3), jnp.float32) * 0.05, 'bn2_gamma': jax.random.uniform(ks[9], (C,), jnp.float32, 0.5, 1.5), 'bn2_beta': jax.random.normal(ks[10], (C,), jnp.float32) * 0.1, 'bn2_mean': jax.random.normal(ks[11], (C,), jnp.float32), 'bn2_var': jax.random.uniform(ks[12], (C,), jnp.float32, 0.5, 1.5)}
        return inp
    _L0_conv_all = _L0_conv_setup()
    _L0_conv_in = {k: v for k, v in _L0_conv_all.items() if k in ('w_shift1', 'w_add1', 'bn1_gamma', 'bn1_beta', 'bn1_mean', 'bn1_var', 'w_shift2', 'w_add2', 'bn2_gamma', 'bn2_beta', 'bn2_mean', 'bn2_var')}
    del _L0_conv_all

    def _L0_ffn_setup():
        import jax, jax.numpy as jnp
        import numpy as np
        NB, NOPS = (33, 19)
        D, H = (32, 128)
        B, S = (8, 256)
        CARRY_OPS = [0, 1, 2, 10, 11, 12, 13]

        def _build_masks():
            am = np.zeros((NB, NOPS), dtype=bool)
            fm = np.zeros((NB, NOPS), dtype=bool)
            fm[0, :] = True
            for b in range(1, 8):
                am[b, CARRY_OPS] = True
                fm[b, CARRY_OPS] = True
            am[8, [14, 15, 8, 9]] = True
            fm[8, [14, 15, 8, 9]] = True
            for b in range(16, 32):
                fm[b, [3, 4]] = True
            am[32, [10, 11, 12, 13]] = True
            fm[32, [5, 6, 7, 2, 4, 10, 11, 12, 13]] = True
            return (jnp.asarray(am), jnp.asarray(fm))
        key = jax.random.key(seed)
        ks = jax.random.split(key, 9)
        sd = 1.0 / np.sqrt(D)
        sh = 1.0 / np.sqrt(H)
        am, fm = _build_masks()
        return {'x': jax.random.normal(ks[0], (B, S, D), jnp.float32), 'ffn_w1': jax.random.normal(ks[1], (NB, NOPS, D, H), jnp.float32) * sd, 'ffn_b1': jnp.zeros((NB, NOPS, H), jnp.float32), 'ffn_w2': jax.random.normal(ks[2], (NB, NOPS, H, D), jnp.float32) * sh, 'ffn_b2': jnp.zeros((NB, NOPS, D), jnp.float32), 'wq': jax.random.normal(ks[3], (NB, NOPS, D, D), jnp.float32) * sd, 'wk': jax.random.normal(ks[4], (NB, NOPS, D, D), jnp.float32) * sd, 'wv': jax.random.normal(ks[5], (NB, NOPS, D, D), jnp.float32) * sd, 'wo': jax.random.normal(ks[6], (NB, NOPS, D, D), jnp.float32) * sd, 'attn_mask': am, 'ffn_mask': fm}
    _L0_ffn_all = _L0_ffn_setup()
    _L0_ffn_in = {k: v for k, v in _L0_ffn_all.items() if k in ('ffn_w1', 'ffn_b1', 'ffn_w2', 'ffn_b2', 'wq', 'wk', 'wv', 'wo', 'attn_mask', 'ffn_mask')}
    del _L0_ffn_all

    def _L1_conv_setup():
        import jax, jax.numpy as jnp
        import numpy as np

        def fq(x, s, qmin, qmax):
            xc = jnp.clip(x, qmin * s, qmax * s)
            return xc + jax.lax.stop_gradient(jnp.round(xc / s) * s - xc)

        def quant_conv_relu(x, w, b, s_in, s_act):
            s_w = jnp.max(jnp.abs(w)) / 127.0
            wq = fq(w, s_w, -128.0, 127.0)
            s_b = s_in * s_w
            bq = fq(b, s_b, -2.0 ** 31, 2.0 ** 31 - 1.0)
            y = jax.lax.conv_general_dilated(x, wq, window_strides=(1, 1), padding='SAME', dimension_numbers=('NCHW', 'OIHW', 'NCHW'))
            y = y + bq[None, :, None, None]
            return fq(jax.nn.relu(y), s_act, 0.0, 255.0)
        key = jax.random.key(seed)
        k = jax.random.split(key, 5)
        B, C, H, W = (16, 32, 16, 16)
        x = jax.random.normal(k[0], (B, C, H, W), dtype=jnp.float32)
        w1 = jax.random.normal(k[1], (C, C, 3, 3), dtype=jnp.float32) * 0.05
        b1 = jax.random.normal(k[2], (C,), dtype=jnp.float32) * 0.1
        w2 = jax.random.normal(k[3], (C, C, 3, 3), dtype=jnp.float32) * 0.05
        b2 = jax.random.normal(k[4], (C,), dtype=jnp.float32) * 0.1
        s_in = jnp.full((1,), 0.03, dtype=jnp.float32)
        s_a1 = jnp.full((1,), 0.05, dtype=jnp.float32)
        s_a2 = jnp.full((1,), 0.05, dtype=jnp.float32)
        return {'x': x, 'w1': w1, 'b1': b1, 'w2': w2, 'b2': b2, 's_in': s_in, 's_a1': s_a1, 's_a2': s_a2}
    _L1_conv_all = _L1_conv_setup()
    _L1_conv_in = {k: v for k, v in _L1_conv_all.items() if k in ('w1', 'b1', 'w2', 'b2', 's_in', 's_a1', 's_a2')}
    del _L1_conv_all

    def _L1_ffn_setup():
        import jax, jax.numpy as jnp
        import numpy as np
        PADDED_SL = 2048
        TEMPERATURE = 1.0
        SIGMA_POW = 0.25

        def _stu_conv(phi, u, n):
            b, sl, d = u.shape
            sgn = jnp.where(jnp.arange(sl) % 2 == 0, 1.0, -1.0).astype(u.dtype)
            sgn3 = sgn[None, :, None]
            Vf = jnp.fft.rfft(phi, n=n, axis=0)
            Uf_p = jnp.fft.rfft(u, n=n, axis=1)
            Uf_m = jnp.fft.rfft(u * sgn3, n=n, axis=1)
            U_plus = jnp.fft.irfft(Vf[None, :, :, None] * Uf_p[:, :, None, :], n=n, axis=1)[:, :sl]
            U_minus = jnp.fft.irfft(Vf[None, :, :, None] * Uf_m[:, :, None, :], n=n, axis=1)[:, :sl]
            U_minus = U_minus * sgn[None, :, None, None]
            return (U_plus, U_minus)

        def _compute_spectral(u, sigma, phi, Mpp, Mpm):
            U_plus, U_minus = _stu_conv(phi, u, PADDED_SL)
            s = sigma ** SIGMA_POW
            out = jnp.einsum('btkd,k,kde->bte', U_plus, s, Mpp)
            out = out + jnp.einsum('btkd,k,kde->bte', U_minus, s, Mpm)
            return out

        def _compute_ar_u(Mu, u):
            sl = u.shape[1]
            out = jnp.zeros(u.shape[:2] + (Mu.shape[-1],), dtype=u.dtype)
            for i in range(Mu.shape[0]):
                ui = jnp.pad(u, ((0, 0), (i, 0), (0, 0)))[:, :sl]
                out = out + jnp.einsum('btd,de->bte', ui, Mu[i])
            return out

        def _stu(u, sigma, phi, Mu, Mpp, Mpm):
            return _compute_spectral(u, sigma, phi, Mpp, Mpm) + _compute_ar_u(Mu, u)
        key = jax.random.key(seed)
        ks = jax.random.split(key, 8)
        b, sl, d, K, k_u = (2, 1024, 32, 16, 3)
        x = jax.random.normal(ks[0], (b, sl, d), dtype=jnp.float32)
        sigma = jax.random.uniform(ks[1], (K,), dtype=jnp.float32, minval=0.001, maxval=1.0)
        phi = jax.random.normal(ks[2], (sl, K), dtype=jnp.float32) / np.sqrt(sl)
        M_u = jax.random.normal(ks[3], (4, k_u, d, d), dtype=jnp.float32) * 0.02
        M_phi_plus = jax.random.normal(ks[4], (4, K, d, d), dtype=jnp.float32) * 0.02
        M_phi_minus = jax.random.normal(ks[5], (4, K, d, d), dtype=jnp.float32) * 0.02
        log_weights = jnp.ones((4,), dtype=jnp.float32)
        u01 = jax.random.uniform(ks[6], (4,), dtype=jnp.float32, minval=1e-06, maxval=1.0 - 1e-06)
        gumbel = -jnp.log(-jnp.log(u01))
        return {'x': x, 'sigma': sigma, 'phi': phi, 'M_u': M_u, 'M_phi_plus': M_phi_plus, 'M_phi_minus': M_phi_minus, 'log_weights': log_weights, 'gumbel': gumbel}
    _L1_ffn_all = _L1_ffn_setup()
    _L1_ffn_in = {k: v for k, v in _L1_ffn_all.items() if k in ('sigma', 'phi', 'M_u', 'M_phi_plus', 'M_phi_minus', 'log_weights', 'gumbel')}
    del _L1_ffn_all
    return {'x': x, 'L0_conv_w_shift1': _L0_conv_in['w_shift1'], 'L0_conv_w_add1': _L0_conv_in['w_add1'], 'L0_conv_bn1_gamma': _L0_conv_in['bn1_gamma'], 'L0_conv_bn1_beta': _L0_conv_in['bn1_beta'], 'L0_conv_bn1_mean': _L0_conv_in['bn1_mean'], 'L0_conv_bn1_var': _L0_conv_in['bn1_var'], 'L0_conv_w_shift2': _L0_conv_in['w_shift2'], 'L0_conv_w_add2': _L0_conv_in['w_add2'], 'L0_conv_bn2_gamma': _L0_conv_in['bn2_gamma'], 'L0_conv_bn2_beta': _L0_conv_in['bn2_beta'], 'L0_conv_bn2_mean': _L0_conv_in['bn2_mean'], 'L0_conv_bn2_var': _L0_conv_in['bn2_var'], 'L0_ffn_ffn_w1': _L0_ffn_in['ffn_w1'], 'L0_ffn_ffn_b1': _L0_ffn_in['ffn_b1'], 'L0_ffn_ffn_w2': _L0_ffn_in['ffn_w2'], 'L0_ffn_ffn_b2': _L0_ffn_in['ffn_b2'], 'L0_ffn_wq': _L0_ffn_in['wq'], 'L0_ffn_wk': _L0_ffn_in['wk'], 'L0_ffn_wv': _L0_ffn_in['wv'], 'L0_ffn_wo': _L0_ffn_in['wo'], 'L0_ffn_attn_mask': _L0_ffn_in['attn_mask'], 'L0_ffn_ffn_mask': _L0_ffn_in['ffn_mask'], 'L1_conv_w1': _L1_conv_in['w1'], 'L1_conv_b1': _L1_conv_in['b1'], 'L1_conv_w2': _L1_conv_in['w2'], 'L1_conv_b2': _L1_conv_in['b2'], 'L1_conv_s_in': _L1_conv_in['s_in'], 'L1_conv_s_a1': _L1_conv_in['s_a1'], 'L1_conv_s_a2': _L1_conv_in['s_a2'], 'L1_ffn_sigma': _L1_ffn_in['sigma'], 'L1_ffn_phi': _L1_ffn_in['phi'], 'L1_ffn_M_u': _L1_ffn_in['M_u'], 'L1_ffn_M_phi_plus': _L1_ffn_in['M_phi_plus'], 'L1_ffn_M_phi_minus': _L1_ffn_in['M_phi_minus'], 'L1_ffn_log_weights': _L1_ffn_in['log_weights'], 'L1_ffn_gumbel': _L1_ffn_in['gumbel']}

def reference(x, L0_conv_w_shift1, L0_conv_w_add1, L0_conv_bn1_gamma, L0_conv_bn1_beta, L0_conv_bn1_mean, L0_conv_bn1_var, L0_conv_w_shift2, L0_conv_w_add2, L0_conv_bn2_gamma, L0_conv_bn2_beta, L0_conv_bn2_mean, L0_conv_bn2_var, L0_ffn_ffn_w1, L0_ffn_ffn_b1, L0_ffn_ffn_w2, L0_ffn_ffn_b2, L0_ffn_wq, L0_ffn_wk, L0_ffn_wv, L0_ffn_wo, L0_ffn_attn_mask, L0_ffn_ffn_mask, L1_conv_w1, L1_conv_b1, L1_conv_w2, L1_conv_b2, L1_conv_s_in, L1_conv_s_a1, L1_conv_s_a2, L1_ffn_sigma, L1_ffn_phi, L1_ffn_M_u, L1_ffn_M_phi_plus, L1_ffn_M_phi_minus, L1_ffn_log_weights, L1_ffn_gumbel):
    import jax
    import jax.numpy as jnp

    def _L0_conv_ref(x, w_shift1, w_add1, bn1_gamma, bn1_beta, bn1_mean, bn1_var, w_shift2, w_add2, bn2_gamma, bn2_beta, bn2_mean, bn2_var):
        import jax, jax.numpy as jnp
        import numpy as np

        def conv2d(x, w, stride=1, padding=0):
            return jax.lax.conv_general_dilated(x, w, window_strides=(stride, stride), padding=[(padding, padding), (padding, padding)], dimension_numbers=('NCHW', 'OIHW', 'NCHW'))

        def adder2d(x, w, stride=1, padding=0):
            N, Ci, H, W = x.shape
            Co, _, K, _ = w.shape
            xp = jnp.pad(x, ((0, 0), (0, 0), (padding, padding), (padding, padding)))
            Ho = (H + 2 * padding - K) // stride + 1
            Wo = (W + 2 * padding - K) // stride + 1
            acc = jnp.zeros((N, Co, Ho, Wo), x.dtype)
            for kh in range(K):
                for kw in range(K):
                    xs = xp[:, :, kh:kh + Ho * stride:stride, kw:kw + Wo * stride:stride]
                    diff = jnp.abs(xs[:, None] - w[None, :, :, kh, kw, None, None])
                    acc = acc - diff.sum(axis=2)
            return acc

        def batchnorm(x, gamma, beta, mean, var, eps=1e-05):
            inv = gamma / jnp.sqrt(var + eps)
            return x * inv[None, :, None, None] + (beta - mean * inv)[None, :, None, None]
        identity = x
        out = conv2d(x, w_shift1, stride=1, padding=0)
        out = adder2d(out, w_add1, stride=1, padding=0)
        out = jax.nn.relu(batchnorm(out, bn1_gamma, bn1_beta, bn1_mean, bn1_var))
        out = conv2d(out, w_shift2, stride=1, padding=1)
        out = adder2d(out, w_add2, stride=1, padding=1)
        out = jax.nn.relu(batchnorm(out, bn2_gamma, bn2_beta, bn2_mean, bn2_var))
        return jax.nn.relu(out + identity)

    def _L0_ffn_ref(x, ffn_w1, ffn_b1, ffn_w2, ffn_b2, wq, wk, wv, wo, attn_mask, ffn_mask):
        import jax, jax.numpy as jnp
        import numpy as np
        NB, NOPS = (33, 19)
        D, H = (32, 128)
        B, S = (8, 256)
        CARRY_OPS = [0, 1, 2, 10, 11, 12, 13]

        def _build_masks():
            am = np.zeros((NB, NOPS), dtype=bool)
            fm = np.zeros((NB, NOPS), dtype=bool)
            fm[0, :] = True
            for b in range(1, 8):
                am[b, CARRY_OPS] = True
                fm[b, CARRY_OPS] = True
            am[8, [14, 15, 8, 9]] = True
            fm[8, [14, 15, 8, 9]] = True
            for b in range(16, 32):
                fm[b, [3, 4]] = True
            am[32, [10, 11, 12, 13]] = True
            fm[32, [5, 6, 7, 2, 4, 10, 11, 12, 13]] = True
            return (jnp.asarray(am), jnp.asarray(fm))
        scale = jnp.asarray(1.0 / np.sqrt(D), x.dtype)

        def step(h, p):
            op = jnp.argmax(h[0, 0, :NOPS])
            q = h @ p['wq'][op]
            k = h @ p['wk'][op]
            v = h @ p['wv'][op]
            attn = jax.nn.softmax(jnp.einsum('bqd,bkd->bqk', q, k) * scale, axis=-1)
            y = jnp.einsum('bqk,bkd->bqd', attn, v) @ p['wo'][op]
            h = jnp.where(p['am'][op], y, h)
            z = jax.nn.relu(h @ p['w1'][op] + p['b1'][op]) @ p['w2'][op] + p['b2'][op]
            h = jnp.where(p['fm'][op], z, h)
            return (h, None)
        xs = {'w1': ffn_w1, 'b1': ffn_b1, 'w2': ffn_w2, 'b2': ffn_b2, 'wq': wq, 'wk': wk, 'wv': wv, 'wo': wo, 'am': attn_mask, 'fm': ffn_mask}
        out, _ = jax.lax.scan(step, x, xs)
        return out

    def _L1_conv_ref(x, w1, b1, w2, b2, s_in, s_a1, s_a2):
        import jax, jax.numpy as jnp
        import numpy as np

        def fq(x, s, qmin, qmax):
            xc = jnp.clip(x, qmin * s, qmax * s)
            return xc + jax.lax.stop_gradient(jnp.round(xc / s) * s - xc)

        def quant_conv_relu(x, w, b, s_in, s_act):
            s_w = jnp.max(jnp.abs(w)) / 127.0
            wq = fq(w, s_w, -128.0, 127.0)
            s_b = s_in * s_w
            bq = fq(b, s_b, -2.0 ** 31, 2.0 ** 31 - 1.0)
            y = jax.lax.conv_general_dilated(x, wq, window_strides=(1, 1), padding='SAME', dimension_numbers=('NCHW', 'OIHW', 'NCHW'))
            y = y + bq[None, :, None, None]
            return fq(jax.nn.relu(y), s_act, 0.0, 255.0)
        s0 = s_in[0]
        s1 = s_a1[0]
        s2 = s_a2[0]
        xq = fq(x, s0, -128.0, 127.0)
        h = quant_conv_relu(xq, w1, b1, s0, s1)
        out = quant_conv_relu(h, w2, b2, s1, s2)
        return out

    def _L1_ffn_ref(x, sigma, phi, M_u, M_phi_plus, M_phi_minus, log_weights, gumbel):
        import jax, jax.numpy as jnp
        import numpy as np
        PADDED_SL = 2048
        TEMPERATURE = 1.0
        SIGMA_POW = 0.25

        def _stu_conv(phi, u, n):
            b, sl, d = u.shape
            sgn = jnp.where(jnp.arange(sl) % 2 == 0, 1.0, -1.0).astype(u.dtype)
            sgn3 = sgn[None, :, None]
            Vf = jnp.fft.rfft(phi, n=n, axis=0)
            Uf_p = jnp.fft.rfft(u, n=n, axis=1)
            Uf_m = jnp.fft.rfft(u * sgn3, n=n, axis=1)
            U_plus = jnp.fft.irfft(Vf[None, :, :, None] * Uf_p[:, :, None, :], n=n, axis=1)[:, :sl]
            U_minus = jnp.fft.irfft(Vf[None, :, :, None] * Uf_m[:, :, None, :], n=n, axis=1)[:, :sl]
            U_minus = U_minus * sgn[None, :, None, None]
            return (U_plus, U_minus)

        def _compute_spectral(u, sigma, phi, Mpp, Mpm):
            U_plus, U_minus = _stu_conv(phi, u, PADDED_SL)
            s = sigma ** SIGMA_POW
            out = jnp.einsum('btkd,k,kde->bte', U_plus, s, Mpp)
            out = out + jnp.einsum('btkd,k,kde->bte', U_minus, s, Mpm)
            return out

        def _compute_ar_u(Mu, u):
            sl = u.shape[1]
            out = jnp.zeros(u.shape[:2] + (Mu.shape[-1],), dtype=u.dtype)
            for i in range(Mu.shape[0]):
                ui = jnp.pad(u, ((0, 0), (i, 0), (0, 0)))[:, :sl]
                out = out + jnp.einsum('btd,de->bte', ui, Mu[i])
            return out

        def _stu(u, sigma, phi, Mu, Mpp, Mpm):
            return _compute_spectral(u, sigma, phi, Mpp, Mpm) + _compute_ar_u(Mu, u)
        T = x.shape[1]
        outs = []
        for i, frac in enumerate((1, 2, 4, 8)):
            xi = x[:, :T // frac]
            si = _stu(xi, sigma, phi, M_u[i], M_phi_plus[i], M_phi_minus[i])
            si = jnp.pad(si, ((0, 0), (0, T - si.shape[1]), (0, 0)))
            outs.append(si)
        y_soft = jax.nn.softmax((log_weights + gumbel) / TEMPERATURE)
        y_hard = jax.nn.one_hot(jnp.argmax(y_soft), 4, dtype=y_soft.dtype)
        weights = y_hard - jax.lax.stop_gradient(y_soft) + y_soft
        stacked = jnp.stack(outs, axis=-1)
        return jnp.sum(stacked * weights, axis=-1)

    def _gn(v, G=32, eps=1e-05):
        B_, C_, H_, W_ = v.shape
        g = v.reshape(B_, G, C_ // G, H_, W_)
        m = jnp.mean(g, axis=(2, 3, 4), keepdims=True)
        s = jnp.var(g, axis=(2, 3, 4), keepdims=True)
        return ((g - m) / jnp.sqrt(s + eps)).reshape(v.shape)

    def _ln_c(v, eps=1e-06):
        m = jnp.mean(v, axis=1, keepdims=True)
        s = jnp.var(v, axis=1, keepdims=True)
        return (v - m) / jnp.sqrt(s + eps)

    def _ln_t(v, eps=1e-05):
        m = jnp.mean(v, axis=-1, keepdims=True)
        s = jnp.var(v, axis=-1, keepdims=True)
        return (v - m) / jnp.sqrt(s + eps)

    def _to_tokens(v):
        B_, C_, H_, W_ = v.shape
        return v.reshape(B_, C_, H_ * W_).transpose(0, 2, 1)

    def _from_tokens(t, like):
        B_, C_, H_, W_ = like.shape
        return t.transpose(0, 2, 1).reshape(B_, C_, H_, W_)
    x = x + _L0_conv_ref(_ln_c(x), L0_conv_w_shift1, L0_conv_w_add1, L0_conv_bn1_gamma, L0_conv_bn1_beta, L0_conv_bn1_mean, L0_conv_bn1_var, L0_conv_w_shift2, L0_conv_w_add2, L0_conv_bn2_gamma, L0_conv_bn2_beta, L0_conv_bn2_mean, L0_conv_bn2_var)
    t = _to_tokens(x)
    t = t + _L0_ffn_ref(_ln_t(t), L0_ffn_ffn_w1, L0_ffn_ffn_b1, L0_ffn_ffn_w2, L0_ffn_ffn_b2, L0_ffn_wq, L0_ffn_wk, L0_ffn_wv, L0_ffn_wo, L0_ffn_attn_mask, L0_ffn_ffn_mask)
    x = _from_tokens(t, x)
    x = x + _L1_conv_ref(_ln_c(x), L1_conv_w1, L1_conv_b1, L1_conv_w2, L1_conv_b2, L1_conv_s_in, L1_conv_s_a1, L1_conv_s_a2)
    t = _to_tokens(x)
    t = t + _L1_ffn_ref(_ln_t(t), L1_ffn_sigma, L1_ffn_phi, L1_ffn_M_u, L1_ffn_M_phi_plus, L1_ffn_M_phi_minus, L1_ffn_log_weights, L1_ffn_gumbel)
    x = _from_tokens(t, x)
    return x

_drawn_inputs = setup_inputs


def setup_inputs(seed=0):
    import zlib

    import numpy as np

    out = dict(_drawn_inputs(seed))
    spreads = {'L0_ffn_ffn_b1': (0.0, 0.1), 'L0_ffn_ffn_b2': (0.0, 0.1), 'L1_ffn_log_weights': (1.0, 0.2)}
    factors = {}
    for name, (base, spread) in spreads.items():
        noise = np.random.default_rng([zlib.crc32(name.encode()), seed]).standard_normal(out[name].shape)
        drawn = base * np.exp(spread * noise) if base else spread * noise
        out[name] = jnp.asarray(drawn.astype(out[name].dtype))
    for name, factor in factors.items():
        out[name] = (out[name] * factor).astype(out[name].dtype)
    return out
```

```python
from contextlib import ExitStack, contextmanager

import concourse.bass as bass
from concourse import mybir

F32 = mybir.dt.float32
BF16 = mybir.dt.bfloat16
I32 = mybir.dt.int32
U32 = mybir.dt.uint32
U8 = mybir.dt.uint8
ALU = mybir.AluOpType
ACT = mybir.ActivationFunctionType
AX = mybir.AxisListType
ds = bass.ds

P = 128
NIMG, C, SIDE = 4, 32, 28
T = SIDE * SIDE
HT = T // 2
HROWS = SIDE // 2
PS_ = SIDE + 2
PADF = 904
NB, NOPS, HID = 33, 19, 128
STEPS = (3, 4, 3)
QT, NQ = 112, 7
NK = 16
NPH = T // 2
LE, LO = NPH + 127, NPH + 128
MAGIC = 12582912.0
SCALE = float(C) ** -0.5
SEGS = [(0, 49, 3), (49, 98, 2), (98, 196, 1), (196, 392, 0)]

PC = dict(g=0, be=2, mu=4, va=6, cb=8, sc=10, lw=13, gu=17, sg=21, n=25)
_c, CC = 0, {}
for _n, _w in (("ident", 128), ("bones", 128), ("nident", 128), ("sel1", 256), ("sel2", 256), ("corr", 128),
               ("perm", 128), ("zero", 128), ("ones", 128), ("dmask", 1), ("eps5", 1), ("eps6", 1),
               ("iota", 4), ("blk4", NB)):
    CC[_n] = _c
    _c += _w
CC["n"] = _c


def on_scalar(c8, cg):
    return cg == 3 or (c8 % 2 == 0 and cg == 2)


RG = 3
DVE_BY = [0]
ACT_BY = [0]
for _c8 in range(8):
    _a = sum(on_scalar(_c8, _g) for _g in range(4))
    ACT_BY.append(ACT_BY[-1] + _a)
    DVE_BY.append(DVE_BY[-1] + 4 - _a)
DVE_TAP, ACT_TAP = DVE_BY[8], ACT_BY[8]


@contextmanager
def active_steps(e, code):
    assert STEPS[0] * STEPS[1] * STEPS[2] >= NB
    with e.Fori(0, STEPS[0]):
        with e.If(e.snap(code, min_val=0, max_val=4 * NB + 7) > 0):
            with e.Fori(0, STEPS[1]):
                with e.If(e.snap(code, min_val=0, max_val=4 * NB + 7) > 0):
                    with e.Fori(0, STEPS[2]):
                        c = e.snap(code, min_val=0, max_val=4 * NB + 7)
                        with e.If(c > 0):
                            yield c
                        e.nop()
                e.nop()
        e.nop()


def build(nc, x, par, con, ws1, wa1c, wa1r, ws2, wa2c, wa2r, amt, fmt, fw1, fb1, fw2, fb2, wq, wk, wv, wo,
          cw1, cw2, phe, pho, mpp, mpm, mu, out):
    with ExitStack() as ctx:
        def sb(name, shape, dt=F32):
            return ctx.enter_context(nc.sbuf_tensor(name, shape, dt))

        def sem(name):
            return ctx.enter_context(nc.semaphore(name))

        PS = ctx.enter_context(nc.psum_tensor("PS", [P, 8, 512], F32))

        X = sb("X", [P, T]); XN = sb("XN", [P, T]); XC = sb("XC", [P, T]); SQ = sb("SQ", [P, T])
        SD = sb("SD", [P, T]); RS = sb("RS", [P, T]); Y1 = sb("Y1", [P, T])
        H1P = sb("H1P", [P, PADF]); Y2P = sb("Y2P", [P, PADF])
        X1 = sb("X1", [P, T]); HSUM = sb("H", [P, PS_ * SIDE]); H = HSUM[:, 0:T]
        arena = sb("arena", [P, 4 * RG * T])
        RING = arena[:, :].rearrange("p (n t) -> p n t", n=4 * RG)
        PT = arena[:, 0:8 * T].rearrange("p (n t) -> p n t", n=8)
        HIDT = arena[:, 0:4 * T].rearrange("p (n t) -> p n t", n=8)
        UEV = arena[:, 0:4 * T].rearrange("p (n t) -> p n t", n=8)
        HE = sb("HE", [P, NK, NPH]); HO = sb("HO", [P, NK, NPH + 1])
        KZ = sb("KZ", [P, 4, T]); QZ = sb("QZ", [P, 4, T])
        PAR = sb("PAR", [P, PC["n"]]); CON = sb("CON", [P, CC["n"]])
        WS1 = sb("WS1", [P, P]); WA1 = sb("WA1", [P, C]); WA1R = sb("WA1R", [P, C])
        WS2 = sb("WS2", [P, 9, P]); WA2 = sb("WA2", [P, 9 * C]); WA2R = sb("WA2R", [P, 9 * C])
        BN = sb("BN", [P, 24])
        AMT = sb("AMT", [P, NOPS * NB], U8); FMT = sb("FMT", [P, NOPS * NB], U8)
        AMF = XC[:, 0:NOPS * NB]; KEYT = sb("KEYT", [P, NOPS * NB])
        ROW = sb("ROW", [P, 32]); MX8 = sb("MX8", [P, 8]); IX8 = sb("IX8", [P, 8], U32)
        CAND = sb("CAND", [P, 40]); KMAX = sb("KMAX", [P, 1]); PREV = sb("PREV", [P, 1])
        KINT = sb("KINT", [P, 1], I32); PINT = sb("PINT", [P, 1], I32)
        W1R = sb("W1R", [P, HID]); W1B = sb("W1B", [P, 4, HID]); W2S = sb("W2S", [P, C])
        B1S = sb("B1S", [P, 1]); B2S = sb("B2S", [P, 1])
        W4R = sb("W4R", [P, 4, C]); W4B = sb("W4B", [P, 4, P])
        VT = sb("VT", [P, NQ, P]); SMX = sb("SMX", [P, 4 * NQ]); YA = XN
        CW1 = sb("CW1", [P, 9 * P]); CW2 = sb("CW2", [P, 9 * P])
        CQ1 = sb("CQ1", [P, 9 * P], BF16); CQ2 = sb("CQ2", [P, 9 * P], BF16)
        XQP = H1P[:, 0:PADF // 2].bitcast(BF16); HQP = H1P[:, PADF // 2:PADF].bitcast(BF16)
        WMX = sb("WMX", [P, 2]); WRW = sb("WRW", [P, 2]); QS = sb("QS", [P, 24])
        MPP = sb("MPP", [P, 4, P]); MPM = sb("MPM", [P, 4, P]); MSC = sb("MSC", [P, 4, P])
        ASEG = sb("ASEG", [P, 2, 4, P]); MUR = sb("MUR", [P, 4, 96]); MUS = sb("MUS", [P, 4, 96])
        MUB = sb("MUB", [P, 12, P]); WSM = sb("WSM", [P, 48]); WIX = sb("WIX", [P, 8], U32)
        UT = WS2[:, 0:8, :]
        XS9 = RS
        UPZ = CW1[:, 0:2 + 1024]

        URV = CW2[:, 0:1024]

        def con_(name, w=None, rows=P):
            a = CC[name]
            return CON[0:rows, a:a + (w or P)]

        def par_(name, i=0, w=1):
            return PAR[:, PC[name] + i:PC[name] + i + w]

        def half(ap, h):
            return ap[:, h * HT:(h + 1) * HT]

        def rows(ap, h, dh=0, dw=0):
            v = ap[:, 0:PS_ * PS_].rearrange("p (a b) -> p a b", a=PS_)
            return v[:, h * HROWS + dh:h * HROWS + dh + HROWS, dw:dw + SIDE]

        def bank(b, w=HT, rows_=slice(0, P)):
            return PS[rows_, b, 0:w]

        def grid(ap):
            return ap.rearrange("p (a b) -> p a b", b=SIDE)

        SEL = {True: con_("sel1", 256).rearrange("p (c m) -> p c m", c=8),
               False: con_("sel2", 256).rearrange("p (c m) -> p c m", c=8)}

        s = {n: sem(n) for n in (
            "sp_woke x_in par_in con_in wa1_in w_a_in sum_in mask_in ws2_in cw_in strip_in mst_in "
            "ln_mean ln_cent ln_sq ln_var ln_sd ln_out ln_chain "
            "bn_sd bn_ready bn_chain pads zeroed c1_done y1_ready ring_free dve_unit act_unit adder_init adder_done "
            "h1_ready c2_done y2_ready xs9_ready xs9_chain h2_ready perm_done x1_tmp x1_ready "
            "key_chain key_ready row_done decided "
            "ffn_w att_w ffn_diag ffn_pad ffn_h1 hid_act hid_dve ffn_out ffn_h att_pad att_diag att_proj kz_done qz_done v_proj v_done "
            "s_done smax_done mrow_done mrow_cp st_done exp_done pv_done att_rs att_y att_wo att_h "
            "wmx_part wmx_rows wmx_row wmx_bc wmx_all q_sc q_chain cq_chain cq_done x2_ready q_xin cc_done cv_relu cv_q x3_ready "
            "wexp w_soft w_chain sg_ready d_chain d_ready ar_done ut_done ut_ready urv_ready u_done uev_act uev_dve mix_done y_ready stored"
        ).split()}
        ctx.enter_context(nc.allow_non_contiguous_dma("weights' rows are short"))
        block = ctx.enter_context(nc.Block())

        @block.sync
        def _(sp):
            sp.dma_start(X[:, :], x).then_inc(s["x_in"], 16)
            sp.dma_start(PAR[:, :], par).then_inc(s["par_in"], 16)
            sp.dma_start(WS1[:, :], ws1).then_inc(s["wa1_in"], 16)
            sp.dma_start(WA1[:, :], wa1c).then_inc(s["wa1_in"], 16)
            sp.dma_start(WA1R[:, :], wa1r).then_inc(s["sum_in"], 16)
            sp.dma_start(WA2R[:, :], wa2r).then_inc(s["sum_in"], 16)
            sp.dma_start(WS2[:, :, :], ws2).then_inc(s["ws2_in"], 16)
            sp.dma_start(WA2[:, :], wa2c).then_inc(s["w_a_in"], 16)
            sp.dma_start(AMT[0:1, :], amt).then_inc(s["mask_in"], 16)
            sp.dma_start(FMT[0:1, :], fmt).then_inc(s["mask_in"], 16)
            sp.dma_start(MPP[:, :, :], mpp).then_inc(s["mst_in"], 16)
            sp.dma_start(MPM[:, :, :], mpm).then_inc(s["mst_in"], 16)
            for b in range(NIMG):
                sp.dma_start(MUR[32 * b:32 * b + 32, :, :], mu).then_inc(s["mst_in"], 16)
            sp.dma_start(CW1[:, :], cw1).then_inc(s["cw_in"], 16)
            sp.dma_start(CW2[:, :], cw2).then_inc(s["cw_in"], 16)
            sp.dma_start(HE[:, :, :], bass.AP(phe.tensor, 0, [[1, P], [LE, NK], [1, NPH]])).then_inc(s["strip_in"], 16)
            sp.dma_start(HO[:, :, :], bass.AP(pho.tensor, 0, [[1, P], [LO, NK], [1, NPH + 1]])).then_inc(s["strip_in"], 16)

            sp.wait_ge(s["decided"], 1)
            code = sp.alloc_register("sp_code"); which = sp.alloc_register("sp_which")
            sp.load(code, KINT[0:1, 0:1], bass_reorder=False)
            chosen = sp.alloc_register("sp_chosen")
            sp.reg_mov(chosen, 1)
            with active_steps(sp, code) as c:
                op = sp.value_load(IX8[0:1, 0:1], min_val=0, max_val=NOPS - 1)
                sp.reg_mov(which, (NB - (c >> 2)) * NOPS + op)
                w = sp.snap(which, min_val=0, max_val=NB * NOPS - 1)
                with sp.If((c & 1) > 0):
                    for i, src in enumerate((wq, wk, wv, wo)):
                        sp.dma_start(W4R[:, i, :],
                                     src[ds(w, 1), :, :].broadcast_to([NIMG, C, C])).then_inc(s["att_w"], 16)
                    sp.nop()
                with sp.If((c & 2) > 0):
                    sp.dma_start(W1R[:, :],
                                 fw1[ds(w, 1), :, :].broadcast_to([NIMG, C, HID])).then_inc(s["ffn_w"], 16)
                    sp.dma_start(B1S[:, :], fb1[ds(w, 1), :].rearrange("a n -> n a")).then_inc(s["ffn_w"], 16)
                    sp.dma_start(W2S[:, :], fw2[ds(w, 1), :, :].rearrange("a h d -> (a h) d")).then_inc(s["ffn_w"], 16)
                    sp.dma_start(B2S[:, :],
                                 fb2[ds(w, 1), :].rearrange("a (n e) -> a n e", e=1).broadcast_to([NIMG, C, 1])
                                 ).then_inc(s["ffn_w"], 16)
                    sp.nop()
                n = sp.snap(chosen, min_val=1, max_val=NB)
                sp.wait_ge(s["decided"], n + 1)
                sp.sem_inc(s["sp_woke"], 1)
                sp.reg_add(chosen, chosen, 1)
                sp.load(code, KINT[0:1, 0:1], bass_reorder=False)

            sp.wait_ge(s["y_ready"], 2)
            sp.dma_start(out, Y1[:, :]).then_inc(s["stored"], 16)
            sp.wait_ge(s["stored"], 16)

        @block.gpsimd
        def _(g):
            g.dma_start(CON[:, :], con).then_inc(s["con_in"], 16)
            g.memset(H1P[:, :], 0.0).then_inc(s["pads"], 1)
            g.memset(Y2P[:, :], 0.0).then_inc(s["pads"], 1)
            g.memset(W1B[:, :, :], 0.0).then_inc(s["zeroed"], 1)
            g.memset(W4B[:, :, :], 0.0).then_inc(s["zeroed"], 1)
            g.memset(MUB[:, :, :], 0.0).then_inc(s["zeroed"], 1)
            g.memset(KZ[:, :, :], 0.0).then_inc(s["zeroed"], 1)
            g.memset(QZ[:, :, :], 0.0).then_inc(s["zeroed"], 1)
            g.wait_ge(s["zeroed"], 5)
            for b in range(NIMG):
                r = 32 * ((b + 1) % NIMG)
                g.memset(KZ[r:r + 1, b, :], 1.0).then_inc(s["zeroed"], 1)
            g.wait_ge(s["zeroed"], 9)

            chain = 0

            def link(ins):
                nonlocal chain
                chain += 1
                ins.then_inc(s["d_chain"], 1)
                g.wait_ge(s["d_chain"], chain)

            g.wait_ge(s["mst_in"], 16 * 6)
            g.wait_ge(s["sg_ready"], 2)
            g.wait_ge(s["w_soft"], 1)
            sg = WSM[:, 40:44].unsqueeze(2).to_broadcast([P, 4, C])
            for par_i, op in enumerate((ALU.add, ALU.subtract)):
                link(g.tensor_tensor(MSC[:, :, :], MPP[:, :, :], MPM[:, :, :], op))
                for i in range(4):
                    v = MSC[:, i, :].rearrange("p (g e) -> p g e", g=4)
                    link(g.tensor_tensor(v, v, sg, ALU.mult))
                    link(g.tensor_scalar(ASEG[:, par_i, i, :], MSC[:, i, :], WSM[:, 24 + i:25 + i], None, ALU.mult))
                    if i:
                        link(g.tensor_tensor(ASEG[:, par_i, i, :], ASEG[:, par_i, i, :], ASEG[:, par_i, i - 1, :], ALU.add))
            for i in range(4):
                link(g.tensor_scalar(MUS[:, i, :], MUR[:, i, :], WSM[:, 24 + i:25 + i], None, ALU.mult))
                if i:
                    link(g.tensor_tensor(MUS[:, i, :], MUS[:, i, :], MUS[:, i - 1, :], ALU.add))
            for b in range(NIMG):
                q = slice(32 * b, 32 * b + 32)
                g.tensor_copy(MUB[q, :, q], MUS[q, :, :].rearrange("p i (l e) -> p (i l) e", e=C)).then_inc(s["d_ready"], 1)

            g.wait_ge(s["d_ready"], 4)

            g.wait_ge(s["q_sc"], 1)
            g.wait_ge(s["cw_in"], 32)
            cq = 0

            def qlink(ins):
                nonlocal cq
                cq += 1
                ins.then_inc(s["cq_chain"], 1)
                g.wait_ge(s["cq_chain"], cq)

            for i, (src, dst) in enumerate(((CW1, CQ1), (CW2, CQ2))):
                qlink(g.tensor_scalar(src[:, :], src[:, :], QS[:, 2 + i:3 + i], -128.0, ALU.mult, ALU.max))
                qlink(g.tensor_scalar(src[:, :], src[:, :], 127.0, MAGIC, ALU.min, ALU.add))
                g.tensor_scalar(dst[:, :], src[:, :], -MAGIC, None, ALU.add).then_inc(s["cq_done"], 1)

            g.wait_ge(s["cq_done"], 2)
            g.memset(UPZ, 0.0).then_inc(s["zeroed"], 1)
            g.memset(URV, 0.0).then_inc(s["zeroed"], 1)

            g.wait_ge(s["y2_ready"], 2)
            g.memset(H1P[:, :], 0.0).then_inc(s["pads"], 1)
            y2 = Y2P[:, 0:PS_ * PS_].rearrange("p (a b) -> p a b", a=PS_)
            hs = HSUM[:, :].rearrange("p (a b) -> p a b", a=PS_)
            g.tensor_tensor(hs, y2[:, :, 0:SIDE], y2[:, :, 1:1 + SIDE], ALU.add).then_inc(s["xs9_chain"], 1)
            g.wait_ge(s["xs9_chain"], 1)
            g.tensor_tensor(hs, hs, y2[:, :, 2:2 + SIDE], ALU.add).then_inc(s["xs9_chain"], 1)
            g.wait_ge(s["xs9_chain"], 2)
            xs = grid(XS9[:, :])
            g.tensor_tensor(xs, hs[:, 0:SIDE, :], hs[:, 1:1 + SIDE, :], ALU.add).then_inc(s["xs9_chain"], 1)
            g.wait_ge(s["xs9_chain"], 3)
            g.tensor_tensor(xs, xs, hs[:, 2:2 + SIDE, :], ALU.add).then_inc(s["xs9_ready"], 1)

            g.wait_ge(s["decided"], 1)
            code = g.alloc_register("g_code"); na = g.alloc_register("g_na"); nf = g.alloc_register("g_nf")
            g.load(code, KINT[0:1, 0:1], bass_reorder=False)
            g.reg_mov(na, 0); g.reg_mov(nf, 0)
            chosen = g.alloc_register("g_chosen")
            g.reg_mov(chosen, 1)
            with active_steps(g, code) as c:
                with g.If((c & 1) > 0):
                    a = g.snap(na, min_val=0, max_val=NB)
                    for b in range(NIMG):
                        r = 32 * ((b + 1) % NIMG)
                        last = g.memset(QZ[r:r + 1, b, :], 0.0)
                        last.then_inc(s["att_pad"], 1)
                    g.wait_ge(s["att_pad"], a * 4 + 4)
                    g.wait_ge(s["att_w"], a * 64 + 64)
                    g.reg_add(na, na, 1)
                    for b in range(NIMG):
                        q = slice(32 * b, 32 * b + 32)
                        g.tensor_copy(W4B[q, :, q], W4R[q, :, :]).then_inc(s["att_diag"], 1)
                with g.If((c & 2) > 0):
                    f = g.snap(nf, min_val=0, max_val=NB)
                    g.wait_ge(s["ffn_w"], f * 64 + 64)
                    g.reg_add(nf, nf, 1)
                    for b in range(NIMG):
                        q = slice(32 * b, 32 * b + 32)
                        last = g.tensor_copy(W1B[q, b, :], W1R[q, :]).then_inc(s["ffn_diag"], 1)
                n = g.snap(chosen, min_val=1, max_val=NB)
                g.wait_ge(s["decided"], n + 1)
                g.reg_add(chosen, chosen, 1)
                g.load(code, KINT[0:1, 0:1], bass_reorder=False)

        @block.scalar
        def _(a):
            def norm(k, eps):
                for h in range(2):
                    a.wait_ge(s["ln_cent"], 2 * k + h + 1)
                    a.activation(half(SQ, h), half(XC, h), ACT.Square).then_inc(s["ln_sq"], 1)
                for h in range(2):
                    a.wait_ge(s["ln_var"], 2 * k + h + 1)
                    a.activation(half(SD, h), bank(2 + h), ACT.Sqrt, bias=con_(eps, 1)).then_inc(s["ln_sd"], 1)

            a.wait_ge(s["w_chain"], 2)
            a.activation(WSM[:, 8:12], WSM[:, 4:8], ACT.Exp, accum_out=WSM[:, 12:13]).then_inc(s["wexp"], 1)
            a.wait_ge(s["par_in"], 16)
            a.wait_ge(s["con_in"], 16)
            a.activation(BN[:, 0:2], par_("va", 0, 2), ACT.Sqrt, bias=con_("eps5", 1)).then_inc(s["bn_sd"], 1)
            a.activation(WSM[:, 36:40], par_("sg", 0, 4), ACT.Sqrt).then_inc(s["sg_ready"], 1)
            a.wait_ge(s["sg_ready"], 1)
            a.activation(WSM[:, 40:44], WSM[:, 36:40], ACT.Sqrt).then_inc(s["sg_ready"], 1)
            norm(0, "eps6")
            a.wait_ge(s["c1_done"], 1)
            a.activation(half(Y1, 0), bank(4), ACT.Copy).then_inc(s["y1_ready"], 1)

            a.wait_ge(s["y1_ready"], 2)
            a.wait_ge(s["wa1_in"], 32)
            for g in range(8):
                slot = g % RG
                if g >= RG:
                    a.wait_ge(s["ring_free"], g - RG + 1)
                for cg in range(4):
                    if on_scalar(g, cg):
                        co = 8 * cg + g
                        a.activation(RING[:, 4 * slot + cg, :], Y1[:, :], ACT.Abs, bias=WA1[:, co:co + 1],
                                     scale=-1.0).then_inc(s["act_unit"], 1)
            a.wait_ge(s["adder_done"], 1)
            a.wait_ge(s["bn_ready"], 1)
            a.wait_ge(s["pads"], 2)
            a.activation(rows(H1P, 0, 1, 1), grid(bank(6)), ACT.Relu, bias=BN[:, 10:11], scale=BN[:, 8:9]).then_inc(s["h1_ready"], 1)
            a.wait_ge(s["c2_done"], 1)
            a.activation(rows(Y2P, 0, 1, 1), grid(bank(4)), ACT.Copy).then_inc(s["y2_ready"], 1)

            a.wait_ge(s["y2_ready"], 2)
            a.wait_ge(s["w_a_in"], 16)
            with a.Fori(0, 3) as dh:
                for dw in range(3):
                    win = Y2P[:, ds(dh * PS_ + dw, SIDE * PS_)].rearrange("p (a b) -> p a b", b=PS_)[:, :, 0:SIDE]
                    for g in range(8):
                        slot = (8 * (dw + 1) + g) % RG
                        a.wait_ge(s["ring_free"], dh * 24 + (8 * (dw + 1) + g - RG + 1))
                        for cg in range(4):
                            if on_scalar(g, cg):
                                co = 8 * cg + g
                                a.activation(grid(RING[:, 4 * slot + cg, :]), win, ACT.Abs,
                                             bias=WA2[:, ds(dh * 96 + (32 * dw + co), 1)], scale=-1.0).then_inc(s["act_unit"], 1)
            a.wait_ge(s["adder_done"], 2)
            a.activation(half(SQ, 0), bank(6), ACT.Relu, bias=BN[:, 11:12], scale=BN[:, 9:10]).then_inc(s["h2_ready"], 1)
            norm(1, "eps5")

            a.wait_ge(s["decided"], 1)
            code = a.alloc_register("a_code"); na = a.alloc_register("a_na"); nf = a.alloc_register("a_nf")
            a.load(code, KINT[0:1, 0:1], bass_reorder=False)
            a.reg_mov(na, 0); a.reg_mov(nf, 0)
            chosen = a.alloc_register("a_chosen")
            a.reg_mov(chosen, 1)
            with active_steps(a, code) as c:
                with a.If((c & 1) > 0):
                    k = a.snap(na, min_val=0, max_val=NB)
                    a.wait_ge(s["att_proj"], k * 4 + 2)
                    for b in range(NIMG):
                        q = slice(32 * b, 32 * b + 32)
                        a.activation(QZ[q, b, :].rearrange("p (h t) -> p h t", h=2), PS[q, 0:2, 0:HT],
                                     ACT.Copy).then_inc(s["qz_done"], 1)
                    for b in range(NIMG):
                        r = 32 * ((b + 1) % NIMG)
                        a.wait_ge(s["mrow_done"], k * 4 + (b + 1))
                        a.activation(QZ[r:r + 1, b, 0:4 * QT], PS[r:r + 1, 6, 0:4 * QT], ACT.Copy)
                        a.activation(QZ[r:r + 1, b, 4 * QT:T], PS[r:r + 1, 7, 0:3 * QT], ACT.Copy).then_inc(s["mrow_cp"], 1)
                    for v in range(4 * NQ):
                        a.wait_ge(s["st_done"], k * 28 + (v + 1))
                        if v >= 8:
                            a.wait_ge(s["pv_done"], k * NQ + (v // 4 - 1))
                        pr = 2 * (v % 2)
                        a.activation(PT[0:QT, v % 8, :].rearrange("p (h t) -> p h t", h=2), PS[0:QT, pr:pr + 2, 0:HT],
                                     ACT.Exp, scale=SCALE).then_inc(s["exp_done"], 1)
                    a.wait_ge(s["att_wo"], k * 2 + 1)
                    a.activation(half(H, 0), bank(0), ACT.Copy).then_inc(s["att_h"], 1)
                    a.reg_add(na, na, 1)
                with a.If((c & 2) > 0):
                    k = a.snap(nf, min_val=0, max_val=NB)
                    a.wait_ge(s["ffn_w"], k * 64 + 64)
                    for u in range(0, 8, 2):
                        a.wait_ge(s["ffn_h1"], k * 8 + (u + 1))
                        a.activation(HIDT[:, u, :], bank(u % 4), ACT.Relu, bias=B1S[:, :]).then_inc(s["hid_act"], 1)
                    a.wait_ge(s["ffn_out"], k * 2 + 1)
                    a.activation(half(H, 0), bank(4), ACT.Identity, bias=B2S[:, :]).then_inc(s["ffn_h"], 1)
                    a.reg_add(nf, nf, 1)
                n = a.snap(chosen, min_val=1, max_val=NB)
                a.wait_ge(s["decided"], n + 1)
                a.reg_add(chosen, chosen, 1)
                a.load(code, KINT[0:1, 0:1], bass_reorder=False)

            norm(2, "eps6")
            for i in range(2):
                for h in range(2):
                    a.wait_ge(s["cc_done"], 2 * i + h + 1)
                    a.activation(half(SQ, h), bank(4 + h), ACT.Relu, bias=QS[:, 10 + i:11 + i],
                                 scale=QS[:, 8 + i:9 + i]).then_inc(s["cv_relu"], 1)
            norm(3, "eps5")
            a.wait_ge(s["zeroed"], 11)
            for h in range(2):
                a.wait_ge(s["ln_out"], 6 + h + 1)
                lo = h * HT
                a.activation(URV[:, 1024 - lo - HT:1024 - lo], UPZ[:, 2 + lo + HT - 1:2 + lo - 1:-1],
                             ACT.Copy).then_inc(s["urv_ready"], 1)
            a.wait_ge(s["ut_done"], 1)
            a.activation(UT[:, 0:4, :], PS[:, 4, 0:512].rearrange("p (i m) -> p i m", i=4), ACT.Copy).then_inc(s["ut_ready"], 1)
            for u in range(0, 64, 2):
                a.wait_ge(s["u_done"], u + 1)
                if u >= 8:
                    a.wait_ge(s["mix_done"], u // 4 - 1)
                a.activation(UEV[:, u % 8, :], bank(u % 6), ACT.Copy).then_inc(s["uev_act"], 1)

        @block.vector
        def _(v):
            nln = 0

            def norm(k, src, dst, dst_free=None):
                for h in range(2):
                    v.wait_ge(s["ln_mean"], 2 * k + h + 1)
                    v.tensor_tensor(half(XC, h), half(src, h), bank(h), ALU.subtract).then_inc(s["ln_cent"], 1)
                for h in range(2):
                    v.wait_ge(s["ln_sd"], 2 * k + h + 1)
                    v.reciprocal(half(RS, h), half(SD, h)).then_inc(s["ln_chain"], 1)
                    v.wait_ge(s["ln_chain"], 2 * k + h + 1)
                    v.tensor_tensor(dst(h), half(XC, h), half(RS, h), ALU.mult).then_inc(s["ln_out"], 1)

            nw = 0

            def wl(ins):
                nonlocal nw
                nw += 1
                ins.then_inc(s["w_chain"], 1)
                v.wait_ge(s["w_chain"], nw)

            v.wait_ge(s["par_in"], 16)
            wl(v.tensor_tensor(WSM[:, 0:4], par_("lw", 0, 4), par_("gu", 0, 4), ALU.add))
            v.tensor_reduce(WSM[:, 13:14], WSM[:, 0:4], AX.X, ALU.max).then_inc(s["bn_chain"], 1)
            v.wait_ge(s["bn_chain"], 1)
            wl(v.tensor_scalar(WSM[:, 4:8], WSM[:, 0:4], WSM[:, 13:14], None, ALU.subtract))
            v.memset(WSM[:, 16:24], -1.0).then_inc(s["bn_chain"], 1)
            v.wait_ge(s["bn_chain"], 2)
            v.wait_ge(s["wexp"], 1)
            v.wait_ge(s["con_in"], 16)
            wl(v.reciprocal(WSM[:, 14:15], WSM[:, 12:13]))
            wl(v.tensor_scalar(WSM[:, 16:20], WSM[:, 8:12], WSM[:, 14:15], None, ALU.mult))
            wl(v.max(MX8[:, :], WSM[:, 16:24]))
            wl(v.max_index(WIX[:, :], MX8[:, :], WSM[:, 16:24]))
            wl(v.tensor_copy(WSM[:, 15:16], WIX[:, 0:1]))
            wl(v.tensor_scalar(WSM[:, 28:32], con_("iota", 4), WSM[:, 15:16], None, ALU.is_equal))
            wl(v.tensor_tensor(WSM[:, 32:36], WSM[:, 28:32], WSM[:, 16:20], ALU.subtract))
            v.tensor_tensor(WSM[:, 24:28], WSM[:, 32:36], WSM[:, 16:20], ALU.add).then_inc(s["w_soft"], 1)

            v.wait_ge(s["x_in"], 16)
            norm(0, X, lambda h: half(XN, h))

            nb = 2

            def bl(ins):
                nonlocal nb
                nb += 1
                ins.then_inc(s["bn_chain"], 1)
                v.wait_ge(s["bn_chain"], nb)

            v.wait_ge(s["sum_in"], 32)
            v.tensor_reduce(BN[:, 2:3], WA1R[:, :], AX.X, ALU.add)
            bl(v.tensor_reduce(BN[:, 3:4], WA2R[:, :], AX.X, ALU.add))
            v.wait_ge(s["bn_sd"], 1)
            bl(v.reciprocal(BN[:, 4:6], BN[:, 0:2]))
            bl(v.tensor_tensor(BN[:, 6:8], BN[:, 4:6], par_("g", 0, 2), ALU.mult))
            v.tensor_scalar(BN[:, 8:10], BN[:, 6:8], -1.0, None, ALU.mult)
            bl(v.scalar_tensor_tensor(BN[:, 12:14], BN[:, 2:4], con_("dmask", 1), par_("mu", 0, 2), ALU.mult, ALU.subtract))
            bl(v.tensor_tensor(BN[:, 14:16], BN[:, 12:14], BN[:, 6:8], ALU.mult))
            v.tensor_tensor(BN[:, 10:12], BN[:, 14:16], par_("be", 0, 2), ALU.add).then_inc(s["bn_ready"], 1)

            v.wait_ge(s["c1_done"], 2)
            v.tensor_copy(half(Y1, 1), bank(5)).then_inc(s["y1_ready"], 1)
            v.wait_ge(s["y1_ready"], 2)
            v.wait_ge(s["wa1_in"], 32)
            for g in range(8):
                slot = g % RG
                if g >= RG:
                    v.wait_ge(s["ring_free"], g - RG + 1)
                for cg in range(4):
                    if not on_scalar(g, cg):
                        co = 8 * cg + g
                        v.tensor_scalar(RING[:, 4 * slot + cg, :], Y1[:, :], WA1[:, co:co + 1], None,
                                        ALU.max).then_inc(s["dve_unit"], 1)

            v.wait_ge(s["adder_done"], 1)
            v.wait_ge(s["bn_ready"], 1)
            v.tensor_scalar(half(SD, 1), bank(7), BN[:, 8:9], BN[:, 10:11], ALU.mult, ALU.add).then_inc(s["q_chain"], 1)
            v.wait_ge(s["q_chain"], 1)
            v.wait_ge(s["pads"], 2)
            v.tensor_scalar(rows(H1P, 1, 1, 1), grid(half(SD, 1)), 0.0, None, ALU.max).then_inc(s["h1_ready"], 1)
            v.wait_ge(s["mask_in"], 32)
            nk = 0

            def kl(ins):
                nonlocal nk
                nk += 1
                ins.then_inc(s["key_chain"], 1)
                v.wait_ge(s["key_chain"], nk)

            v.tensor_copy(AMF[0:1, :], AMT[0:1, :])
            kl(v.tensor_copy(KEYT[0:1, :], FMT[0:1, :]))
            kl(v.scalar_tensor_tensor(KEYT[0:1, :], KEYT[0:1, :], 2.0, AMF[0:1, :], ALU.mult, ALU.add))
            kl(v.tensor_scalar(AMF[0:1, :], KEYT[0:1, :], 0.0, None, ALU.is_gt))
            kt = KEYT[0:1, :].rearrange("p (o b) -> p o b", o=NOPS)
            af = AMF[0:1, :].rearrange("p (o b) -> p o b", o=NOPS)
            b4 = con_("blk4", NB, 1).unsqueeze(1).to_broadcast([1, NOPS, NB])
            kl(v.tensor_tensor(af, af, b4, ALU.mult))
            v.tensor_tensor(kt, kt, af, ALU.add).then_inc(s["key_ready"], 1)
            v.memset(PREV[0:1, :], 1e6).then_inc(s["key_ready"], 1)

            v.wait_ge(s["cw_in"], 32)
            v.tensor_reduce(WMX[:, 0:1], CW1[:, :], AX.X, ALU.max, apply_absolute_value=True).then_inc(s["wmx_part"], 1)
            v.tensor_reduce(WMX[:, 1:2], CW2[:, :], AX.X, ALU.max, apply_absolute_value=True).then_inc(s["wmx_part"], 1)
            v.wait_ge(s["wmx_rows"], 1)
            v.tensor_reduce(WRW[0:1, :], PS[0:1, 0, 0:256].rearrange("p (a b) -> p a b", a=2), AX.X, ALU.max).then_inc(s["wmx_row"], 1)
            v.wait_ge(s["wmx_bc"], 1)
            nq = 1

            def ql(ins):
                nonlocal nq
                nq += 1
                ins.then_inc(s["q_chain"], 1)
                v.wait_ge(s["q_chain"], nq)

            ql(v.tensor_scalar(QS[:, 0:2], PS[:, 1, 0:2], 1.0 / 127.0, None, ALU.mult))
            v.reciprocal(QS[:, 2:4], QS[:, 0:2]).then_inc(s["q_sc"], 1)
            ql(v.reciprocal(QS[:, 4:7], par_("sc", 0, 3)))
            ql(v.tensor_tensor(QS[:, 8:10], QS[:, 0:2], par_("sc", 0, 2), ALU.mult))
            ql(v.reciprocal(QS[:, 12:14], QS[:, 8:10]))
            ql(v.tensor_tensor(QS[:, 14:16], par_("cb", 0, 2), QS[:, 12:14], ALU.mult))
            ql(v.tensor_scalar(QS[:, 14:16], QS[:, 14:16], -2.0 ** 31, 2.0 ** 31, ALU.max, ALU.min))
            ql(v.tensor_scalar(QS[:, 16:18], QS[:, 14:16], MAGIC, -MAGIC, ALU.add, ALU.add))
            ql(v.tensor_tensor(QS[:, 18:20], QS[:, 14:16], QS[:, 14:16], ALU.mult))
            ql(v.tensor_scalar(QS[:, 18:20], QS[:, 18:20], 2.0 ** 44, None, ALU.is_lt))
            ql(v.tensor_tensor(QS[:, 16:18], QS[:, 16:18], QS[:, 14:16], ALU.subtract))
            ql(v.tensor_tensor(QS[:, 16:18], QS[:, 16:18], QS[:, 18:20], ALU.mult))
            ql(v.tensor_tensor(QS[:, 16:18], QS[:, 16:18], QS[:, 14:16], ALU.add))
            ql(v.tensor_tensor(QS[:, 10:12], QS[:, 16:18], QS[:, 8:10], ALU.mult))

            v.wait_ge(s["c2_done"], 2)
            v.tensor_copy(rows(Y2P, 1, 1, 1), grid(bank(5))).then_inc(s["y2_ready"], 1)
            v.wait_ge(s["y2_ready"], 2)
            v.wait_ge(s["w_a_in"], 16)
            with v.Fori(0, 3) as dh:
                for dw in range(3):
                    win = Y2P[:, ds(dh * PS_ + dw, SIDE * PS_)].rearrange("p (a b) -> p a b", b=PS_)[:, :, 0:SIDE]
                    for g in range(8):
                        slot = (8 * (dw + 1) + g) % RG
                        v.wait_ge(s["ring_free"], dh * 24 + (8 * (dw + 1) + g - RG + 1))
                        for cg in range(4):
                            if not on_scalar(g, cg):
                                co = 8 * cg + g
                                v.tensor_scalar(grid(RING[:, 4 * slot + cg, :]), win,
                                                WA2[:, ds(dh * 96 + (32 * dw + co), 1)], None, ALU.max).then_inc(s["dve_unit"], 1)
            v.wait_ge(s["adder_done"], 2)
            ql(v.tensor_scalar(half(SD, 1), bank(7), BN[:, 9:10], BN[:, 11:12], ALU.mult, ALU.add))
            v.tensor_scalar(half(SQ, 1), half(SD, 1), 0.0, None, ALU.max).then_inc(s["h2_ready"], 1)
            for h in range(2):
                v.wait_ge(s["perm_done"], h + 1)
                v.tensor_tensor(half(XC, h), bank(4 + h), half(XN, h), ALU.add).then_inc(s["x1_tmp"], 1)
                v.wait_ge(s["x1_tmp"], h + 1)
                v.scalar_tensor_tensor(half(X1, h), half(XC, h), 0.0, half(X, h), ALU.max, ALU.add).then_inc(s["x1_ready"], 1)
            v.wait_ge(s["x1_ready"], 2)
            norm(1, X1, lambda h: half(H, h))

            def decide(count):
                v.wait_ge(s["row_done"], count)
                v.tensor_copy(ROW[0:1, :], PS[0:1, 6, 0:32])
                v.drain()
                v.max(MX8[0:1, :], ROW[0:1, 0:NOPS])
                v.drain()
                v.max_index(IX8[0:1, :], MX8[0:1, :], ROW[0:1, 0:NOPS])
                v.drain()
                op = v.value_load(IX8[0:1, 0:1], min_val=0, max_val=NOPS - 1)
                v.scalar_tensor_tensor(CAND[0:1, 0:NB], con_("blk4", NB, 1), PREV[0:1, :],
                                       KEYT[0:1, ds(op * NB, NB)], ALU.is_lt, ALU.mult)
                v.drain()
                v.tensor_reduce(KMAX[0:1, :], CAND[0:1, 0:NB], AX.X, ALU.max)
                v.drain()
                v.tensor_copy(KINT[0:1, :], KMAX[0:1, :]).then_inc(s["decided"], 1)
                v.drain()
                v.tensor_single_scalar(PINT[0:1, :], KINT[0:1, :], 0x7ffffffc, ALU.bitwise_and)
                v.drain()
                v.tensor_copy(PREV[0:1, :], PINT[0:1, :])
                v.drain()

            v.wait_ge(s["key_ready"], 2)
            decide(1)
            code = v.alloc_register("v_code"); na = v.alloc_register("v_na"); nf = v.alloc_register("v_nf")
            v.wait_ge(s["decided"], 1)
            v.load(code, KINT[0:1, 0:1], bass_reorder=False)
            chosen = v.alloc_register("v_chosen")
            v.reg_mov(chosen, 1)
            v.reg_mov(na, 0); v.reg_mov(nf, 0)
            with active_steps(v, code) as c:
                with v.If((c & 1) > 0):
                    k = v.snap(na, min_val=0, max_val=NB)
                    v.wait_ge(s["att_proj"], k * 4 + 4)
                    for b in range(NIMG):
                        q = slice(32 * b, 32 * b + 32)
                        v.tensor_copy(KZ[q, b, :].rearrange("p (h t) -> p h t", h=2), PS[q, 2:4, 0:HT]).then_inc(s["kz_done"], 1)
                    v.wait_ge(s["v_proj"], k + 1)
                    v.tensor_copy(VT[0:QT, 0:4, :], PS[0:QT, 6, 0:512].rearrange("p (j m) -> p j m", j=4))
                    v.tensor_copy(VT[0:QT, 4:7, :], PS[0:QT, 7, 0:384].rearrange("p (j m) -> p j m", j=3)).then_inc(s["v_done"], 1)
                    for u in range(4 * NQ):
                        v.wait_ge(s["s_done"], k * 28 + (u + 1))
                        pr = 2 * (u % 3)
                        v.tensor_reduce(SMX[0:QT, u:u + 1], PS[0:QT, pr:pr + 2, 0:HT], AX.XY, ALU.max).then_inc(s["smax_done"], 1)
                    v.wait_ge(s["pv_done"], k * NQ + NQ)
                    for h in range(2):
                        v.reciprocal(half(RS, h), bank(6 + h)).then_inc(s["att_rs"], 1)
                        v.wait_ge(s["att_rs"], k * 2 + (h + 1))
                        v.tensor_tensor(half(YA, h), bank(4 + h), half(RS, h), ALU.mult).then_inc(s["att_y"], 1)
                    v.wait_ge(s["att_wo"], k * 2 + 2)
                    v.tensor_copy(half(H, 1), bank(1)).then_inc(s["att_h"], 1)
                    v.reg_add(na, na, 1)
                with v.If((c & 2) > 0):
                    k = v.snap(nf, min_val=0, max_val=NB)
                    v.wait_ge(s["ffn_w"], k * 64 + 64)
                    for u in range(1, 8, 2):
                        v.wait_ge(s["ffn_h1"], k * 8 + (u + 1))
                        v.tensor_scalar(HIDT[:, u, :], bank(u % 4), B1S[:, :], 0.0, ALU.add, ALU.max).then_inc(s["hid_dve"], 1)
                    v.wait_ge(s["ffn_out"], k * 2 + 2)
                    v.tensor_scalar(half(H, 1), bank(5), B2S[:, :], None, ALU.add).then_inc(s["ffn_h"], 1)
                    v.reg_add(nf, nf, 1)
                n = v.snap(chosen, min_val=1, max_val=NB)
                decide(n + 1)
                v.reg_add(chosen, chosen, 1)
                v.load(code, KINT[0:1, 0:1], bass_reorder=False)

            v.tensor_tensor(X[:, :], X1[:, :], H[:, :], ALU.add).then_inc(s["x2_ready"], 1)
            v.wait_ge(s["x2_ready"], 1)
            norm(2, X, lambda h: half(XN, h))

            def quantise(src, dst, recip, low, high, tmp):
                ql(v.tensor_scalar(tmp, src, recip, low, ALU.mult, ALU.max))
                ql(v.tensor_scalar(tmp, tmp, high, MAGIC, ALU.min, ALU.add))
                return v.tensor_scalar(dst, grid(tmp) if len(dst.shape) == 3 else tmp, -MAGIC, None, ALU.add)

            v.wait_ge(s["pads"], 3)
            for h in range(2):
                v.wait_ge(s["ln_out"], 4 + h + 1)
                quantise(half(XN, h), rows(XQP, h, 1, 1), QS[:, 4:5], -128.0, 127.0, half(SD, h)).then_inc(s["q_xin"], 1)
            for h in range(2):
                v.wait_ge(s["cv_relu"], h + 1)
                quantise(half(SQ, h), rows(HQP, h, 1, 1), QS[:, 5:6], 0.0, 255.0, half(XC, h)).then_inc(s["cv_q"], 1)
            for h in range(2):
                v.wait_ge(s["cv_relu"], 2 + h + 1)
                ql(quantise(half(SQ, h), half(RS, h), QS[:, 6:7], 0.0, 255.0, half(SD, h)))
                v.scalar_tensor_tensor(half(X1, h), half(RS, h), par_("sc", 2), half(X, h), ALU.mult, ALU.add).then_inc(s["x3_ready"], 1)
            v.wait_ge(s["x3_ready"], 2)
            v.wait_ge(s["zeroed"], 11)
            norm(3, X1, lambda h: UPZ[:, 2 + h * HT:2 + (h + 1) * HT])
            v.wait_ge(s["ut_done"], 2)
            v.tensor_copy(UT[:, 4:8, :], PS[:, 5, 0:512].rearrange("p (i m) -> p i m", i=4)).then_inc(s["ut_ready"], 1)
            for u in range(1, 64, 2):
                v.wait_ge(s["u_done"], u + 1)
                if u >= 8:
                    v.wait_ge(s["mix_done"], u // 4 - 1)
                v.tensor_copy(UEV[:, u % 8, :], bank(u % 6)).then_inc(s["uev_dve"], 1)
            v.wait_ge(s["mix_done"], 16)
            x3 = X1[:, :].rearrange("p (t a) -> p t a", a=2)
            y = Y1[:, :].rearrange("p (t a) -> p t a", a=2)
            for a2 in range(2):
                v.tensor_tensor(y[:, :, a2], x3[:, :, a2], bank(6 + a2), ALU.add).then_inc(s["y_ready"], 1)

        @block.tensor
        def _(t):
            def mm(out_, lhsT, rhs, start=True, stop=True):
                return t.matmul(out_, lhsT, rhs, start=start, stop=stop, skip_group_check=True)

            def norm(k, src):
                for h in range(2):
                    mm(bank(h), con_("bones"), half(src, h)).then_inc(s["ln_mean"], 1)
                for h in range(2):
                    t.wait_ge(s["ln_sq"], 2 * k + h + 1)
                    mm(bank(2 + h), con_("bones"), half(SQ, h)).then_inc(s["ln_var"], 1)

            t.wait_ge(s["con_in"], 16)
            t.wait_ge(s["x_in"], 16)
            norm(0, X)
            t.wait_ge(s["wa1_in"], 32)
            for h in range(2):
                t.wait_ge(s["ln_out"], h + 1)
                mm(bank(4 + h), WS1[:, :], half(XN, h)).then_inc(s["c1_done"], 1)

            def group(g, slot):
                for h in range(2):
                    for cg in range(4):
                        last = mm(PS[32 * cg:32 * cg + 32, 6 + h, 0:HT], SEL[on_scalar(g, cg)][:, g, :],
                                  half(RING[:, 4 * slot + cg, :], h), start=False, stop=False)
                return last

            t.wait_ge(s["y1_ready"], 2)
            for h in range(2):
                mm(bank(6 + h), con_("corr"), half(Y1, h))
            for g in range(8):
                t.wait_ge(s["dve_unit"], DVE_BY[g + 1])
                t.wait_ge(s["act_unit"], ACT_BY[g + 1])
                last = group(g, g % RG)
                last.then_inc(s["ring_free"], 1)
            mm(PS[0:1, 5, 500:501], CON[:, 0:1], CON[:, 0:1]).then_inc(s["adder_done"], 1)
            t.wait_ge(s["ws2_in"], 16)
            t.wait_ge(s["h1_ready"], 2)
            for h in range(2):
                for tap in range(9):
                    last = mm(grid(bank(4 + h)), WS2[:, tap, :], rows(H1P, h, tap // 3, tap % 3), tap == 0, tap == 8)
                last.then_inc(s["c2_done"], 1)
            t.wait_ge(s["wmx_part"], 2)
            for i in range(2):
                last = mm(PS[0:1, 0, 128 * i:128 * i + 128], WMX[:, i:i + 1], con_("ident"))
            last.then_inc(s["wmx_rows"], 1)
            t.wait_ge(s["wmx_row"], 1)
            mm(PS[:, 1, 0:2], con_("ones", P, 1), WRW[0:1, :]).then_inc(s["wmx_bc"], 1)

            t.wait_ge(s["y2_ready"], 2)
            for h in range(2):
                mm(grid(bank(6 + h)), con_("zero"), rows(Y2P, h, 1, 1))
            with t.Fori(0, 3) as dh:
                for dw in range(3):
                    for g in range(8):
                        t.wait_ge(s["dve_unit"], dh * (3 * DVE_TAP) + (DVE_TAP * (dw + 1) + DVE_BY[g + 1]))
                        t.wait_ge(s["act_unit"], dh * (3 * ACT_TAP) + (ACT_TAP * (dw + 1) + ACT_BY[g + 1]))
                        group(g, (8 * (dw + 1) + g) % RG).then_inc(s["ring_free"], 1)
            t.wait_ge(s["xs9_ready"], 1)
            for h in range(2):
                last = mm(bank(6 + h), con_("corr"), half(XS9, h), start=False, stop=False)
            last.then_inc(s["adder_done"], 1)
            t.wait_ge(s["h2_ready"], 2)
            for h in range(2):
                mm(bank(4 + h), con_("perm"), half(SQ, h)).then_inc(s["perm_done"], 1)
            t.wait_ge(s["x1_ready"], 2)
            norm(1, X1)
            t.wait_ge(s["ln_out"], 4)

            def token_row():
                mm(PS[0:1, 6, 0:32], H[:, 0:1], con_("ident", 32)).then_inc(s["row_done"], 1)

            token_row()
            t.wait_ge(s["decided"], 1)
            code = t.alloc_register("t_code"); na = t.alloc_register("t_na"); nf = t.alloc_register("t_nf")
            t.load(code, KINT[0:1, 0:1], bass_reorder=False)
            t.reg_mov(na, 0); t.reg_mov(nf, 0)
            chosen = t.alloc_register("t_chosen")
            t.reg_mov(chosen, 1)
            with active_steps(t, code) as c:
                with t.If((c & 1) > 0):
                    k = t.snap(na, min_val=0, max_val=NB)
                    t.wait_ge(s["zeroed"], 9)
                    t.wait_ge(s["att_diag"], k * 4 + 4)
                    for i in range(2):
                        for h in range(2):
                            mm(bank(2 * i + h), W4B[:, i, :], half(H, h)).then_inc(s["att_proj"], 1)
                    for j in range(NQ):
                        last = mm(PS[0:QT, 6 + j // 4, P * (j % 4):P * (j % 4) + P], H[:, QT * j:QT * j + QT], W4B[:, 2, :])
                    last.then_inc(s["v_proj"], 1)
                    t.wait_ge(s["qz_done"], k * 4 + 4)
                    t.wait_ge(s["kz_done"], k * 4 + 4)
                    t.wait_ge(s["att_pad"], k * 4 + 4)
                    t.wait_ge(s["v_done"], k + 1)
                    for b in range(NIMG):
                        for j in range(NQ):
                            u = b * NQ + j
                            if u >= 3:
                                t.wait_ge(s["smax_done"], k * 28 + (u - 2))
                            for h in range(2):
                                last = mm(PS[0:QT, 2 * (u % 3) + h, 0:HT], QZ[:, b, QT * j:QT * j + QT], half(KZ[:, b, :], h))
                            last.then_inc(s["s_done"], 1)
                        t.wait_ge(s["smax_done"], k * 28 + NQ * (b + 1))
                        r = 32 * ((b + 1) % NIMG)
                        for j in range(NQ):
                            last = mm(PS[r:r + 1, 6 + j // 4, QT * (j % 4):QT * (j % 4) + QT],
                                      SMX[0:QT, b * NQ + j:b * NQ + j + 1], con_("nident", QT, QT))
                        last.then_inc(s["mrow_done"], 1)
                    t.wait_ge(s["mrow_cp"], k * 4 + 4)

                    def weigh(j):
                        t.wait_ge(s["exp_done"], k * 28 + (4 * j + 4))
                        for half_sum in range(2):
                            for h in range(2):
                                for b in range(NIMG):
                                    w = con_("ones", C, QT) if half_sum else VT[0:QT, j, 32 * b:32 * b + 32]
                                    last = mm(PS[32 * b:32 * b + 32, 4 + 2 * half_sum + h, 0:HT], w,
                                              half(PT[0:QT, 4 * (j % 2) + b, :], h), j == 0, j == NQ - 1)
                        last.then_inc(s["pv_done"], 1)

                    for j in range(NQ):
                        for b in range(NIMG):
                            u = 4 * j + b
                            if u >= 2:
                                t.wait_ge(s["exp_done"], k * 28 + (u - 1))
                            for h in range(2):
                                last = mm(PS[0:QT, 2 * (u % 2) + h, 0:HT], KZ[:, b, QT * j:QT * j + QT], half(QZ[:, b, :], h))
                            last.then_inc(s["st_done"], 1)
                        if j:
                            weigh(j - 1)
                    weigh(NQ - 1)
                    for h in range(2):
                        t.wait_ge(s["att_y"], k * 2 + (h + 1))
                        mm(bank(h), W4B[:, 3, :], half(YA, h)).then_inc(s["att_wo"], 1)
                    t.wait_ge(s["att_h"], k * 2 + 2)
                    t.reg_add(na, na, 1)
                with t.If((c & 2) > 0):
                    k = t.snap(nf, min_val=0, max_val=NB)
                    t.wait_ge(s["ffn_diag"], k * 4 + 4)
                    for h in range(2):
                        for b in range(NIMG):
                            u = 4 * h + b
                            if u >= 4:
                                t.wait_ge(s["hid_act" if u % 2 == 0 else "hid_dve"], k * 4 + (u - 4) // 2 + 1)
                            mm(bank(u % 4), W1B[:, b, :], half(H, h)).then_inc(s["ffn_h1"], 1)
                    for h in range(2):
                        t.wait_ge(s["hid_act"], k * 4 + 2 * h + 2)
                        t.wait_ge(s["hid_dve"], k * 4 + 2 * h + 2)
                        for b in range(NIMG):
                            last = mm(PS[32 * b:32 * b + 32, 4 + h, 0:HT], W2S[:, :], HIDT[:, 4 * h + b, :])
                        last.then_inc(s["ffn_out"], 1)
                    t.wait_ge(s["ffn_h"], k * 2 + 2)
                    t.reg_add(nf, nf, 1)
                token_row()
                n = t.snap(chosen, min_val=1, max_val=NB)
                t.wait_ge(s["decided"], n + 1)
                t.reg_add(chosen, chosen, 1)
                t.load(code, KINT[0:1, 0:1], bass_reorder=False)

            t.wait_ge(s["x2_ready"], 1)
            norm(2, X)
            t.wait_ge(s["cq_done"], 2)
            t.wait_ge(s["q_xin"], 2)
            for i, (w, src) in enumerate(((CQ1, XQP), (CQ2, HQP))):
                if i:
                    t.wait_ge(s["cv_q"], 2)
                for h in range(2):
                    for tap in range(9):
                        last = mm(grid(bank(4 + h)), w[:, P * tap:P * tap + P], rows(src, h, tap // 3, tap % 3), tap == 0, tap == 8)
                    last.then_inc(s["cc_done"], 1)
            t.wait_ge(s["x3_ready"], 2)
            norm(3, X1)
            t.wait_ge(s["ln_out"], 8)

            t.wait_ge(s["urv_ready"], 2)
            for c in range(2):
                for i in range(4):
                    a0 = 1024 - 255 - c - 256 * i
                    last = mm(PS[:, 4 + c, P * i:P * i + P], URV[:, a0:a0 + 255:2], con_("ident"))
                last.then_inc(s["ut_done"], 1)
            t.wait_ge(s["d_ready"], 4)
            for a2 in range(2):
                for n, (lo, hi, sgm) in enumerate(SEGS):
                    for lag in range(3):
                        c0 = 2 + a2 - lag + 2 * lo
                        last = mm(PS[:, 6 + a2, lo:hi], MUB[:, 3 * sgm + lag, :], UPZ[:, c0:c0 + 2 * (hi - lo) - 1:2],
                                  start=(n == 0 and lag == 0), stop=False)
            last.then_inc(s["ar_done"], 1)
            t.wait_ge(s["ut_ready"], 2)
            t.wait_ge(s["strip_in"], 32)

            def filtered(u):
                grp, b = u // 4, u % 4
                g, a2, odd = grp // 4, (grp // 2) % 2, grp % 2
                c = a2 ^ odd
                if u >= 6:
                    t.wait_ge(s["uev_act" if u % 2 == 0 else "uev_dve"], (u - 6) // 2 + 1)
                for i in range(4):
                    n = NPH - P * i
                    for kk in range(4):
                        k = 4 * g + kk
                        if not odd:
                            m = HE[:, k, 0:n]
                        else:
                            m = HO[:, k, 1:1 + n] if a2 else HO[:, k, 0:n]
                        last = mm(PS[32 * kk:32 * kk + 32, u % 6, P * i:NPH], UT[:, 4 * c + i, 32 * b:32 * b + 32], m,
                                  i == 0, i == 3)
                last.then_inc(s["u_done"], 1)

            def mixed(grp):
                g, a2, odd = grp // 4, (grp // 2) % 2, grp % 2
                t.wait_ge(s["uev_act"], 2 * grp + 2)
                t.wait_ge(s["uev_dve"], 2 * grp + 2)
                for lo, hi, sgm in SEGS:
                    for b in range(4):
                        last = mm(PS[32 * b:32 * b + 32, 6 + a2, lo:hi], ASEG[:, odd, sgm, 32 * g:32 * g + 32],
                                  UEV[:, (4 * grp + b) % 8, lo:hi], False, False)
                last.then_inc(s["mix_done"], 1)

            for grp in range(16):
                for b in range(4):
                    filtered(4 * grp + b)
                if grp:
                    mixed(grp - 1)
            mixed(15)


def _constants():
    import numpy as np

    con = np.zeros((P, CC["n"]), np.float32)
    p = np.arange(P)
    con[:, CC["ident"]:CC["ident"] + P] = np.eye(P)
    con[:, CC["nident"]:CC["nident"] + P] = -np.eye(P)
    con[:, CC["bones"]:CC["bones"] + P] = (p[:, None] // 32 == p[None, :] // 32) / 32.0
    for c8 in range(8):
        for b in range(4):
            con[32 * b:32 * b + 32, CC["sel1"] + 32 * c8 + 8 * b + c8] = 1.0
            con[32 * b:32 * b + 32, CC["sel2"] + 32 * c8 + 8 * b + c8] = 2.0
    for r in range(P):
        cg, b, c8 = r // 32, (r // 8) % 4, r % 8
        if not on_scalar(c8, cg):
            con[32 * b:32 * b + 32, CC["corr"] + r] = -1.0
            con[r, CC["dmask"]] = 1.0
        con[r, CC["perm"] + 32 * b + 8 * cg + c8] = 1.0
    con[:, CC["ones"]:CC["ones"] + P] = 1.0
    con[:, CC["eps5"]] = 1e-5
    con[:, CC["eps6"]] = 1e-6
    con[:, CC["iota"]:CC["iota"] + 4] = np.arange(4)
    con[:, CC["blk4"]:CC["blk4"] + NB] = 4.0 * (NB - np.arange(NB))
    return con


def _diag(w):
    import numpy as np

    z = np.zeros((NIMG, C, w.shape[1], NIMG, C), w.dtype)
    for b in range(NIMG):
        z[b, :, :, b, :] = w
    return z.reshape(P, w.shape[1], P)


def _layout(i):
    import numpy as np

    co_of_r = np.array([8 * (r // 32) + r % 8 for r in range(P)])
    img_of_r = np.array([(r // 8) % 4 for r in range(P)])
    co_of_bc = np.tile(np.arange(C), NIMG)
    par = np.zeros((P, PC["n"]), np.float32)
    for k in range(2):
        for col, name in (("g", "gamma"), ("be", "beta"), ("mu", "mean"), ("va", "var")):
            par[:, PC[col] + k] = i[f"L0_conv_bn{k + 1}_{name}"][co_of_r]
        par[:, PC["cb"] + k] = i[f"L1_conv_b{k + 1}"][co_of_bc]
    for k, name in enumerate(("s_in", "s_a1", "s_a2")):
        par[:, PC["sc"] + k] = i[f"L1_conv_{name}"][0]
    par[:, PC["lw"]:PC["lw"] + 4] = i["L1_ffn_log_weights"]
    par[:, PC["gu"]:PC["gu"] + 4] = i["L1_ffn_gumbel"]
    par[:, PC["sg"]:PC["sg"] + 4] = np.repeat(i["L1_ffn_sigma"].reshape(4, 4).T, C, axis=0)
    ws2 = i["L0_conv_w_shift2"].reshape(C, C, 9).transpose(1, 2, 0)
    ws2r = np.zeros((P, 9, P), np.float32)
    for r in range(P):
        ws2r[r, :, 32 * img_of_r[r]:32 * img_of_r[r] + 32] = ws2[co_of_r[r]]
    wa2 = i["L0_conv_w_add2"].reshape(C, C, 9)
    phi = i["L1_ffn_phi"][:T]
    phe = np.zeros((NK, LE), np.float32)
    pho = np.zeros((NK, LO), np.float32)
    phe[:, 127:] = phi[0::2].T
    pho[:, 128:] = phi[1::2].T

    def mst(m):
        return m.reshape(4, 4, 4, C, C).transpose(2, 3, 0, 1, 4).reshape(P, 4, P)

    def conv(w):
        return _diag(w.reshape(C, C, 9).transpose(1, 2, 0)).reshape(P, 9 * P)

    return {
        "x": i["x"].reshape(P, T), "par": par, "con": _constants(),
        "ws1": _diag(i["L0_conv_w_shift1"].reshape(C, 1, C).transpose(2, 1, 0)).reshape(P, P),
        "wa1c": np.tile(i["L0_conv_w_add1"].reshape(C, C).T, (NIMG, 1)),
        "wa1r": i["L0_conv_w_add1"].reshape(C, C)[co_of_r],
        "ws2": ws2r,
        "wa2c": np.tile(wa2.transpose(1, 2, 0).reshape(C, 9 * C), (NIMG, 1)),
        "wa2r": wa2.reshape(C, 9 * C)[co_of_r],
        "amt": i["L0_ffn_attn_mask"].T.reshape(1, -1),
        "fmt": i["L0_ffn_ffn_mask"].T.reshape(1, -1),
        "fw1": i["L0_ffn_ffn_w1"].reshape(NB * NOPS, C, HID), "fb1": i["L0_ffn_ffn_b1"].reshape(NB * NOPS, HID),
        "fw2": i["L0_ffn_ffn_w2"].reshape(NB * NOPS, HID, C), "fb2": i["L0_ffn_ffn_b2"].reshape(NB * NOPS, C),
        "wq": i["L0_ffn_wq"].reshape(NB * NOPS, C, C), "wk": i["L0_ffn_wk"].reshape(NB * NOPS, C, C),
        "wv": i["L0_ffn_wv"].reshape(NB * NOPS, C, C), "wo": i["L0_ffn_wo"].reshape(NB * NOPS, C, C),
        "cw1": conv(i["L1_conv_w1"]), "cw2": conv(i["L1_conv_w2"]), "phe": phe, "pho": pho,
        "mpp": mst(i["L1_ffn_M_phi_plus"]), "mpm": mst(i["L1_ffn_M_phi_minus"]),
        "mu": i["L1_ffn_M_u"].transpose(2, 0, 1, 3).reshape(C, 4, 96),
    }


def kernel(**inputs):
    import numpy as np
    import concourse.bacc as bacc
    from concourse.bass_utils import run_bass_kernel_spmd

    arrays = {k: np.ascontiguousarray(v) for k, v in _layout({k: np.asarray(v) for k, v in inputs.items()}).items()}
    nc = bacc.Bacc("TRN2", target_bir_lowering=False, num_devices=1)
    args = [nc.dram_tensor(f"in_{n}", a.shape, mybir.dt.from_np(a.dtype), kind="ExternalInput").ap() for n, a in arrays.items()]
    out = nc.dram_tensor("out_y", (P, T), F32, kind="ExternalOutput").ap()
    build(nc, *args, out)
    r = run_bass_kernel_spmd(nc, [{f"in_{n}": a for n, a in arrays.items()}], core_ids=[0])
    return r.results[0]["out_y"].reshape(NIMG, C, SIDE, SIDE)
```

```python
from contextlib import ExitStack, contextmanager

import concourse.bass as bass
from concourse import mybir

F32 = mybir.dt.float32
BF16 = mybir.dt.bfloat16
I32 = mybir.dt.int32
U32 = mybir.dt.uint32
U8 = mybir.dt.uint8
ALU = mybir.AluOpType
ACT = mybir.ActivationFunctionType
AX = mybir.AxisListType
ds = bass.ds

P = 128
NIMG, C, SIDE = 4, 32, 28
T = SIDE * SIDE
QU = T // 4
HT = T // 2
HROWS = SIDE // 2
PS_ = SIDE + 2
PADF = 904
NB, NOPS, HID = 33, 19, 128
STEPS = (3, 4, 3)
QT, NQ = 112, 7
NK = 16
NPH = T // 2
LE, LO = NPH + 127, NPH + 128
MAGIC = 12582912.0
SCALE = float(C) ** -0.5
SEGS = [(0, 49, 3), (49, 98, 2), (98, 196, 1), (196, 392, 0)]

PC = dict(g=0, be=2, mu=4, va=6, cb=8, sc=10, lw=13, gu=17, sg=21, n=25)
_c, CC = 0, {}
for _n, _w in (("bones", 128), ("vsel", 32), ("spread", 512), ("eps5", 1), ("eps6", 1), ("head", 0), ("ident", 128), ("nident", 128), ("sel1", 256), ("sel2", 256), ("corr", 128),
               ("perm", 128), ("zero", 128), ("ones", 128), ("dsel", 128), ("dmask", 1),
               ("iota", 4), ("blk4", NB)):
    CC[_n] = _c
    _c += _w
CC["n"] = _c


def on_scalar(c8, cg):
    return (c8 + 2 * cg) % 8 in (0, 3, 6) or (c8, cg) == (5, 0)


RG = 3
DVE_BY = [0]
ACT_BY = [0]
for _c8 in range(8):
    _a = sum(on_scalar(_c8, _g) for _g in range(4))
    ACT_BY.append(ACT_BY[-1] + _a)
    DVE_BY.append(DVE_BY[-1] + 4 - _a)
KINDS = ((2, 0, 0, 1, 0, 0, 1), (0, 2, 1, 0, 1, 0, 1), (1, 0, 1, 2, 0, 1, 0), (0, 1, 1, 0, 2, 1, 0))


def _row_plan():
    units = []
    for cg in range(4):
        on_act = [c8 for c8 in range(8) if on_scalar(c8, cg)]
        on_dve = [c8 for c8 in range(8) if not on_scalar(c8, cg)]
        acts = [(c8, (dw,)) for dw in range(3) for c8 in on_act]
        pairs = [(c8, (0, 1)) for c8 in on_dve[:3]]
        ones = [(c8, (2,)) for c8 in on_dve[:3]] + [(c8, (dw,)) for dw in range(3) for c8 in on_dve[3:]]
        units.append([(acts, ones, pairs)[KINDS[cg][p % 7]].pop(0) for p in range(21)])
    return [[units[cg][p] for cg in range(4)] for p in range(21)]


PLAN = _row_plan()
GROUPS = len(PLAN)
assert GROUPS % RG == 0
DVE_ROW = [0]
ACT_ROW = [0]
for _units in PLAN:
    _a = sum(on_scalar(_u[0], _g) for _g, _u in enumerate(_units))
    ACT_ROW.append(ACT_ROW[-1] + _a)
    DVE_ROW.append(DVE_ROW[-1] + 4 - _a)
PAIRS = sum(len(_u[1]) == 2 for _units in PLAN for _u in _units)


@contextmanager
def active_steps(e, code):
    assert STEPS[0] * STEPS[1] * STEPS[2] >= NB
    with e.Fori(0, STEPS[0]):
        with e.If(e.snap(code, min_val=0, max_val=4 * NB + 7) > 0):
            with e.Fori(0, STEPS[1]):
                with e.If(e.snap(code, min_val=0, max_val=4 * NB + 7) > 0):
                    with e.Fori(0, STEPS[2]):
                        c = e.snap(code, min_val=0, max_val=4 * NB + 7)
                        with e.If(c > 0):
                            yield c
                        e.nop()
                e.nop()
        e.nop()


def build(nc, x, par, con, ws1, wa1c, wa1r, ws2, wa2c, wa2r, amt, fmt, fw1, fb1, fw2, fb2, wq, wk, wv, wo,
          cw1, cw2, phe, pho, mpp, mpm, mu, out):
    with ExitStack() as ctx:
        def sb(name, shape, dt=F32):
            return ctx.enter_context(nc.sbuf_tensor(name, shape, dt))

        def sem(name):
            return ctx.enter_context(nc.semaphore(name))

        PS = ctx.enter_context(nc.psum_tensor("PS", [P, 8, 512], F32))

        X = sb("X", [P, T]); XN = sb("XN", [P, T]); XC = sb("XC", [P, T]); SQ = sb("SQ", [P, T])
        SD = sb("SD", [P, T]); RS = sb("RS", [P, T]); SDC = sb("SDC", [P, QU]); RSC = sb("RSC", [P, QU]); Y1 = sb("Y1", [P, T])
        H1P = sb("H1P", [P, PADF]); Y2P = sb("Y2P", [P, PADF])
        X1 = sb("X1", [P, T]); HSUM = sb("H", [P, PS_ * SIDE]); H = HSUM[:, 0:T]
        arena = sb("arena", [P, 2 * NQ * T])
        RING = arena[:, 0:4 * RG * T].rearrange("p (n t) -> p n t", n=4 * RG)
        SCR = arena[:, :].rearrange("p (n t) -> p n t", n=2 * NQ)
        HIDT = arena[:, 0:4 * T].rearrange("p (n t) -> p n t", n=8)
        UEV = arena[:, 0:4 * T].rearrange("p (n t) -> p n t", n=8)
        HE = sb("HE", [P, NK, NPH]); HO = sb("HO", [P, NK, NPH + 1])
        QZ = sb("QZ", [P, 4, T])
        PAR = sb("PAR", [P, PC["n"]]); CON = sb("CON", [P, CC["n"]])
        WS1 = sb("WS1", [P, P]); WA1 = sb("WA1", [P, C]); WA1R = sb("WA1R", [P, C])
        WS2 = sb("WS2", [P, 9, P]); WA2 = sb("WA2", [P, 9 * C]); WA2R = sb("WA2R", [P, 9 * C])
        BN = sb("BN", [P, 24])
        AMT = sb("AMT", [P, NOPS * NB], U8); FMT = sb("FMT", [P, NOPS * NB], U8)
        AMF = XC[:, 0:NOPS * NB]; KEYT = sb("KEYT", [P, NOPS * NB])
        ROW = sb("ROW", [P, 32]); MX8 = sb("MX8", [P, 8]); IX8 = sb("IX8", [P, 8], U32)
        CAND = sb("CAND", [P, 40]); KMAX = sb("KMAX", [P, 1]); PREV = sb("PREV", [P, 1])
        KINT = sb("KINT", [P, 1], I32); PINT = sb("PINT", [P, 1], I32)
        W1R = sb("W1R", [P, HID]); W1B = sb("W1B", [P, 4, HID]); W2S = sb("W2S", [P, C])
        B1S = sb("B1S", [P, 1]); B2S = sb("B2S", [P, 1])
        W4R = sb("W4R", [P, 4, C]); W4B = sb("W4B", [P, 4, P])
        VT = sb("VT", [P, NQ, P]); SMX = sb("SMX", [P, NQ])
        KEYS = Y1; TOP = SD
        AE = [X, XN, XC, SQ]
        CW1 = sb("CW1", [P, 9 * P]); CW2 = sb("CW2", [P, 9 * P])
        CQ1 = sb("CQ1", [P, 9 * P], BF16); CQ2 = sb("CQ2", [P, 9 * P], BF16)
        XQP = H1P[:, 0:PADF // 2].bitcast(BF16); HQP = H1P[:, PADF // 2:PADF].bitcast(BF16)
        WMX = sb("WMX", [P, 2]); WRW = sb("WRW", [P, 2]); QS = sb("QS", [P, 24])
        MPP = sb("MPP", [P, 4, P]); MPM = sb("MPM", [P, 4, P]); MSC = sb("MSC", [P, 4, P])
        ASEG = sb("ASEG", [P, 2, 4, P]); MUR = sb("MUR", [P, 4, 96]); MUS = sb("MUS", [P, 4, 96])
        MUB = sb("MUB", [P, 12, P]); WSM = sb("WSM", [P, 48]); WIX = sb("WIX", [P, 8], U32)
        UT = WS2[:, 0:8, :]
        XS9 = RS
        UPZ = CW1[:, 0:2 + 1024]

        URV = CW2[:, 0:1024]

        def con_(name, w=None, rows=P):
            a = CC[name]
            return CON[0:rows, a:a + (w or P)]

        def par_(name, i=0, w=1):
            return PAR[:, PC[name] + i:PC[name] + i + w]

        def half(ap, h):
            return ap[:, h * HT:(h + 1) * HT]

        def quarter(ap, q):
            return ap[:, q * QU:(q + 1) * QU]

        def rows(ap, h, dh=0, dw=0):
            v = ap[:, 0:PS_ * PS_].rearrange("p (a b) -> p a b", a=PS_)
            return v[:, h * HROWS + dh:h * HROWS + dh + HROWS, dw:dw + SIDE]

        def bank(b, w=HT, rows_=slice(0, P)):
            return PS[rows_, b, 0:w]

        def score_banks(b, j):
            return 0 if b and j == 0 else 2 * ((j + 1) % 2)

        def window(dh, dw):
            return Y2P[:, ds(dh * PS_ + dw, SIDE * PS_)].rearrange("p (a b) -> p a b", b=PS_)[:, :, 0:SIDE]

        def grid(ap):
            return ap.rearrange("p (a b) -> p a b", b=SIDE)

        SEL = {True: con_("sel1", 256).rearrange("p (c m) -> p c m", c=8),
               False: con_("sel2", 256).rearrange("p (c m) -> p c m", c=8)}

        s = {n: sem(n) for n in (
            "sp_woke x_in par_in con_in wa1_in w_a_in sum_in mask_in ws2_in cw_in strip_in mst_in "
            "ln_mean ln_cent ln_sq ln_var ln_sd ln_rs ln_bc ln_out con_head "
            "bn_sd bn_ready bn_chain pads zeroed c1_done y1_ready ring_free dve_unit pair_part act_unit adder_init adder_done "
            "h1_ready c2_done y2_ready xs9_ready xs9_chain h2_ready perm_done x1_tmp x1_ready "
            "key_chain key_ready row_done decided "
            "ffn_w att_w ffn_diag ffn_h1 hid_act hid_dve ffn_out ffn_h att_diag wo_diag att_proj keys_done qz_act qz_dve v_proj v_done "
            "st_done score_cp top_step top_tr smax_done mrow_done less_max exp_done pv_done ae_done att_den att_rs att_bc att_wo att_num att_h "
            "wmx_part wmx_rows wmx_row wmx_bc wmx_all q_sc q_chain cq_chain cq_done x2_ready q_xin cc_done cv_relu cv_q x3_ready "
            "wexp w_soft w_chain sg_ready d_chain d_ready ar_done ut_done ut_ready urv_ready u_done uev_act uev_dve mix_done y_ready stored"
        ).split()}
        ctx.enter_context(nc.allow_non_contiguous_dma("weights' rows are short"))
        block = ctx.enter_context(nc.Block())

        @block.sync
        def _(sp):
            sp.dma_start(X[:, :], x).then_inc(s["x_in"], 16)
            sp.dma_start(PAR[:, :], par).then_inc(s["par_in"], 16)
            sp.dma_start(WS1[:, :], ws1).then_inc(s["wa1_in"], 16)
            sp.dma_start(WA1[:, :], wa1c).then_inc(s["wa1_in"], 16)
            sp.dma_start(WA1R[:, :], wa1r).then_inc(s["sum_in"], 16)
            sp.dma_start(WA2R[:, :], wa2r).then_inc(s["sum_in"], 16)
            sp.dma_start(WS2[:, :, :], ws2).then_inc(s["ws2_in"], 16)
            sp.dma_start(WA2[:, :], wa2c).then_inc(s["w_a_in"], 16)
            sp.dma_start(AMT[0:1, :], amt).then_inc(s["mask_in"], 16)
            sp.dma_start(FMT[0:1, :], fmt).then_inc(s["mask_in"], 16)
            sp.dma_start(MPP[:, :, :], mpp).then_inc(s["mst_in"], 16)
            sp.dma_start(MPM[:, :, :], mpm).then_inc(s["mst_in"], 16)
            for b in range(NIMG):
                sp.dma_start(MUR[32 * b:32 * b + 32, :, :], mu).then_inc(s["mst_in"], 16)
            sp.dma_start(CW1[:, :], cw1).then_inc(s["cw_in"], 16)
            sp.dma_start(CW2[:, :], cw2).then_inc(s["cw_in"], 16)
            sp.dma_start(HE[:, :, :], bass.AP(phe.tensor, 0, [[1, P], [LE, NK], [1, NPH]])).then_inc(s["strip_in"], 16)
            sp.dma_start(HO[:, :, :], bass.AP(pho.tensor, 0, [[1, P], [LO, NK], [1, NPH + 1]])).then_inc(s["strip_in"], 16)

            sp.wait_ge(s["decided"], 1)
            code = sp.alloc_register("sp_code"); which = sp.alloc_register("sp_which")
            sp.load(code, KINT[0:1, 0:1], bass_reorder=False)
            chosen = sp.alloc_register("sp_chosen")
            sp.reg_mov(chosen, 1)
            with active_steps(sp, code) as c:
                op = sp.value_load(IX8[0:1, 0:1], min_val=0, max_val=NOPS - 1)
                sp.reg_mov(which, (NB - (c >> 2)) * NOPS + op)
                w = sp.snap(which, min_val=0, max_val=NB * NOPS - 1)
                with sp.If((c & 1) > 0):
                    for i, src in enumerate((wq, wk, wv, wo)):
                        sp.dma_start(W4R[:, i, :],
                                     src[ds(w, 1), :, :].broadcast_to([NIMG, C, C])).then_inc(s["att_w"], 16)
                    sp.nop()
                with sp.If((c & 2) > 0):
                    sp.dma_start(W1R[:, :],
                                 fw1[ds(w, 1), :, :].broadcast_to([NIMG, C, HID])).then_inc(s["ffn_w"], 16)
                    sp.dma_start(B1S[:, :], fb1[ds(w, 1), :].rearrange("a n -> n a")).then_inc(s["ffn_w"], 16)
                    sp.dma_start(W2S[:, :], fw2[ds(w, 1), :, :].rearrange("a h d -> (a h) d")).then_inc(s["ffn_w"], 16)
                    sp.dma_start(B2S[:, :],
                                 fb2[ds(w, 1), :].rearrange("a (n e) -> a n e", e=1).broadcast_to([NIMG, C, 1])
                                 ).then_inc(s["ffn_w"], 16)
                    sp.nop()
                n = sp.snap(chosen, min_val=1, max_val=NB)
                sp.wait_ge(s["decided"], n + 1)
                sp.sem_inc(s["sp_woke"], 1)
                sp.reg_add(chosen, chosen, 1)
                sp.load(code, KINT[0:1, 0:1], bass_reorder=False)

            sp.wait_ge(s["y_ready"], 2)
            sp.dma_start(out, Y1[:, :]).then_inc(s["stored"], 16)
            sp.wait_ge(s["stored"], 16)

        @block.gpsimd
        def _(g):
            hd = CC["head"]
            g.dma_start(CON[:, 0:hd], con[:, 0:hd]).then_inc(s["con_head"], 16)
            g.dma_start(CON[:, hd:], con[:, hd:]).then_inc(s["con_in"], 16)
            g.memset(H1P[:, :], 0.0).then_inc(s["pads"], 1)
            g.memset(Y2P[:, :], 0.0).then_inc(s["pads"], 1)
            g.memset(W1B[:, :, :], 0.0).then_inc(s["zeroed"], 1)
            g.memset(W4B[:, :, :], 0.0).then_inc(s["zeroed"], 1)
            g.memset(MUB[:, :, :], 0.0).then_inc(s["zeroed"], 1)
            g.memset(QZ[:, :, :], 0.0).then_inc(s["zeroed"], 1)
            g.wait_ge(s["zeroed"], 4)

            chain = 0

            def link(ins):
                nonlocal chain
                chain += 1
                ins.then_inc(s["d_chain"], 1)
                g.wait_ge(s["d_chain"], chain)

            g.wait_ge(s["mst_in"], 16 * 6)
            g.wait_ge(s["sg_ready"], 2)
            g.wait_ge(s["w_soft"], 1)
            sg = WSM[:, 40:44].unsqueeze(2).to_broadcast([P, 4, C])
            for par_i, op in enumerate((ALU.add, ALU.subtract)):
                link(g.tensor_tensor(MSC[:, :, :], MPP[:, :, :], MPM[:, :, :], op))
                for i in range(4):
                    v = MSC[:, i, :].rearrange("p (g e) -> p g e", g=4)
                    link(g.tensor_tensor(v, v, sg, ALU.mult))
                    link(g.tensor_scalar(ASEG[:, par_i, i, :], MSC[:, i, :], WSM[:, 24 + i:25 + i], None, ALU.mult))
                    if i:
                        link(g.tensor_tensor(ASEG[:, par_i, i, :], ASEG[:, par_i, i, :], ASEG[:, par_i, i - 1, :], ALU.add))
            for i in range(4):
                link(g.tensor_scalar(MUS[:, i, :], MUR[:, i, :], WSM[:, 24 + i:25 + i], None, ALU.mult))
                if i:
                    link(g.tensor_tensor(MUS[:, i, :], MUS[:, i, :], MUS[:, i - 1, :], ALU.add))
            for b in range(NIMG):
                q = slice(32 * b, 32 * b + 32)
                g.tensor_copy(MUB[q, :, q], MUS[q, :, :].rearrange("p i (l e) -> p (i l) e", e=C)).then_inc(s["d_ready"], 1)

            g.wait_ge(s["d_ready"], 4)

            g.wait_ge(s["q_sc"], 1)
            g.wait_ge(s["cw_in"], 32)
            cq = 0

            def qlink(ins):
                nonlocal cq
                cq += 1
                ins.then_inc(s["cq_chain"], 1)
                g.wait_ge(s["cq_chain"], cq)

            for i, (src, dst) in enumerate(((CW1, CQ1), (CW2, CQ2))):
                qlink(g.tensor_scalar(src[:, :], src[:, :], QS[:, 2 + i:3 + i], -128.0, ALU.mult, ALU.max))
                qlink(g.tensor_scalar(src[:, :], src[:, :], 127.0, MAGIC, ALU.min, ALU.add))
                g.tensor_scalar(dst[:, :], src[:, :], -MAGIC, None, ALU.add).then_inc(s["cq_done"], 1)

            g.wait_ge(s["cq_done"], 2)
            g.memset(UPZ, 0.0).then_inc(s["zeroed"], 1)
            g.memset(URV, 0.0).then_inc(s["zeroed"], 1)

            g.wait_ge(s["y2_ready"], 2)
            g.memset(H1P[:, :], 0.0).then_inc(s["pads"], 1)
            y2 = Y2P[:, 0:PS_ * PS_].rearrange("p (a b) -> p a b", a=PS_)
            hs = HSUM[:, :].rearrange("p (a b) -> p a b", a=PS_)
            g.tensor_tensor(hs, y2[:, :, 0:SIDE], y2[:, :, 1:1 + SIDE], ALU.add).then_inc(s["xs9_chain"], 1)
            g.wait_ge(s["xs9_chain"], 1)
            g.tensor_tensor(hs, hs, y2[:, :, 2:2 + SIDE], ALU.add).then_inc(s["xs9_chain"], 1)
            g.wait_ge(s["xs9_chain"], 2)
            xs = grid(XS9[:, :])
            g.tensor_tensor(xs, hs[:, 0:SIDE, :], hs[:, 1:1 + SIDE, :], ALU.add).then_inc(s["xs9_chain"], 1)
            g.wait_ge(s["xs9_chain"], 3)
            g.tensor_tensor(xs, xs, hs[:, 2:2 + SIDE, :], ALU.add).then_inc(s["xs9_ready"], 1)

            g.wait_ge(s["decided"], 1)
            code = g.alloc_register("g_code"); na = g.alloc_register("g_na"); nf = g.alloc_register("g_nf")
            g.load(code, KINT[0:1, 0:1], bass_reorder=False)
            g.reg_mov(na, 0); g.reg_mov(nf, 0)
            chosen = g.alloc_register("g_chosen")
            g.reg_mov(chosen, 1)
            with active_steps(g, code) as c:
                with g.If((c & 1) > 0):
                    a = g.snap(na, min_val=0, max_val=NB)
                    g.wait_ge(s["att_w"], a * 64 + 64)
                    g.reg_add(na, na, 1)
                    for b in range(NIMG):
                        q = slice(32 * b, 32 * b + 32)
                        g.tensor_copy(W4B[q, 0:3, q], W4R[q, 0:3, :]).then_inc(s["att_diag"], 1)
                with g.If((c & 2) > 0):
                    f = g.snap(nf, min_val=0, max_val=NB)
                    g.wait_ge(s["ffn_w"], f * 64 + 64)
                    g.reg_add(nf, nf, 1)
                    for b in range(NIMG):
                        q = slice(32 * b, 32 * b + 32)
                        last = g.tensor_copy(W1B[q, b, :], W1R[q, :]).then_inc(s["ffn_diag"], 1)
                n = g.snap(chosen, min_val=1, max_val=NB)
                g.wait_ge(s["decided"], n + 1)
                g.reg_add(chosen, chosen, 1)
                g.load(code, KINT[0:1, 0:1], bass_reorder=False)

        @block.scalar
        def _(a):
            def norm(k, eps):
                for h in range(2):
                    a.wait_ge(s["ln_cent"], 2 * k + h + 1)
                    a.activation(half(SQ, h), half(XC, h), ACT.Square).then_inc(s["ln_sq"], 1)
                a.wait_ge(s["ln_var"], k + 1)
                a.activation(SDC[:, :], bank(2, QU), ACT.Sqrt, bias=con_(eps, 1)).then_inc(s["ln_sd"], 1)

            a.wait_ge(s["w_chain"], 2)
            a.activation(WSM[:, 8:12], WSM[:, 4:8], ACT.Exp, accum_out=WSM[:, 12:13]).then_inc(s["wexp"], 1)
            a.wait_ge(s["par_in"], 16)
            a.wait_ge(s["con_head"], 16)
            a.activation(BN[:, 0:2], par_("va", 0, 2), ACT.Sqrt, bias=con_("eps5", 1)).then_inc(s["bn_sd"], 1)
            a.activation(WSM[:, 36:40], par_("sg", 0, 4), ACT.Sqrt).then_inc(s["sg_ready"], 1)
            a.wait_ge(s["sg_ready"], 1)
            a.activation(WSM[:, 40:44], WSM[:, 36:40], ACT.Sqrt).then_inc(s["sg_ready"], 1)
            norm(0, "eps6")
            a.wait_ge(s["c1_done"], 1)
            a.activation(half(Y1, 0), bank(4), ACT.Copy).then_inc(s["y1_ready"], 1)

            a.wait_ge(s["y1_ready"], 2)
            a.wait_ge(s["wa1_in"], 32)
            for g in range(8):
                slot = g % RG
                if g >= RG:
                    a.wait_ge(s["ring_free"], g - RG + 1)
                for cg in range(4):
                    if on_scalar(g, cg):
                        co = 8 * cg + g
                        a.activation(RING[:, 4 * slot + cg, :], Y1[:, :], ACT.Abs, bias=WA1[:, co:co + 1],
                                     scale=-1.0).then_inc(s["act_unit"], 1)
            a.wait_ge(s["adder_done"], 1)
            a.wait_ge(s["bn_ready"], 1)
            a.wait_ge(s["pads"], 2)
            a.activation(rows(H1P, 0, 1, 1), grid(bank(6)), ACT.Relu, bias=BN[:, 10:11], scale=BN[:, 8:9]).then_inc(s["h1_ready"], 1)
            a.wait_ge(s["c2_done"], 1)
            a.activation(rows(Y2P, 0, 1, 1), grid(bank(4)), ACT.Copy).then_inc(s["y2_ready"], 1)

            a.wait_ge(s["y2_ready"], 2)
            a.wait_ge(s["w_a_in"], 16)
            with a.Fori(0, 3) as dh:
                for p, units in enumerate(PLAN):
                    a.wait_ge(s["ring_free"], dh * GROUPS + (8 + p - RG + 1))
                    for cg, (c8, dws) in enumerate(units):
                        if on_scalar(c8, cg):
                            a.activation(grid(RING[:, 4 * ((8 + p) % RG) + cg, :]), window(dh, dws[0]), ACT.Abs,
                                         bias=WA2[:, ds(dh * 96 + (32 * dws[0] + 8 * cg + c8), 1)],
                                         scale=-1.0).then_inc(s["act_unit"], 1)
            a.wait_ge(s["adder_done"], 2)
            a.activation(half(SQ, 0), bank(6), ACT.Relu, bias=BN[:, 11:12], scale=BN[:, 9:10]).then_inc(s["h2_ready"], 1)
            norm(1, "eps5")

            a.wait_ge(s["decided"], 1)
            code = a.alloc_register("a_code"); na = a.alloc_register("a_na"); nf = a.alloc_register("a_nf")
            a.load(code, KINT[0:1, 0:1], bass_reorder=False)
            a.reg_mov(na, 0); a.reg_mov(nf, 0)
            chosen = a.alloc_register("a_chosen")
            a.reg_mov(chosen, 1)
            with active_steps(a, code) as c:
                with a.If((c & 1) > 0):
                    k = a.snap(na, min_val=0, max_val=NB)
                    a.wait_ge(s["att_proj"], k * 4 + 2)
                    for b in range(2):
                        q = slice(32 * b, 32 * b + 32)
                        a.activation(QZ[q, b, :].rearrange("p (h t) -> p h t", h=2), PS[q, 4:6, 0:HT],
                                     ACT.Copy).then_inc(s["qz_act"], 1)

                    def exponential(b, j):
                        a.wait_ge(s["less_max"], k * 28 + (NQ * b + j + 1))
                        tile = SCR[0:QT, NQ * (b % 2) + j, :]
                        a.activation(tile, tile, ACT.Exp, scale=SCALE).then_inc(s["exp_done"], 1)

                    def sums_out(b):
                        a.wait_ge(s["pv_done"], k * 16 + (4 * b + 4))
                        a.activation(AE[b][:, :].rearrange("p (h t) -> p h t", h=2), PS[:, 6:8, 0:HT],
                                     ACT.Copy).then_inc(s["ae_done"], 1)

                    for b in range(NIMG + 1):
                        for j in range(NQ):
                            if b < NIMG:
                                u = NQ * b + j
                                a.wait_ge(s["st_done"], k * 28 + (u + 1))
                                if b >= 2:
                                    a.wait_ge(s["pv_done"], k * 16 + (4 * (b - 2) + j // 2 + 1))
                                pr = score_banks(b, j)
                                a.activation(SCR[0:QT, NQ * (b % 2) + j, :].rearrange("p (h t) -> p h t", h=2),
                                             PS[0:QT, pr:pr + 2, 0:HT], ACT.Copy).then_inc(s["score_cp"], 1)
                            if b >= 2 and j == 0:
                                exponential(b - 2, NQ - 1)
                            if b >= 2 and j == 1:
                                sums_out(b - 2)
                            if b >= 1 and j >= 2:
                                exponential(b - 1, j - 2)
                        if b >= 1:
                            exponential(b - 1, NQ - 2)
                    exponential(NIMG - 1, NQ - 1)
                    sums_out(NIMG - 1)
                    for h in range(2):
                        a.wait_ge(s["att_wo"], k * 2 + (h + 1))
                        a.activation(half(RS, h), bank(h), ACT.Copy).then_inc(s["att_num"], 1)
                    a.reg_add(na, na, 1)
                with a.If((c & 2) > 0):
                    k = a.snap(nf, min_val=0, max_val=NB)
                    a.wait_ge(s["ffn_w"], k * 64 + 64)
                    for u in range(0, 8, 2):
                        a.wait_ge(s["ffn_h1"], k * 8 + (u + 1))
                        a.activation(HIDT[:, u, :], bank(u % 4), ACT.Relu, bias=B1S[:, :]).then_inc(s["hid_act"], 1)
                    a.wait_ge(s["ffn_out"], k * 2 + 1)
                    a.activation(half(H, 0), bank(4), ACT.Identity, bias=B2S[:, :]).then_inc(s["ffn_h"], 1)
                    a.reg_add(nf, nf, 1)
                n = a.snap(chosen, min_val=1, max_val=NB)
                a.wait_ge(s["decided"], n + 1)
                a.reg_add(chosen, chosen, 1)
                a.load(code, KINT[0:1, 0:1], bass_reorder=False)

            norm(2, "eps6")
            for i in range(2):
                for h in range(2):
                    a.wait_ge(s["cc_done"], 2 * i + h + 1)
                    a.activation(half(SQ, h), bank(4 + h), ACT.Relu, bias=QS[:, 10 + i:11 + i],
                                 scale=QS[:, 8 + i:9 + i]).then_inc(s["cv_relu"], 1)
            norm(3, "eps5")
            a.wait_ge(s["zeroed"], 6)
            for h in range(2):
                a.wait_ge(s["ln_out"], 6 + h + 1)
                lo = h * HT
                a.activation(URV[:, 1024 - lo - HT:1024 - lo], UPZ[:, 2 + lo + HT - 1:2 + lo - 1:-1],
                             ACT.Copy).then_inc(s["urv_ready"], 1)
            a.wait_ge(s["ut_done"], 1)
            a.activation(UT[:, 0:4, :], PS[:, 4, 0:512].rearrange("p (i m) -> p i m", i=4), ACT.Copy).then_inc(s["ut_ready"], 1)
            for u in range(0, 64, 2):
                a.wait_ge(s["u_done"], u + 1)
                if u >= 8:
                    a.wait_ge(s["mix_done"], u // 4 - 1)
                a.activation(UEV[:, u % 8, :], bank(u % 6), ACT.Copy).then_inc(s["uev_act"], 1)

        @block.vector
        def _(v):
            nln = 0

            def norm(k, src, dst, dst_free=None):
                for h in range(2):
                    v.wait_ge(s["ln_mean"], 2 * k + h + 1)
                    v.tensor_tensor(half(XC, h), half(src, h), bank(h), ALU.subtract).then_inc(s["ln_cent"], 1)
                v.wait_ge(s["ln_sd"], k + 1)
                v.reciprocal(RSC[:, :], SDC[:, :]).then_inc(s["ln_rs"], 1)
                for h in range(2):
                    v.wait_ge(s["ln_bc"], 2 * k + h + 1)
                    v.tensor_tensor(dst(h), half(XC, h), bank(h), ALU.mult).then_inc(s["ln_out"], 1)

            nw = 0

            def wl(ins):
                nonlocal nw
                nw += 1
                ins.then_inc(s["w_chain"], 1)
                v.wait_ge(s["w_chain"], nw)

            v.wait_ge(s["par_in"], 16)
            wl(v.tensor_tensor(WSM[:, 0:4], par_("lw", 0, 4), par_("gu", 0, 4), ALU.add))
            v.tensor_reduce(WSM[:, 13:14], WSM[:, 0:4], AX.X, ALU.max).then_inc(s["bn_chain"], 1)
            v.wait_ge(s["bn_chain"], 1)
            wl(v.tensor_scalar(WSM[:, 4:8], WSM[:, 0:4], WSM[:, 13:14], None, ALU.subtract))
            v.memset(WSM[:, 16:24], -1.0).then_inc(s["bn_chain"], 1)
            v.wait_ge(s["bn_chain"], 2)
            v.wait_ge(s["wexp"], 1)
            v.wait_ge(s["con_in"], 16)
            wl(v.reciprocal(WSM[:, 14:15], WSM[:, 12:13]))
            wl(v.tensor_scalar(WSM[:, 16:20], WSM[:, 8:12], WSM[:, 14:15], None, ALU.mult))
            wl(v.max(MX8[:, :], WSM[:, 16:24]))
            wl(v.max_index(WIX[:, :], MX8[:, :], WSM[:, 16:24]))
            wl(v.tensor_copy(WSM[:, 15:16], WIX[:, 0:1]))
            wl(v.tensor_scalar(WSM[:, 28:32], con_("iota", 4), WSM[:, 15:16], None, ALU.is_equal))
            wl(v.tensor_tensor(WSM[:, 32:36], WSM[:, 28:32], WSM[:, 16:20], ALU.subtract))
            v.tensor_tensor(WSM[:, 24:28], WSM[:, 32:36], WSM[:, 16:20], ALU.add).then_inc(s["w_soft"], 1)

            v.wait_ge(s["x_in"], 16)
            norm(0, X, lambda h: half(XN, h))

            nb = 2

            def bl(ins):
                nonlocal nb
                nb += 1
                ins.then_inc(s["bn_chain"], 1)
                v.wait_ge(s["bn_chain"], nb)

            v.wait_ge(s["sum_in"], 32)
            v.tensor_reduce(BN[:, 2:3], WA1R[:, :], AX.X, ALU.add)
            bl(v.tensor_reduce(BN[:, 3:4], WA2R[:, :], AX.X, ALU.add))
            v.wait_ge(s["bn_sd"], 1)
            bl(v.reciprocal(BN[:, 4:6], BN[:, 0:2]))
            bl(v.tensor_tensor(BN[:, 6:8], BN[:, 4:6], par_("g", 0, 2), ALU.mult))
            v.tensor_scalar(BN[:, 8:10], BN[:, 6:8], -1.0, None, ALU.mult)
            bl(v.scalar_tensor_tensor(BN[:, 12:14], BN[:, 2:4], con_("dmask", 1), par_("mu", 0, 2), ALU.mult, ALU.subtract))
            bl(v.tensor_tensor(BN[:, 14:16], BN[:, 12:14], BN[:, 6:8], ALU.mult))
            v.tensor_tensor(BN[:, 10:12], BN[:, 14:16], par_("be", 0, 2), ALU.add).then_inc(s["bn_ready"], 1)

            v.wait_ge(s["c1_done"], 2)
            v.tensor_copy(half(Y1, 1), bank(5)).then_inc(s["y1_ready"], 1)
            v.wait_ge(s["y1_ready"], 2)
            v.wait_ge(s["wa1_in"], 32)
            for g in range(8):
                slot = g % RG
                if g >= RG:
                    v.wait_ge(s["ring_free"], g - RG + 1)
                for cg in range(4):
                    if not on_scalar(g, cg):
                        co = 8 * cg + g
                        v.tensor_scalar(RING[:, 4 * slot + cg, :], Y1[:, :], WA1[:, co:co + 1], None,
                                        ALU.max).then_inc(s["dve_unit"], 1)

            v.wait_ge(s["adder_done"], 1)
            v.wait_ge(s["bn_ready"], 1)
            v.tensor_scalar(half(SD, 1), bank(7), BN[:, 8:9], BN[:, 10:11], ALU.mult, ALU.add).then_inc(s["q_chain"], 1)
            v.wait_ge(s["q_chain"], 1)
            v.wait_ge(s["pads"], 2)
            v.tensor_scalar(rows(H1P, 1, 1, 1), grid(half(SD, 1)), 0.0, None, ALU.max).then_inc(s["h1_ready"], 1)
            v.wait_ge(s["mask_in"], 32)
            nk = 0

            def kl(ins):
                nonlocal nk
                nk += 1
                ins.then_inc(s["key_chain"], 1)
                v.wait_ge(s["key_chain"], nk)

            v.tensor_copy(AMF[0:1, :], AMT[0:1, :])
            kl(v.tensor_copy(KEYT[0:1, :], FMT[0:1, :]))
            kl(v.scalar_tensor_tensor(KEYT[0:1, :], KEYT[0:1, :], 2.0, AMF[0:1, :], ALU.mult, ALU.add))
            kl(v.tensor_scalar(AMF[0:1, :], KEYT[0:1, :], 0.0, None, ALU.is_gt))
            kt = KEYT[0:1, :].rearrange("p (o b) -> p o b", o=NOPS)
            af = AMF[0:1, :].rearrange("p (o b) -> p o b", o=NOPS)
            b4 = con_("blk4", NB, 1).unsqueeze(1).to_broadcast([1, NOPS, NB])
            kl(v.tensor_tensor(af, af, b4, ALU.mult))
            v.tensor_tensor(kt, kt, af, ALU.add).then_inc(s["key_ready"], 1)
            v.memset(PREV[0:1, :], 1e6).then_inc(s["key_ready"], 1)

            v.wait_ge(s["cw_in"], 32)
            v.tensor_reduce(WMX[:, 0:1], CW1[:, :], AX.X, ALU.max, apply_absolute_value=True).then_inc(s["wmx_part"], 1)
            v.tensor_reduce(WMX[:, 1:2], CW2[:, :], AX.X, ALU.max, apply_absolute_value=True).then_inc(s["wmx_part"], 1)
            v.wait_ge(s["wmx_rows"], 1)
            v.tensor_reduce(WRW[0:1, :], PS[0:1, 0, 0:256].rearrange("p (a b) -> p a b", a=2), AX.X, ALU.max).then_inc(s["wmx_row"], 1)
            v.wait_ge(s["wmx_bc"], 1)
            nq = 1

            def ql(ins):
                nonlocal nq
                nq += 1
                ins.then_inc(s["q_chain"], 1)
                v.wait_ge(s["q_chain"], nq)

            ql(v.tensor_scalar(QS[:, 0:2], PS[:, 1, 0:2], 1.0 / 127.0, None, ALU.mult))
            v.reciprocal(QS[:, 2:4], QS[:, 0:2]).then_inc(s["q_sc"], 1)
            ql(v.reciprocal(QS[:, 4:7], par_("sc", 0, 3)))
            ql(v.tensor_tensor(QS[:, 8:10], QS[:, 0:2], par_("sc", 0, 2), ALU.mult))
            ql(v.reciprocal(QS[:, 12:14], QS[:, 8:10]))
            ql(v.tensor_tensor(QS[:, 14:16], par_("cb", 0, 2), QS[:, 12:14], ALU.mult))
            ql(v.tensor_scalar(QS[:, 14:16], QS[:, 14:16], -2.0 ** 31, 2.0 ** 31, ALU.max, ALU.min))
            ql(v.tensor_scalar(QS[:, 16:18], QS[:, 14:16], MAGIC, -MAGIC, ALU.add, ALU.add))
            ql(v.tensor_tensor(QS[:, 18:20], QS[:, 14:16], QS[:, 14:16], ALU.mult))
            ql(v.tensor_scalar(QS[:, 18:20], QS[:, 18:20], 2.0 ** 44, None, ALU.is_lt))
            ql(v.tensor_tensor(QS[:, 16:18], QS[:, 16:18], QS[:, 14:16], ALU.subtract))
            ql(v.tensor_tensor(QS[:, 16:18], QS[:, 16:18], QS[:, 18:20], ALU.mult))
            ql(v.tensor_tensor(QS[:, 16:18], QS[:, 16:18], QS[:, 14:16], ALU.add))
            ql(v.tensor_tensor(QS[:, 10:12], QS[:, 16:18], QS[:, 8:10], ALU.mult))

            v.wait_ge(s["c2_done"], 2)
            v.tensor_copy(rows(Y2P, 1, 1, 1), grid(bank(5))).then_inc(s["y2_ready"], 1)
            v.wait_ge(s["y2_ready"], 2)
            v.wait_ge(s["w_a_in"], 16)
            with v.Fori(0, 3) as dh:
                done = 0
                for p, units in enumerate(PLAN):
                    v.wait_ge(s["ring_free"], dh * GROUPS + (8 + p - RG + 1))
                    mine = [(cg, u) for cg, u in enumerate(units) if not on_scalar(u[0], cg)]
                    for cg, (c8, dws) in sorted(mine, key=lambda m: -len(m[1][1])):
                        ins = v.tensor_scalar(grid(RING[:, 4 * ((8 + p) % RG) + cg, :]), window(dh, dws[0]),
                                              WA2[:, ds(dh * 96 + (32 * dws[0] + 8 * cg + c8), 1)], None, ALU.max)
                        ins.then_inc(s["dve_unit" if len(dws) == 1 else "pair_part"], 1)
                    for cg, (c8, dws) in mine:
                        if len(dws) == 2:
                            done += 1
                            v.wait_ge(s["pair_part"], dh * PAIRS + done)
                            unit = grid(RING[:, 4 * ((8 + p) % RG) + cg, :])
                            v.scalar_tensor_tensor(unit, window(dh, dws[1]),
                                                   WA2[:, ds(dh * 96 + (32 * dws[1] + 8 * cg + c8), 1)], unit,
                                                   ALU.max, ALU.add).then_inc(s["dve_unit"], 1)
            v.wait_ge(s["adder_done"], 2)
            ql(v.tensor_scalar(half(SD, 1), bank(7), BN[:, 9:10], BN[:, 11:12], ALU.mult, ALU.add))
            v.tensor_scalar(half(SQ, 1), half(SD, 1), 0.0, None, ALU.max).then_inc(s["h2_ready"], 1)
            for h in range(2):
                v.wait_ge(s["perm_done"], h + 1)
                v.tensor_tensor(half(XC, h), bank(4 + h), half(XN, h), ALU.add).then_inc(s["x1_tmp"], 1)
                v.wait_ge(s["x1_tmp"], h + 1)
                v.scalar_tensor_tensor(half(X1, h), half(XC, h), 0.0, half(X, h), ALU.max, ALU.add).then_inc(s["x1_ready"], 1)
            v.wait_ge(s["x1_ready"], 2)
            norm(1, X1, lambda h: half(H, h))

            def decide(count):
                v.wait_ge(s["row_done"], count)
                v.tensor_copy(ROW[0:1, :], PS[0:1, 6, 0:32])
                v.drain()
                v.max(MX8[0:1, :], ROW[0:1, 0:NOPS])
                v.drain()
                v.max_index(IX8[0:1, :], MX8[0:1, :], ROW[0:1, 0:NOPS])
                v.drain()
                op = v.value_load(IX8[0:1, 0:1], min_val=0, max_val=NOPS - 1)
                v.scalar_tensor_tensor(CAND[0:1, 0:NB], con_("blk4", NB, 1), PREV[0:1, :],
                                       KEYT[0:1, ds(op * NB, NB)], ALU.is_lt, ALU.mult)
                v.drain()
                v.tensor_reduce(KMAX[0:1, :], CAND[0:1, 0:NB], AX.X, ALU.max)
                v.drain()
                v.tensor_copy(KINT[0:1, :], KMAX[0:1, :]).then_inc(s["decided"], 1)
                v.drain()
                v.tensor_single_scalar(PINT[0:1, :], KINT[0:1, :], 0x7ffffffc, ALU.bitwise_and)
                v.drain()
                v.tensor_copy(PREV[0:1, :], PINT[0:1, :])
                v.drain()

            v.wait_ge(s["key_ready"], 2)
            decide(1)
            code = v.alloc_register("v_code"); na = v.alloc_register("v_na"); nf = v.alloc_register("v_nf")
            v.wait_ge(s["decided"], 1)
            v.load(code, KINT[0:1, 0:1], bass_reorder=False)
            chosen = v.alloc_register("v_chosen")
            v.reg_mov(chosen, 1)
            v.reg_mov(na, 0); v.reg_mov(nf, 0)
            with active_steps(v, code) as c:
                with v.If((c & 1) > 0):
                    k = v.snap(na, min_val=0, max_val=NB)
                    v.wait_ge(s["att_w"], k * 64 + 64)
                    v.tensor_copy(W4B[0:64, 3, 0:C], W4R[0:64, 3, :]).then_inc(s["wo_diag"], 1)
                    v.wait_ge(s["att_proj"], k * 4 + 4)
                    v.tensor_copy(KEYS[:, :].rearrange("p (h t) -> p h t", h=2), PS[:, 2:4, 0:HT]).then_inc(s["keys_done"], 1)
                    for b in range(2, NIMG):
                        q = slice(32 * b, 32 * b + 32)
                        v.tensor_copy(QZ[q, b, :].rearrange("p (h t) -> p h t", h=2), PS[q, 4:6, 0:HT]).then_inc(s["qz_dve"], 1)
                    v.wait_ge(s["v_proj"], k + 1)
                    v.tensor_copy(VT[0:QT, 0:4, :], PS[0:QT, 6, 0:512].rearrange("p (j m) -> p j m", j=4))
                    v.tensor_copy(VT[0:QT, 4:7, :], PS[0:QT, 7, 0:384].rearrange("p (j m) -> p j m", j=3)).then_inc(s["v_done"], 1)

                    def less_max(b, j):
                        v.wait_ge(s["mrow_done"], k * 4 + (b + 1))
                        tile = SCR[0:QT, NQ * (b % 2) + j, :].rearrange("p (h t) -> p h t", h=2)
                        v.tensor_tensor(tile, tile, PS[0:QT, 4:6, 0:HT], ALU.add).then_inc(s["less_max"], 1)

                    for b in range(NIMG):
                        for j in range(1, NQ):
                            v.wait_ge(s["score_cp"], k * 28 + (NQ * b + j + 1))
                            if j == 1:
                                if b:
                                    v.wait_ge(s["top_tr"], k * 4 + b)
                                before = SCR[0:QT, NQ * (b % 2), :]
                            else:
                                v.wait_ge(s["top_step"], k * 24 + (6 * b + j - 1))
                                before = TOP[0:QT, :]
                            v.tensor_tensor(TOP[0:QT, :], before, SCR[0:QT, NQ * (b % 2) + j, :], ALU.max).then_inc(s["top_step"], 1)
                            if b:
                                less_max(b - 1, j - 1)
                        v.wait_ge(s["top_tr"], k * 4 + (b + 1))
                        v.tensor_reduce(SMX[0:QT, 0:4], PS[0:QT, 2, 0:4 * QT].rearrange("p (j m) -> p j m", j=4), AX.X, ALU.max)
                        v.tensor_reduce(SMX[0:QT, 4:NQ], PS[0:QT, 3, 0:3 * QT].rearrange("p (j m) -> p j m", j=3), AX.X,
                                        ALU.max).then_inc(s["smax_done"], 1)
                        if b:
                            less_max(b - 1, NQ - 1)
                    for j in range(NQ):
                        less_max(NIMG - 1, j)
                    v.wait_ge(s["att_den"], k + 1)
                    v.reciprocal(RSC[:, :], bank(4, QU)).then_inc(s["att_rs"], 1)
                    for h in range(2):
                        v.wait_ge(s["att_num"], k * 2 + (h + 1))
                        v.wait_ge(s["att_bc"], k * 2 + (h + 1))
                        v.tensor_tensor(half(H, h), half(RS, h), bank(2 + h), ALU.mult).then_inc(s["att_h"], 1)
                    v.reg_add(na, na, 1)
                with v.If((c & 2) > 0):
                    k = v.snap(nf, min_val=0, max_val=NB)
                    v.wait_ge(s["ffn_w"], k * 64 + 64)
                    for u in range(1, 8, 2):
                        v.wait_ge(s["ffn_h1"], k * 8 + (u + 1))
                        v.tensor_scalar(HIDT[:, u, :], bank(u % 4), B1S[:, :], 0.0, ALU.add, ALU.max).then_inc(s["hid_dve"], 1)
                    v.wait_ge(s["ffn_out"], k * 2 + 2)
                    v.tensor_scalar(half(H, 1), bank(5), B2S[:, :], None, ALU.add).then_inc(s["ffn_h"], 1)
                    v.reg_add(nf, nf, 1)
                n = v.snap(chosen, min_val=1, max_val=NB)
                decide(n + 1)
                v.reg_add(chosen, chosen, 1)
                v.load(code, KINT[0:1, 0:1], bass_reorder=False)

            v.tensor_tensor(X[:, :], X1[:, :], H[:, :], ALU.add).then_inc(s["x2_ready"], 1)
            v.wait_ge(s["x2_ready"], 1)
            norm(2, X, lambda h: half(XN, h))

            def quantise(src, dst, recip, low, high, tmp):
                ql(v.tensor_scalar(tmp, src, recip, low, ALU.mult, ALU.max))
                ql(v.tensor_scalar(tmp, tmp, high, MAGIC, ALU.min, ALU.add))
                return v.tensor_scalar(dst, grid(tmp) if len(dst.shape) == 3 else tmp, -MAGIC, None, ALU.add)

            v.wait_ge(s["pads"], 3)
            for h in range(2):
                v.wait_ge(s["ln_out"], 4 + h + 1)
                quantise(half(XN, h), rows(XQP, h, 1, 1), QS[:, 4:5], -128.0, 127.0, half(SD, h)).then_inc(s["q_xin"], 1)
            for h in range(2):
                v.wait_ge(s["cv_relu"], h + 1)
                quantise(half(SQ, h), rows(HQP, h, 1, 1), QS[:, 5:6], 0.0, 255.0, half(XC, h)).then_inc(s["cv_q"], 1)
            for h in range(2):
                v.wait_ge(s["cv_relu"], 2 + h + 1)
                ql(quantise(half(SQ, h), half(RS, h), QS[:, 6:7], 0.0, 255.0, half(SD, h)))
                v.scalar_tensor_tensor(half(X1, h), half(RS, h), par_("sc", 2), half(X, h), ALU.mult, ALU.add).then_inc(s["x3_ready"], 1)
            v.wait_ge(s["x3_ready"], 2)
            v.wait_ge(s["zeroed"], 6)
            norm(3, X1, lambda h: UPZ[:, 2 + h * HT:2 + (h + 1) * HT])
            v.wait_ge(s["ut_done"], 2)
            v.tensor_copy(UT[:, 4:8, :], PS[:, 5, 0:512].rearrange("p (i m) -> p i m", i=4)).then_inc(s["ut_ready"], 1)
            for u in range(1, 64, 2):
                v.wait_ge(s["u_done"], u + 1)
                if u >= 8:
                    v.wait_ge(s["mix_done"], u // 4 - 1)
                v.tensor_copy(UEV[:, u % 8, :], bank(u % 6)).then_inc(s["uev_dve"], 1)
            v.wait_ge(s["mix_done"], 16)
            x3 = X1[:, :].rearrange("p (t a) -> p t a", a=2)
            y = Y1[:, :].rearrange("p (t a) -> p t a", a=2)
            for a2 in range(2):
                v.tensor_tensor(y[:, :, a2], x3[:, :, a2], bank(6 + a2), ALU.add).then_inc(s["y_ready"], 1)

        @block.tensor
        def _(t):
            def mm(out_, lhsT, rhs, start=True, stop=True):
                return t.matmul(out_, lhsT, rhs, start=start, stop=stop, skip_group_check=True)

            def spread(h, to):
                for q in (2 * h, 2 * h + 1):
                    last = mm(PS[:, to + h, QU * (q % 2):QU * (q % 2) + QU], con_("spread", 512)[:, P * q:P * q + P], RSC[:, :])
                return last

            def norm(k, src):
                for h in range(2):
                    mm(bank(h), con_("bones"), half(src, h)).then_inc(s["ln_mean"], 1)
                for q in range(4):
                    t.wait_ge(s["ln_sq"], 2 * k + q // 2 + 1)
                    last = mm(PS[32 * q:32 * q + 32, 2, 0:QU], con_("vsel", C), quarter(SQ, q))
                last.then_inc(s["ln_var"], 1)
                t.wait_ge(s["ln_rs"], k + 1)
                for h in range(2):
                    spread(h, 0).then_inc(s["ln_bc"], 1)

            t.wait_ge(s["con_head"], 16)
            t.wait_ge(s["x_in"], 16)
            norm(0, X)
            t.wait_ge(s["wa1_in"], 32)
            for h in range(2):
                t.wait_ge(s["ln_out"], h + 1)
                mm(bank(4 + h), WS1[:, :], half(XN, h)).then_inc(s["c1_done"], 1)

            def group(c8s, slot):
                for h in range(2):
                    for cg in range(4):
                        last = mm(PS[32 * cg:32 * cg + 32, 6 + h, 0:HT], SEL[on_scalar(c8s[cg], cg)][:, c8s[cg], :],
                                  half(RING[:, 4 * slot + cg, :], h), start=False, stop=False)
                return last

            t.wait_ge(s["con_in"], 16)
            t.wait_ge(s["y1_ready"], 2)
            for h in range(2):
                mm(bank(6 + h), con_("corr"), half(Y1, h))
            for g in range(8):
                t.wait_ge(s["dve_unit"], DVE_BY[g + 1])
                t.wait_ge(s["act_unit"], ACT_BY[g + 1])
                last = group([g] * 4, g % RG)
                last.then_inc(s["ring_free"], 1)
            mm(PS[0:1, 5, 500:501], CON[:, 0:1], CON[:, 0:1]).then_inc(s["adder_done"], 1)
            t.wait_ge(s["ws2_in"], 16)
            t.wait_ge(s["h1_ready"], 2)
            for h in range(2):
                for tap in range(9):
                    if h and tap == 2:
                        t.wait_ge(s["wmx_part"], 2)
                        for i in range(2):
                            last = mm(PS[0:1, 0, 128 * i:128 * i + 128], WMX[:, i:i + 1], con_("ident"))
                        last.then_inc(s["wmx_rows"], 1)
                    if h and tap == 5:
                        t.wait_ge(s["wmx_row"], 1)
                        mm(PS[:, 1, 0:2], con_("ones", P, 1), WRW[0:1, :]).then_inc(s["wmx_bc"], 1)
                    last = mm(grid(bank(4 + h)), WS2[:, tap, :], rows(H1P, h, tap // 3, tap % 3), tap == 0, tap == 8)
                last.then_inc(s["c2_done"], 1)

            t.wait_ge(s["y2_ready"], 2)
            for h in range(2):
                mm(grid(bank(6 + h)), con_("zero"), rows(Y2P, h, 1, 1))
            with t.Fori(0, 3) as dh:
                for p, units in enumerate(PLAN):
                    t.wait_ge(s["dve_unit"], dh * DVE_ROW[GROUPS] + (DVE_BY[8] + DVE_ROW[p + 1]))
                    t.wait_ge(s["act_unit"], dh * ACT_ROW[GROUPS] + (ACT_BY[8] + ACT_ROW[p + 1]))
                    group([c8 for c8, _ in units], (8 + p) % RG).then_inc(s["ring_free"], 1)
            t.wait_ge(s["xs9_ready"], 1)
            for h in range(2):
                last = mm(bank(6 + h), con_("corr"), half(XS9, h), start=False, stop=False)
            last.then_inc(s["adder_done"], 1)
            t.wait_ge(s["h2_ready"], 2)
            for h in range(2):
                mm(bank(4 + h), con_("perm"), half(SQ, h)).then_inc(s["perm_done"], 1)
            t.wait_ge(s["x1_ready"], 2)
            norm(1, X1)
            t.wait_ge(s["ln_out"], 4)

            def token_row():
                mm(PS[0:1, 6, 0:32], H[:, 0:1], con_("ident", 32)).then_inc(s["row_done"], 1)

            token_row()
            t.wait_ge(s["decided"], 1)
            code = t.alloc_register("t_code"); na = t.alloc_register("t_na"); nf = t.alloc_register("t_nf")
            t.load(code, KINT[0:1, 0:1], bass_reorder=False)
            t.reg_mov(na, 0); t.reg_mov(nf, 0)
            chosen = t.alloc_register("t_chosen")
            t.reg_mov(chosen, 1)
            with active_steps(t, code) as c:
                with t.If((c & 1) > 0):
                    k = t.snap(na, min_val=0, max_val=NB)
                    t.wait_ge(s["zeroed"], 4)
                    t.wait_ge(s["att_diag"], k * 4 + 4)
                    for i, b0 in ((0, 4), (1, 2)):
                        for h in range(2):
                            mm(bank(b0 + h), W4B[:, i, :], half(H, h)).then_inc(s["att_proj"], 1)
                    for j in range(NQ):
                        last = mm(PS[0:QT, 6 + j // 4, P * (j % 4):P * (j % 4) + P], H[:, QT * j:QT * j + QT], W4B[:, 2, :])
                    last.then_inc(s["v_proj"], 1)
                    t.wait_ge(s["keys_done"], k + 1)

                    def scores(b, j):
                        u, pr = NQ * b + j, score_banks(b, j)
                        if j == 0:
                            t.wait_ge(s["qz_act" if b < 2 else "qz_dve"], k * 2 + (b % 2 + 1))
                        if b and j < 2:
                            t.wait_ge(s["score_cp"], k * 28 + (u if j else u - 1))
                        elif j > 2 or (b == 0 and j == 2):
                            t.wait_ge(s["score_cp"], k * 28 + (u - 1))
                        for h in range(2):
                            last = mm(PS[0:QT, pr + h, 0:HT], KEYS[:, QT * j:QT * j + QT], half(QZ[:, b, :], h))
                        last.then_inc(s["st_done"], 1)

                    def maxima_transposed(b):
                        t.wait_ge(s["top_step"], k * 24 + (6 * b + 6))
                        for j in range(NQ):
                            last = mm(PS[0:QT, 2 + j // 4, QT * (j % 4):QT * (j % 4) + QT], TOP[0:QT, QT * j:QT * j + QT],
                                      con_("ident", QT, QT))
                        last.then_inc(s["top_tr"], 1)

                    def maxima_spread(b):
                        t.wait_ge(s["smax_done"], k * 4 + (b + 1))
                        if b:
                            t.wait_ge(s["less_max"], k * 28 + NQ * b)
                        else:
                            t.wait_ge(s["qz_act"], k * 2 + 2)
                            t.wait_ge(s["qz_dve"], k * 2 + 2)
                        for lo in (0, 112, 224, 336, 392, 448, 560, 672):
                            j, h = lo // QT, lo // HT
                            n = min(QT * (j + 1), HT if lo < HT else T) - lo
                            last = mm(PS[0:QT, 4 + h, lo - HT * h:lo - HT * h + n], SMX[0:QT, j:j + 1].to_broadcast([QT, QT]),
                                      con_("nident", QT, QT)[:, lo - QT * j:lo - QT * j + n])
                        last.then_inc(s["mrow_done"], 1)

                    def weigh(b, pair):
                        t.wait_ge(s["exp_done"], k * 28 + (NQ * b + min(2 * pair + 2, NQ)))
                        if pair == 0:
                            if b:
                                t.wait_ge(s["ae_done"], k * 4 + b)
                            else:
                                t.wait_ge(s["v_done"], k + 1)
                        for h in range(2):
                            for w in range(2):
                                for e in range(2):
                                    j = 2 * pair + e
                                    if j < NQ:
                                        q = 64 * w + 32 * e
                                        last = mm(PS[q:q + 32, 6 + h, 0:HT],
                                                  con_("ones", C, QT) if w else VT[0:QT, j, 32 * b:32 * b + 32],
                                                  half(SCR[0:QT, NQ * (b % 2) + j, :], h), pair == 0, j + 2 >= NQ)
                        last.then_inc(s["pv_done"], 1)

                    for b in range(NIMG):
                        for j in range(NQ):
                            scores(b, j)
                            if b >= 1 and j == 0:
                                if b >= 2:
                                    weigh(b - 2, 2)
                                maxima_transposed(b - 1)
                            if b >= 1 and j == 1:
                                if b >= 2:
                                    weigh(b - 2, 3)
                                maxima_spread(b - 1)
                            if b >= 1 and j in (5, 6):
                                weigh(b - 1, j - 5)
                    maxima_transposed(NIMG - 1)
                    weigh(NIMG - 2, 2)
                    maxima_spread(NIMG - 1)
                    weigh(NIMG - 2, 3)
                    for pair in range(4):
                        weigh(NIMG - 1, pair)
                    t.wait_ge(s["wo_diag"], k + 1)
                    t.wait_ge(s["ae_done"], k * 4 + 4)
                    for b in range(NIMG):
                        for q in range(4):
                            last = mm(PS[32 * q:32 * q + 32, 4, 0:QU], con_("dsel")[:, 32 * b:32 * b + 32], quarter(AE[b], q),
                                      b == 0, b == 3)
                    last.then_inc(s["att_den"], 1)
                    for h in range(2):
                        for b in range(NIMG):
                            last = mm(PS[32 * b:32 * b + 32, h, 0:HT], W4B[:, 3, 0:C], half(AE[b], h))
                        last.then_inc(s["att_wo"], 1)
                    t.wait_ge(s["att_rs"], k + 1)
                    for h in range(2):
                        spread(h, 2).then_inc(s["att_bc"], 1)
                    t.wait_ge(s["att_h"], k * 2 + 2)
                    t.reg_add(na, na, 1)
                with t.If((c & 2) > 0):
                    k = t.snap(nf, min_val=0, max_val=NB)
                    t.wait_ge(s["ffn_diag"], k * 4 + 4)
                    for h in range(2):
                        for b in range(NIMG):
                            u = 4 * h + b
                            if u >= 4:
                                t.wait_ge(s["hid_act" if u % 2 == 0 else "hid_dve"], k * 4 + (u - 4) // 2 + 1)
                            mm(bank(u % 4), W1B[:, b, :], half(H, h)).then_inc(s["ffn_h1"], 1)
                    for h in range(2):
                        t.wait_ge(s["hid_act"], k * 4 + 2 * h + 2)
                        t.wait_ge(s["hid_dve"], k * 4 + 2 * h + 2)
                        for b in range(NIMG):
                            last = mm(PS[32 * b:32 * b + 32, 4 + h, 0:HT], W2S[:, :], HIDT[:, 4 * h + b, :])
                        last.then_inc(s["ffn_out"], 1)
                    t.wait_ge(s["ffn_h"], k * 2 + 2)
                    t.reg_add(nf, nf, 1)
                token_row()
                n = t.snap(chosen, min_val=1, max_val=NB)
                t.wait_ge(s["decided"], n + 1)
                t.reg_add(chosen, chosen, 1)
                t.load(code, KINT[0:1, 0:1], bass_reorder=False)

            t.wait_ge(s["x2_ready"], 1)
            norm(2, X)
            t.wait_ge(s["cq_done"], 2)
            t.wait_ge(s["q_xin"], 2)
            for i, (w, src) in enumerate(((CQ1, XQP), (CQ2, HQP))):
                if i:
                    t.wait_ge(s["cv_q"], 2)
                for h in range(2):
                    for tap in range(9):
                        last = mm(grid(bank(4 + h)), w[:, P * tap:P * tap + P], rows(src, h, tap // 3, tap % 3), tap == 0, tap == 8)
                    last.then_inc(s["cc_done"], 1)
            t.wait_ge(s["x3_ready"], 2)
            norm(3, X1)
            t.wait_ge(s["ln_out"], 8)

            t.wait_ge(s["urv_ready"], 2)
            for c in range(2):
                for i in range(4):
                    a0 = 1024 - 255 - c - 256 * i
                    last = mm(PS[:, 4 + c, P * i:P * i + P], URV[:, a0:a0 + 255:2], con_("ident"))
                last.then_inc(s["ut_done"], 1)
            t.wait_ge(s["d_ready"], 4)
            for a2 in range(2):
                for n, (lo, hi, sgm) in enumerate(SEGS):
                    for lag in range(3):
                        c0 = 2 + a2 - lag + 2 * lo
                        last = mm(PS[:, 6 + a2, lo:hi], MUB[:, 3 * sgm + lag, :], UPZ[:, c0:c0 + 2 * (hi - lo) - 1:2],
                                  start=(n == 0 and lag == 0), stop=False)
            last.then_inc(s["ar_done"], 1)
            t.wait_ge(s["ut_ready"], 2)
            t.wait_ge(s["strip_in"], 32)

            def filtered(u):
                grp, b = u // 4, u % 4
                g, a2, odd = grp // 4, (grp // 2) % 2, grp % 2
                c = a2 ^ odd
                if u >= 6:
                    t.wait_ge(s["uev_act" if u % 2 == 0 else "uev_dve"], (u - 6) // 2 + 1)
                for i in range(4):
                    n = NPH - P * i
                    for kk in range(4):
                        k = 4 * g + kk
                        if not odd:
                            m = HE[:, k, 0:n]
                        else:
                            m = HO[:, k, 1:1 + n] if a2 else HO[:, k, 0:n]
                        last = mm(PS[32 * kk:32 * kk + 32, u % 6, P * i:NPH], UT[:, 4 * c + i, 32 * b:32 * b + 32], m,
                                  i == 0, i == 3)
                last.then_inc(s["u_done"], 1)

            def mixed(grp):
                g, a2, odd = grp // 4, (grp // 2) % 2, grp % 2
                t.wait_ge(s["uev_act"], 2 * grp + 2)
                t.wait_ge(s["uev_dve"], 2 * grp + 2)
                for lo, hi, sgm in SEGS:
                    for b in range(4):
                        last = mm(PS[32 * b:32 * b + 32, 6 + a2, lo:hi], ASEG[:, odd, sgm, 32 * g:32 * g + 32],
                                  UEV[:, (4 * grp + b) % 8, lo:hi], False, False)
                last.then_inc(s["mix_done"], 1)

            for grp in range(16):
                for b in range(4):
                    filtered(4 * grp + b)
                if grp:
                    mixed(grp - 1)
            mixed(15)


def _constants():
    import numpy as np

    con = np.zeros((P, CC["n"]), np.float32)
    p = np.arange(P)
    con[:, CC["ident"]:CC["ident"] + P] = np.eye(P)
    con[:, CC["nident"]:CC["nident"] + P] = -np.eye(P)
    con[:, CC["bones"]:CC["bones"] + P] = (p[:, None] // 32 == p[None, :] // 32) / 32.0
    for c8 in range(8):
        for b in range(4):
            con[32 * b:32 * b + 32, CC["sel1"] + 32 * c8 + 8 * b + c8] = 1.0
            con[32 * b:32 * b + 32, CC["sel2"] + 32 * c8 + 8 * b + c8] = 2.0
    for r in range(P):
        cg, b, c8 = r // 32, (r // 8) % 4, r % 8
        if not on_scalar(c8, cg):
            con[32 * b:32 * b + 32, CC["corr"] + r] = -1.0
            con[r, CC["dmask"]] = 1.0
        con[r, CC["perm"] + 32 * b + 8 * cg + c8] = 1.0
    con[:, CC["ones"]:CC["ones"] + P] = 1.0
    for b in range(NIMG):
        con[[64, 96], CC["dsel"] + 40 * b:CC["dsel"] + 40 * b + 8] = 1.0
        con[32 * b:32 * b + 32, CC["vsel"] + 8 * b:CC["vsel"] + 8 * b + 8] = 1.0 / 32.0
        for q in range(4):
            a = CC["spread"] + P * q + 32 * b
            con[32 * q + 8 * b, a:a + 32] = 1.0
    con[:, CC["eps5"]] = 1e-5
    con[:, CC["eps6"]] = 1e-6
    con[:, CC["iota"]:CC["iota"] + 4] = np.arange(4)
    con[:, CC["blk4"]:CC["blk4"] + NB] = 4.0 * (NB - np.arange(NB))
    return con


def _diag(w):
    import numpy as np

    z = np.zeros((NIMG, C, w.shape[1], NIMG, C), w.dtype)
    for b in range(NIMG):
        z[b, :, :, b, :] = w
    return z.reshape(P, w.shape[1], P)


def _layout(i):
    import numpy as np

    co_of_r = np.array([8 * (r // 32) + r % 8 for r in range(P)])
    img_of_r = np.array([(r // 8) % 4 for r in range(P)])
    co_of_bc = np.tile(np.arange(C), NIMG)
    par = np.zeros((P, PC["n"]), np.float32)
    for k in range(2):
        for col, name in (("g", "gamma"), ("be", "beta"), ("mu", "mean"), ("va", "var")):
            par[:, PC[col] + k] = i[f"L0_conv_bn{k + 1}_{name}"][co_of_r]
        par[:, PC["cb"] + k] = i[f"L1_conv_b{k + 1}"][co_of_bc]
    for k, name in enumerate(("s_in", "s_a1", "s_a2")):
        par[:, PC["sc"] + k] = i[f"L1_conv_{name}"][0]
    par[:, PC["lw"]:PC["lw"] + 4] = i["L1_ffn_log_weights"]
    par[:, PC["gu"]:PC["gu"] + 4] = i["L1_ffn_gumbel"]
    par[:, PC["sg"]:PC["sg"] + 4] = np.repeat(i["L1_ffn_sigma"].reshape(4, 4).T, C, axis=0)
    ws2 = i["L0_conv_w_shift2"].reshape(C, C, 9).transpose(1, 2, 0)
    ws2r = np.zeros((P, 9, P), np.float32)
    for r in range(P):
        ws2r[r, :, 32 * img_of_r[r]:32 * img_of_r[r] + 32] = ws2[co_of_r[r]]
    wa2 = i["L0_conv_w_add2"].reshape(C, C, 9)
    phi = i["L1_ffn_phi"][:T]
    phe = np.zeros((NK, LE), np.float32)
    pho = np.zeros((NK, LO), np.float32)
    phe[:, 127:] = phi[0::2].T
    pho[:, 128:] = phi[1::2].T

    def mst(m):
        return m.reshape(4, 4, 4, C, C).transpose(2, 3, 0, 1, 4).reshape(P, 4, P)

    def conv(w):
        return _diag(w.reshape(C, C, 9).transpose(1, 2, 0)).reshape(P, 9 * P)

    return {
        "x": i["x"].reshape(P, T), "par": par, "con": _constants(),
        "ws1": _diag(i["L0_conv_w_shift1"].reshape(C, 1, C).transpose(2, 1, 0)).reshape(P, P),
        "wa1c": np.tile(i["L0_conv_w_add1"].reshape(C, C).T, (NIMG, 1)),
        "wa1r": i["L0_conv_w_add1"].reshape(C, C)[co_of_r],
        "ws2": ws2r,
        "wa2c": np.tile(wa2.transpose(1, 2, 0).reshape(C, 9 * C), (NIMG, 1)),
        "wa2r": wa2.reshape(C, 9 * C)[co_of_r],
        "amt": i["L0_ffn_attn_mask"].T.reshape(1, -1),
        "fmt": i["L0_ffn_ffn_mask"].T.reshape(1, -1),
        "fw1": i["L0_ffn_ffn_w1"].reshape(NB * NOPS, C, HID), "fb1": i["L0_ffn_ffn_b1"].reshape(NB * NOPS, HID),
        "fw2": i["L0_ffn_ffn_w2"].reshape(NB * NOPS, HID, C), "fb2": i["L0_ffn_ffn_b2"].reshape(NB * NOPS, C),
        "wq": i["L0_ffn_wq"].reshape(NB * NOPS, C, C), "wk": i["L0_ffn_wk"].reshape(NB * NOPS, C, C),
        "wv": i["L0_ffn_wv"].reshape(NB * NOPS, C, C), "wo": i["L0_ffn_wo"].reshape(NB * NOPS, C, C),
        "cw1": conv(i["L1_conv_w1"]), "cw2": conv(i["L1_conv_w2"]), "phe": phe, "pho": pho,
        "mpp": mst(i["L1_ffn_M_phi_plus"]), "mpm": mst(i["L1_ffn_M_phi_minus"]),
        "mu": i["L1_ffn_M_u"].transpose(2, 0, 1, 3).reshape(C, 4, 96),
    }


def kernel(**inputs):
    import numpy as np
    import concourse.bacc as bacc
    from concourse.bass_utils import run_bass_kernel_spmd

    arrays = {k: np.ascontiguousarray(v) for k, v in _layout({k: np.asarray(v) for k, v in inputs.items()}).items()}
    nc = bacc.Bacc("TRN2", target_bir_lowering=False, num_devices=1)
    args = [nc.dram_tensor(f"in_{n}", a.shape, mybir.dt.from_np(a.dtype), kind="ExternalInput").ap() for n, a in arrays.items()]
    out = nc.dram_tensor("out_y", (P, T), F32, kind="ExternalOutput").ap()
    build(nc, *args, out)
    r = run_bass_kernel_spmd(nc, [{f"in_{n}": a for n, a in arrays.items()}], core_ids=[0])
    return r.results[0]["out_y"].reshape(NIMG, C, SIDE, SIDE)
```

```python
from contextlib import ExitStack, contextmanager

import concourse.bass as bass
from concourse import mybir

F32 = mybir.dt.float32
BF16 = mybir.dt.bfloat16
I32 = mybir.dt.int32
U32 = mybir.dt.uint32
U8 = mybir.dt.uint8
ALU = mybir.AluOpType
ACT = mybir.ActivationFunctionType
AX = mybir.AxisListType
ds = bass.ds

P = 128
NIMG, C, SIDE = 4, 32, 28
T = SIDE * SIDE
QU = T // 4
HT = T // 2
HROWS = SIDE // 2
PS_ = SIDE + 2
PADF = 904
NB, NOPS, HID = 33, 19, 128
STEPS = (3, 4, 3)
WARM = dict(inputs=4, means=1, deviations=4, choice=8, weights=8, exponentials=5, sums=2)
OPW = 1024
QT, NQ = 112, 7
NK = 16
NPH = T // 2
LE, LO = NPH + 127, NPH + 128
MAGIC = 12582912.0
SCALE = float(C) ** -0.5
SEGS = [(0, 49, 3), (49, 98, 2), (98, 196, 1), (196, 392, 0)]

PC = dict(g=0, be=2, mu=4, va=6, cb=8, sc=10, lw=13, gu=17, sg=21, n=25)
_c, CC = 0, {}
for _n, _w in (("bones", 128), ("vsel", 32), ("spread", 512), ("eps5", 1), ("eps6", 1), ("head", 0), ("ident", 128), ("nident", 128), ("sel1", 256), ("sel2", 256), ("corr", 128),
               ("perm", 128), ("zero", 128), ("ones", 128), ("dsel", 128), ("dmask", 1),
               ("iota", 4), ("blk4", NB), ("opw", NOPS)):
    CC[_n] = _c
    _c += _w
CC["n"] = _c


def on_scalar(c8, cg):
    return (c8 + 2 * cg) % 8 in (0, 3, 6) or (c8, cg) == (5, 0)


RG = 3
DVE_BY = [0]
ACT_BY = [0]
for _c8 in range(8):
    _a = sum(on_scalar(_c8, _g) for _g in range(4))
    ACT_BY.append(ACT_BY[-1] + _a)
    DVE_BY.append(DVE_BY[-1] + 4 - _a)
KINDS = ((0, 1, 1, 0, 0, 0, 2), (0, 1, 1, 2, 1, 0, 0), (1, 0, 1, 0, 0, 2, 1), (2, 0, 0, 1, 1, 1, 0))


def _row_plan():
    units = []
    for cg in range(4):
        on_act = [c8 for c8 in range(8) if on_scalar(c8, cg)]
        on_dve = [c8 for c8 in range(8) if not on_scalar(c8, cg)]
        acts = [(c8, (dw,)) for dw in range(3) for c8 in on_act]
        pairs = [(c8, (0, 1)) for c8 in on_dve[:3]]
        ones = [(c8, (2,)) for c8 in on_dve[:3]] + [(c8, (dw,)) for dw in range(3) for c8 in on_dve[3:]]
        units.append([(acts, ones, pairs)[KINDS[cg][p % 7]].pop(0) for p in range(21)])
    return [[units[cg][p] for cg in range(4)] for p in range(21)]


PLAN = _row_plan()
GROUPS = len(PLAN)
assert GROUPS % RG == 0
DVE_ROW = [0]
ACT_ROW = [0]
for _units in PLAN:
    _a = sum(on_scalar(_u[0], _g) for _g, _u in enumerate(_units))
    ACT_ROW.append(ACT_ROW[-1] + _a)
    DVE_ROW.append(DVE_ROW[-1] + 4 - _a)
PAIRS = sum(len(_u[1]) == 2 for _units in PLAN for _u in _units)


@contextmanager
def active_steps(e, code):
    assert STEPS[0] * STEPS[1] * STEPS[2] >= NB
    with e.Fori(0, STEPS[0]):
        with e.If(e.snap(code, min_val=0, max_val=4 * NB + 7) > 0):
            with e.Fori(0, STEPS[1]):
                with e.If(e.snap(code, min_val=0, max_val=4 * NB + 7) > 0):
                    with e.Fori(0, STEPS[2]):
                        c = e.snap(code, min_val=0, max_val=4 * NB + 7)
                        with e.If(c > 0):
                            yield c
                        e.nop()
                e.nop()
        e.nop()


def build(nc, x, par, con, ws1, wa1c, wa1r, ws2, wa2c, wa2r, amt, fmt, fwa, fwb, aw,
          cw1, cw2, phe, pho, mpp, mpm, mu, out):
    with ExitStack() as ctx:
        def sb(name, shape, dt=F32):
            return ctx.enter_context(nc.sbuf_tensor(name, shape, dt))

        def sem(name):
            return ctx.enter_context(nc.semaphore(name))

        PS = ctx.enter_context(nc.psum_tensor("PS", [P, 8, 512], F32))

        X = sb("X", [P, T]); XN = sb("XN", [P, T]); XC = sb("XC", [P, T]); SQ = sb("SQ", [P, T])
        SD = sb("SD", [P, T]); RS = sb("RS", [P, T]); SDC = sb("SDC", [P, QU]); RSC = sb("RSC", [P, QU]); Y1 = sb("Y1", [P, T])
        H1P = sb("H1P", [P, PADF]); Y2P = sb("Y2P", [P, PADF])
        X1 = sb("X1", [P, T]); HSUM = sb("H", [P, PS_ * SIDE]); H = HSUM[:, 0:T]
        arena = sb("arena", [P, 2 * NQ * T])
        RING = arena[:, 0:4 * RG * T].rearrange("p (n t) -> p n t", n=4 * RG)
        SCR = arena[:, :].rearrange("p (n t) -> p n t", n=2 * NQ)
        HIDT = arena[:, 0:4 * T].rearrange("p (n t) -> p n t", n=8)
        UEV = arena[:, 0:4 * T].rearrange("p (n t) -> p n t", n=8)
        HE = sb("HE", [P, NK, NPH]); HO = sb("HO", [P, NK, NPH + 1])
        QZ = sb("QZ", [P, 4, T])
        PAR = sb("PAR", [P, PC["n"]]); CON = sb("CON", [P, CC["n"]])
        WS1 = sb("WS1", [P, P]); WA1 = sb("WA1", [P, C]); WA1R = sb("WA1R", [P, C])
        WS2 = sb("WS2", [P, 9, P]); WA2 = sb("WA2", [P, 9 * C]); WA2R = sb("WA2R", [P, 9 * C])
        BN = sb("BN", [P, 24])
        AMT = sb("AMT", [P, NOPS * NB], U8); FMT = sb("FMT", [P, NOPS * NB], U8)
        AMF = XC[:, 0:NOPS * NB]; KEYT = sb("KEYT", [P, NOPS * NB])
        LOOK = sb("LOOK", [P, NOPS * NB]); NEXT = sb("NEXT", [P, NOPS]); CAND = sb("CAND", [P, NOPS]); MX8 = sb("MX8", [P, 8])
        KMAX = sb("KMAX", [P, 1]); PREV = sb("PREV", [P, 1])
        KINT = sb("KINT", [P, 1], I32); PINT = sb("PINT", [P, 1], I32)
        W1R = sb("W1R", [P, HID + 1]); W1B = sb("W1B", [P, 4, HID]); W2S = sb("W2S", [P, C + 1])
        B1S = W2S[:, C:C + 1]; B2S = W1R[:, HID:HID + 1]
        W4R = sb("W4R", [P, 4, C]); W4B = sb("W4B", [P, 4, P])
        VT = sb("VT", [P, NQ, P]); SMX = sb("SMX", [P, NQ])
        KEYS = Y1; TOP = SD
        AE = [X, XN, XC, SQ]
        CW1 = sb("CW1", [P, 9 * P]); CW2 = sb("CW2", [P, 9 * P])
        CQ1 = sb("CQ1", [P, 9 * P], BF16); CQ2 = sb("CQ2", [P, 9 * P], BF16)
        XQP = H1P[:, 0:PADF // 2].bitcast(BF16); HQP = H1P[:, PADF // 2:PADF].bitcast(BF16)
        WMX = sb("WMX", [P, 2]); WRW = sb("WRW", [P, 2]); QS = sb("QS", [P, 24])
        MPP = sb("MPP", [P, 4, P]); MPM = sb("MPM", [P, 4, P]); MSC = sb("MSC", [P, 4, P])
        ASEG = sb("ASEG", [P, 2, 4, P]); MUR = sb("MUR", [P, 4, 96]); MUS = sb("MUS", [P, 4, 96])
        MUB = sb("MUB", [P, 12, P]); WSM = sb("WSM", [P, 48]); WIX = sb("WIX", [P, 8], U32)
        UT = WS2[:, 0:8, :]
        XS9 = RS
        UPZ = CW1[:, 0:2 + 1024]

        URV = CW2[:, 0:1024]

        def con_(name, w=None, rows=P):
            a = CC[name]
            return CON[0:rows, a:a + (w or P)]

        def par_(name, i=0, w=1):
            return PAR[:, PC[name] + i:PC[name] + i + w]

        def half(ap, h):
            return ap[:, h * HT:(h + 1) * HT]

        def quarter(ap, q):
            return ap[:, q * QU:(q + 1) * QU]

        def rows(ap, h, dh=0, dw=0):
            v = ap[:, 0:PS_ * PS_].rearrange("p (a b) -> p a b", a=PS_)
            return v[:, h * HROWS + dh:h * HROWS + dh + HROWS, dw:dw + SIDE]

        def bank(b, w=HT, rows_=slice(0, P)):
            return PS[rows_, b, 0:w]

        def score_banks(b, j):
            return 0 if b and j == 0 else 2 * ((j + 1) % 2)

        def window(dh, dw):
            return Y2P[:, ds(dh * PS_ + dw, SIDE * PS_)].rearrange("p (a b) -> p a b", b=PS_)[:, :, 0:SIDE]

        def grid(ap):
            return ap.rearrange("p (a b) -> p a b", b=SIDE)

        SEL = {True: con_("sel1", 256).rearrange("p (c m) -> p c m", c=8),
               False: con_("sel2", 256).rearrange("p (c m) -> p c m", c=8)}

        s = {n: sem(n) for n in (
            "sp_woke idle_src x_low_in x_in par_in con_in wa1_in w_a_in sum_in mask_in ws2_in cw_in strip_in mst_in "
            "ln_mean ln_cent ln_sq ln_var ln_sd ln_rs ln_bc ln_out con_head "
            "bn_sd bn_ready bn_chain pads zeroed c1_done y1_ready ring_free dve_unit pair_part act_unit adder_done "
            "h1_ready c2_done y2_ready xs9_ready xs9_chain h2_ready perm_done x1_tmp x1_ready "
            "key_chain key_ready row_done decided "
            "ffn_wa ffn_wb att_w ffn_diag ffn_h1 hid_act hid_dve ffn_out ffn_h att_diag wo_diag att_proj keys_done qz_act qz_dve v_proj v_done "
            "st_done score_cp top_step top_tr smax_done mrow_done less_max exp_done pv_done ae_done att_den att_rs att_bc att_wo att_num att_h "
            "wmx_part wmx_rows wmx_row wmx_bc q_sc q_chain cq_chain cq_done x2_ready q_xin cc_done cv_relu cv_q x3_ready "
            "wexp w_soft w_chain sg_ready d_chain d_ready ar_done ut_done ut_ready urv_ready u_done uev_act uev_dve mix_done y_ready stored"
        ).split()}
        ctx.enter_context(nc.allow_non_contiguous_dma("weights' rows are short"))
        block = ctx.enter_context(nc.Block())

        @block.sync
        def _(sp):
            sp.dma_start(half(X, 0), half(x, 0)).then_inc(s["x_in"], 16)
            sp.dma_start(PAR[:, :], par).then_inc(s["par_in"], 16)
            sp.dma_start(WS1[:, :], ws1).then_inc(s["wa1_in"], 16)
            sp.dma_start(WA1[:, :], wa1c).then_inc(s["wa1_in"], 16)
            sp.dma_start(WA1R[:, :], wa1r).then_inc(s["sum_in"], 16)
            sp.dma_start(WA2R[:, :], wa2r).then_inc(s["sum_in"], 16)
            sp.dma_start(WS2[:, :, :], ws2).then_inc(s["ws2_in"], 16)
            sp.dma_start(WA2[:, :], wa2c).then_inc(s["w_a_in"], 16)
            sp.dma_start(AMT[0:1, :], amt).then_inc(s["mask_in"], 16)
            sp.dma_start(FMT[0:1, :], fmt).then_inc(s["mask_in"], 16)
            sp.dma_start(MPP[:, :, :], mpp).then_inc(s["mst_in"], 16)
            sp.dma_start(MPM[:, :, :], mpm).then_inc(s["mst_in"], 16)
            for b in range(NIMG):
                sp.dma_start(MUR[32 * b:32 * b + 32, :, :], mu).then_inc(s["mst_in"], 16)
            sp.dma_start(CW1[:, :], cw1).then_inc(s["cw_in"], 16)
            sp.dma_start(CW2[:, :], cw2).then_inc(s["cw_in"], 16)
            sp.dma_start(HE[:, :, :], bass.AP(phe.tensor, 0, [[1, P], [LE, NK], [1, NPH]])).then_inc(s["strip_in"], 16)
            sp.dma_start(HO[:, :, :], bass.AP(pho.tensor, 0, [[1, P], [LO, NK], [1, NPH + 1]])).then_inc(s["strip_in"], 16)

            sp.wait_ge(s["decided"], 1)
            code = sp.alloc_register("sp_code"); which = sp.alloc_register("sp_which")
            raw = sp.alloc_register("sp_raw")
            sp.load(raw, KINT[0:1, 0:1], bass_reorder=False)
            sp.reg_mov(code, sp.snap(raw) & (OPW - 1))
            chosen = sp.alloc_register("sp_chosen")
            sp.reg_mov(chosen, 1)
            with active_steps(sp, code) as c:
                op = NOPS - (sp.snap(raw, min_val=0, max_val=(NOPS + 1) * OPW - 1) >> OPW.bit_length() - 1)
                sp.reg_mov(which, (NB - (c >> 2)) * NOPS + op)
                w = sp.snap(which, min_val=0, max_val=NB * NOPS - 1)
                with sp.If((c & 1) > 0):
                    sp.dma_start(W4R[:, :, :].rearrange("p i m -> p (i m)"),
                                 aw[ds(w, 1), :, :].broadcast_to([NIMG, C, 4 * C])).then_inc(s["att_w"], 16)
                    sp.nop()
                with sp.If((c & 2) > 0):
                    sp.dma_start(W1R[:, :],
                                 fwa[ds(w, 1), :, :].broadcast_to([NIMG, C, HID + 1])).then_inc(s["ffn_wa"], 16)
                    sp.dma_start(W2S[:, :], fwb[ds(w, 1), :, :].rearrange("a h d -> (a h) d")).then_inc(s["ffn_wb"], 16)
                    sp.nop()
                n = sp.snap(chosen, min_val=1, max_val=NB)
                sp.wait_ge(s["decided"], n + 1)
                sp.sem_inc(s["sp_woke"], 1)
                sp.reg_add(chosen, chosen, 1)
                sp.load(raw, KINT[0:1, 0:1], bass_reorder=False)
                sp.reg_mov(code, sp.snap(raw) & (OPW - 1))

            sp.wait_ge(s["y_ready"], 2)
            sp.dma_start(out, Y1[:, :]).then_inc(s["stored"], 16)
            sp.wait_ge(s["stored"], 16)

        @block.gpsimd
        def _(g):
            hd = CC["head"]
            g.dma_start(CON[:, 0:hd], con[:, 0:hd]).then_inc(s["con_head"], 16)
            g.dma_start(CON[:, hd:], con[:, hd:]).then_inc(s["con_in"], 16)
            g.memset(H1P[:, :], 0.0).then_inc(s["pads"], 1)
            g.memset(Y2P[:, :], 0.0).then_inc(s["pads"], 1)
            g.memset(W1B[:, :, :], 0.0).then_inc(s["zeroed"], 1)
            g.memset(W4B[:, :, :], 0.0).then_inc(s["zeroed"], 1)
            g.memset(MUB[:, :, :], 0.0).then_inc(s["zeroed"], 1)
            g.memset(QZ[:, :, :], 0.0).then_inc(s["zeroed"], 1)
            g.wait_ge(s["zeroed"], 4)

            chain = 0

            def link(ins):
                nonlocal chain
                chain += 1
                ins.then_inc(s["d_chain"], 1)
                g.wait_ge(s["d_chain"], chain)

            g.wait_ge(s["mst_in"], 16 * 6)
            g.wait_ge(s["sg_ready"], 2)
            g.wait_ge(s["w_soft"], 1)
            sg = WSM[:, 40:44].unsqueeze(2).to_broadcast([P, 4, C])
            for par_i, op in enumerate((ALU.add, ALU.subtract)):
                link(g.tensor_tensor(MSC[:, :, :], MPP[:, :, :], MPM[:, :, :], op))
                for i in range(4):
                    v = MSC[:, i, :].rearrange("p (g e) -> p g e", g=4)
                    link(g.tensor_tensor(v, v, sg, ALU.mult))
                    link(g.tensor_scalar(ASEG[:, par_i, i, :], MSC[:, i, :], WSM[:, 24 + i:25 + i], None, ALU.mult))
                    if i:
                        link(g.tensor_tensor(ASEG[:, par_i, i, :], ASEG[:, par_i, i, :], ASEG[:, par_i, i - 1, :], ALU.add))
            for i in range(4):
                link(g.tensor_scalar(MUS[:, i, :], MUR[:, i, :], WSM[:, 24 + i:25 + i], None, ALU.mult))
                if i:
                    link(g.tensor_tensor(MUS[:, i, :], MUS[:, i, :], MUS[:, i - 1, :], ALU.add))
            for b in range(NIMG):
                q = slice(32 * b, 32 * b + 32)
                g.tensor_copy(MUB[q, :, q], MUS[q, :, :].rearrange("p i (l e) -> p (i l) e", e=C)).then_inc(s["d_ready"], 1)

            g.wait_ge(s["d_ready"], 4)

            g.wait_ge(s["q_sc"], 1)
            g.wait_ge(s["cw_in"], 32)
            cq = 0

            def qlink(ins):
                nonlocal cq
                cq += 1
                ins.then_inc(s["cq_chain"], 1)
                g.wait_ge(s["cq_chain"], cq)

            for i, (src, dst) in enumerate(((CW1, CQ1), (CW2, CQ2))):
                qlink(g.tensor_scalar(src[:, :], src[:, :], QS[:, 2 + i:3 + i], -128.0, ALU.mult, ALU.max))
                qlink(g.tensor_scalar(src[:, :], src[:, :], 127.0, MAGIC, ALU.min, ALU.add))
                g.tensor_scalar(dst[:, :], src[:, :], -MAGIC, None, ALU.add).then_inc(s["cq_done"], 1)

            g.wait_ge(s["cq_done"], 2)
            g.memset(UPZ, 0.0).then_inc(s["zeroed"], 1)
            g.memset(URV, 0.0).then_inc(s["zeroed"], 1)

            g.wait_ge(s["y2_ready"], 2)
            g.memset(H1P[:, :], 0.0).then_inc(s["pads"], 1)
            y2 = Y2P[:, 0:PS_ * PS_].rearrange("p (a b) -> p a b", a=PS_)
            hs = HSUM[:, :].rearrange("p (a b) -> p a b", a=PS_)
            g.tensor_tensor(hs, y2[:, :, 0:SIDE], y2[:, :, 1:1 + SIDE], ALU.add).then_inc(s["xs9_chain"], 1)
            g.wait_ge(s["xs9_chain"], 1)
            g.tensor_tensor(hs, hs, y2[:, :, 2:2 + SIDE], ALU.add).then_inc(s["xs9_chain"], 1)
            g.wait_ge(s["xs9_chain"], 2)
            xs = grid(XS9[:, :])
            g.tensor_tensor(xs, hs[:, 0:SIDE, :], hs[:, 1:1 + SIDE, :], ALU.add).then_inc(s["xs9_chain"], 1)
            g.wait_ge(s["xs9_chain"], 3)
            g.tensor_tensor(xs, xs, hs[:, 2:2 + SIDE, :], ALU.add).then_inc(s["xs9_ready"], 1)

        @block.scalar
        def _(a):
            def norm(k, eps):
                for h in range(2):
                    a.wait_ge(s["ln_cent"], 2 * k + h + 1)
                    a.activation(half(SQ, h), half(XC, h), ACT.Square).then_inc(s["ln_sq"], 1)
                a.wait_ge(s["ln_var"], k + 1)
                a.activation(SDC[:, :], bank(2, QU), ACT.Sqrt, bias=con_(eps, 1)).then_inc(s["ln_sd"], 1)

            a.dma_start(half(X, 1), half(x, 1)).then_inc(s["x_low_in"], 16)
            a.wait_ge(s["par_in"], 16)
            a.wait_ge(s["con_head"], 16)
            a.activation(BN[:, 0:2], par_("va", 0, 2), ACT.Sqrt, bias=con_("eps5", 1)).then_inc(s["bn_sd"], 1)
            a.activation(WSM[:, 36:40], par_("sg", 0, 4), ACT.Sqrt).then_inc(s["sg_ready"], 1)
            a.wait_ge(s["sg_ready"], 1)
            a.activation(WSM[:, 40:44], WSM[:, 36:40], ACT.Sqrt).then_inc(s["sg_ready"], 1)
            norm(0, "eps6")
            a.wait_ge(s["c1_done"], 1)
            a.activation(half(Y1, 0), bank(4), ACT.Copy).then_inc(s["y1_ready"], 1)

            a.wait_ge(s["y1_ready"], 2)
            a.wait_ge(s["wa1_in"], 32)
            for g in range(8):
                slot = g % RG
                if g >= RG:
                    a.wait_ge(s["ring_free"], g - RG + 1)
                for cg in range(4):
                    if on_scalar(g, cg):
                        co = 8 * cg + g
                        a.activation(RING[:, 4 * slot + cg, :], Y1[:, :], ACT.Abs, bias=WA1[:, co:co + 1],
                                     scale=-1.0).then_inc(s["act_unit"], 1)
            a.wait_ge(s["adder_done"], 1)
            a.wait_ge(s["bn_ready"], 1)
            a.wait_ge(s["pads"], 2)
            for h in range(2):
                a.activation(rows(H1P, h, 1, 1), grid(bank(6 + h)), ACT.Relu, bias=BN[:, 10:11],
                             scale=BN[:, 8:9]).then_inc(s["h1_ready"], 1)
            a.wait_ge(s["w_chain"], 2)
            a.activation(WSM[:, 8:12], WSM[:, 4:8], ACT.Exp, accum_out=WSM[:, 12:13]).then_inc(s["wexp"], 1)
            a.activation(WSM[:, 44:45], con_("eps6", 1), ACT.Sqrt)
            a.wait_ge(s["c2_done"], 1)
            a.activation(rows(Y2P, 0, 1, 1), grid(bank(4)), ACT.Copy).then_inc(s["y2_ready"], 1)

            a.wait_ge(s["y2_ready"], 2)
            a.wait_ge(s["w_a_in"], 16)
            with a.Fori(0, 3) as dh:
                for p, units in enumerate(PLAN):
                    a.wait_ge(s["ring_free"], dh * GROUPS + (8 + p - RG + 1))
                    for cg, (c8, dws) in enumerate(units):
                        if on_scalar(c8, cg):
                            a.activation(grid(RING[:, 4 * ((8 + p) % RG) + cg, :]), window(dh, dws[0]), ACT.Abs,
                                         bias=WA2[:, ds(dh * 96 + (32 * dws[0] + 8 * cg + c8), 1)],
                                         scale=-1.0).then_inc(s["act_unit"], 1)
            a.wait_ge(s["adder_done"], 2)
            for h in range(2):
                a.activation(half(SQ, h), bank(6 + h), ACT.Relu, bias=BN[:, 11:12], scale=BN[:, 9:10]).then_inc(s["h2_ready"], 1)
            norm(1, "eps5")

            a.wait_ge(s["decided"], 1)
            code = a.alloc_register("a_code"); na = a.alloc_register("a_na"); nf = a.alloc_register("a_nf")
            a.load(code, KINT[0:1, 0:1], bass_reorder=False)
            a.reg_mov(code, a.snap(code) & (OPW - 1))
            a.reg_mov(na, 0); a.reg_mov(nf, 0)
            chosen = a.alloc_register("a_chosen")
            a.reg_mov(chosen, 1)
            with active_steps(a, code) as c:
                with a.If((c & 1) > 0):
                    k = a.snap(na, min_val=0, max_val=NB)
                    a.wait_ge(s["att_proj"], k * 4 + 2)
                    for b in range(2):
                        q = slice(32 * b, 32 * b + 32)
                        a.activation(QZ[q, b, :].rearrange("p (h t) -> p h t", h=2), PS[q, 4:6, 0:HT],
                                     ACT.Copy).then_inc(s["qz_act"], 1)

                    def exponential(b, j):
                        a.wait_ge(s["less_max"], k * 28 + (NQ * b + j + 1))
                        tile = SCR[0:QT, NQ * (b % 2) + j, :]
                        a.activation(tile, tile, ACT.Exp, scale=SCALE).then_inc(s["exp_done"], 1)

                    def sums_out(b):
                        a.wait_ge(s["pv_done"], k * 16 + (4 * b + 4))
                        a.activation(AE[b][:, :].rearrange("p (h t) -> p h t", h=2), PS[:, 6:8, 0:HT],
                                     ACT.Copy).then_inc(s["ae_done"], 1)

                    for b in range(NIMG + 1):
                        for j in range(NQ):
                            if b < NIMG:
                                u = NQ * b + j
                                a.wait_ge(s["st_done"], k * 28 + (u + 1))
                                if b >= 2:
                                    a.wait_ge(s["pv_done"], k * 16 + (4 * (b - 2) + j // 2 + 1))
                                pr = score_banks(b, j)
                                a.activation(SCR[0:QT, NQ * (b % 2) + j, :].rearrange("p (h t) -> p h t", h=2),
                                             PS[0:QT, pr:pr + 2, 0:HT], ACT.Copy).then_inc(s["score_cp"], 1)
                            if b >= 2 and j == 0:
                                exponential(b - 2, NQ - 1)
                            if b >= 2 and j == 1:
                                sums_out(b - 2)
                            if b >= 1 and j >= 2:
                                exponential(b - 1, j - 2)
                        if b >= 1:
                            exponential(b - 1, NQ - 2)
                    exponential(NIMG - 1, NQ - 1)
                    sums_out(NIMG - 1)
                    for h in range(2):
                        a.wait_ge(s["att_wo"], k * 2 + (h + 1))
                        a.activation(half(RS, h), bank(h), ACT.Copy).then_inc(s["att_num"], 1)
                    a.reg_add(na, na, 1)
                with a.If((c & 2) > 0):
                    k = a.snap(nf, min_val=0, max_val=NB)
                    a.wait_ge(s["ffn_wa"], k * 16 + 16)
                    a.wait_ge(s["ffn_wb"], k * 16 + 16)
                    for u in range(0, 8, 2):
                        a.wait_ge(s["ffn_h1"], k * 8 + (u + 1))
                        a.activation(HIDT[:, u, :], bank(u % 4), ACT.Relu, bias=B1S).then_inc(s["hid_act"], 1)
                    a.wait_ge(s["ffn_out"], k * 2 + 1)
                    a.activation(half(H, 0), bank(4), ACT.Identity, bias=B2S).then_inc(s["ffn_h"], 1)
                    a.reg_add(nf, nf, 1)
                n = a.snap(chosen, min_val=1, max_val=NB)
                a.wait_ge(s["decided"], n + 1)
                a.reg_add(chosen, chosen, 1)
                a.load(code, KINT[0:1, 0:1], bass_reorder=False)
                a.reg_mov(code, a.snap(code) & (OPW - 1))

            a.activation(WSM[:, 44:45], con_("eps6", 1), ACT.Sqrt)
            norm(2, "eps6")
            for i in range(2):
                for h in range(2):
                    a.wait_ge(s["cc_done"], 2 * i + h + 1)
                    a.activation(half(SQ, h), bank(4 + h), ACT.Relu, bias=QS[:, 10 + i:11 + i],
                                 scale=QS[:, 8 + i:9 + i]).then_inc(s["cv_relu"], 1)
            norm(3, "eps5")
            a.wait_ge(s["zeroed"], 6)
            for h in range(2):
                a.wait_ge(s["ln_out"], 6 + h + 1)
                lo = h * HT
                a.activation(URV[:, 1024 - lo - HT:1024 - lo], UPZ[:, 2 + lo + HT - 1:2 + lo - 1:-1],
                             ACT.Copy).then_inc(s["urv_ready"], 1)
            a.wait_ge(s["ut_done"], 1)
            a.activation(UT[:, 0:4, :], PS[:, 4, 0:512].rearrange("p (i m) -> p i m", i=4), ACT.Copy).then_inc(s["ut_ready"], 1)
            for u in range(0, 64, 2):
                a.wait_ge(s["u_done"], u + 1)
                if u >= 8:
                    a.wait_ge(s["mix_done"], u // 4 - 1)
                a.activation(UEV[:, u % 8, :], bank(u % 6), ACT.Copy).then_inc(s["uev_act"], 1)

        @block.vector
        def _(v):
            nln = 0

            def norm(k, src, dst, dst_free=None):
                for h in range(2):
                    v.wait_ge(s["ln_mean"], 2 * k + h + 1)
                    v.tensor_tensor(half(XC, h), half(src, h), bank(h), ALU.subtract).then_inc(s["ln_cent"], 1)
                v.wait_ge(s["ln_sd"], k + 1)
                v.reciprocal(RSC[:, :], SDC[:, :]).then_inc(s["ln_rs"], 1)
                for h in range(2):
                    v.wait_ge(s["ln_bc"], 2 * k + h + 1)
                    v.tensor_tensor(dst(h), half(XC, h), bank(h), ALU.mult).then_inc(s["ln_out"], 1)

            nw = 0

            def wl(ins):
                nonlocal nw
                nw += 1
                ins.then_inc(s["w_chain"], 1)
                v.wait_ge(s["w_chain"], nw)

            v.memset(XC[:, 0:QU], 0.0).then_inc(s["idle_src"], 1)
            v.wait_ge(s["par_in"], 16)
            wl(v.tensor_tensor(WSM[:, 0:4], par_("lw", 0, 4), par_("gu", 0, 4), ALU.add))
            v.tensor_reduce(WSM[:, 13:14], WSM[:, 0:4], AX.X, ALU.max).then_inc(s["bn_chain"], 1)
            v.wait_ge(s["bn_chain"], 1)
            wl(v.tensor_scalar(WSM[:, 4:8], WSM[:, 0:4], WSM[:, 13:14], None, ALU.subtract))
            v.memset(WSM[:, 16:24], -1.0).then_inc(s["bn_chain"], 1)
            v.wait_ge(s["x_in"], 16)
            v.wait_ge(s["x_low_in"], 16)
            norm(0, X, lambda h: half(XN, h))
            v.wait_ge(s["bn_chain"], 2)

            nb = 2

            def bl(ins):
                nonlocal nb
                nb += 1
                ins.then_inc(s["bn_chain"], 1)
                v.wait_ge(s["bn_chain"], nb)

            def batch_norms():
                v.wait_ge(s["sum_in"], 32)
                v.tensor_reduce(BN[:, 2:3], WA1R[:, :], AX.X, ALU.add)
                bl(v.tensor_reduce(BN[:, 3:4], WA2R[:, :], AX.X, ALU.add))
                v.wait_ge(s["bn_sd"], 1)
                bl(v.reciprocal(BN[:, 4:6], BN[:, 0:2]))
                bl(v.tensor_tensor(BN[:, 6:8], BN[:, 4:6], par_("g", 0, 2), ALU.mult))
                v.tensor_scalar(BN[:, 8:10], BN[:, 6:8], -1.0, None, ALU.mult)
                bl(v.scalar_tensor_tensor(BN[:, 12:14], BN[:, 2:4], con_("dmask", 1), par_("mu", 0, 2), ALU.mult, ALU.subtract))
                bl(v.tensor_tensor(BN[:, 14:16], BN[:, 12:14], BN[:, 6:8], ALU.mult))
                v.tensor_tensor(BN[:, 10:12], BN[:, 14:16], par_("be", 0, 2), ALU.add).then_inc(s["bn_ready"], 1)

            v.wait_ge(s["c1_done"], 2)
            v.tensor_copy(half(Y1, 1), bank(5)).then_inc(s["y1_ready"], 1)
            v.wait_ge(s["y1_ready"], 2)
            v.wait_ge(s["wa1_in"], 32)
            for g in range(8):
                slot = g % RG
                if g == 4:
                    batch_norms()
                if g >= RG:
                    v.wait_ge(s["ring_free"], g - RG + 1)
                for cg in range(4):
                    if not on_scalar(g, cg):
                        co = 8 * cg + g
                        v.tensor_scalar(RING[:, 4 * slot + cg, :], Y1[:, :], WA1[:, co:co + 1], None,
                                        ALU.max).then_inc(s["dve_unit"], 1)

            v.wait_ge(s["mask_in"], 32)
            nk = 0

            def kl(ins):
                nonlocal nk
                nk += 1
                ins.then_inc(s["key_chain"], 1)
                v.wait_ge(s["key_chain"], nk)

            v.tensor_copy(AMF[0:1, :], AMT[0:1, :])
            kl(v.tensor_copy(KEYT[0:1, :], FMT[0:1, :]))
            kl(v.scalar_tensor_tensor(KEYT[0:1, :], KEYT[0:1, :], 2.0, AMF[0:1, :], ALU.mult, ALU.add))
            kl(v.tensor_scalar(AMF[0:1, :], KEYT[0:1, :], 0.0, None, ALU.is_gt))
            kt = KEYT[0:1, :].rearrange("p (o b) -> p o b", o=NOPS)
            af = AMF[0:1, :].rearrange("p (o b) -> p o b", o=NOPS)
            b4 = con_("blk4", NB, 1).unsqueeze(1).to_broadcast([1, NOPS, NB])
            kl(v.tensor_tensor(af, af, b4, ALU.mult))
            v.tensor_tensor(kt, kt, af, ALU.add).then_inc(s["key_ready"], 1)
            v.memset(PREV[0:1, :], 1e6).then_inc(s["key_ready"], 1)
            v.wait_ge(s["key_ready"], 2)

            lk = LOOK[0:1, :].rearrange("p (o b) -> p o b", o=NOPS)

            def look_ahead():
                v.tensor_tensor(lk, b4, PREV[0:1, :].unsqueeze(2).to_broadcast([1, NOPS, NB]), ALU.is_lt)
                v.drain()
                v.tensor_tensor(lk, lk, kt, ALU.mult)
                v.drain()
                v.tensor_reduce(NEXT[0:1, :], lk, AX.X, ALU.max)
                v.drain()
                v.tensor_tensor(NEXT[0:1, :], NEXT[0:1, :], con_("opw", NOPS, 1), ALU.add)
                v.drain()

            def past():
                v.tensor_single_scalar(PINT[0:1, :], KINT[0:1, :], OPW - 4, ALU.bitwise_and)
                v.drain()
                v.tensor_copy(PREV[0:1, :], PINT[0:1, :])
                v.drain()

            look_ahead()

            v.wait_ge(s["cw_in"], 32)
            v.tensor_reduce(WMX[:, 0:1], CW1[:, :], AX.X, ALU.max, apply_absolute_value=True).then_inc(s["wmx_part"], 1)
            v.tensor_reduce(WMX[:, 1:2], CW2[:, :], AX.X, ALU.max, apply_absolute_value=True).then_inc(s["wmx_part"], 1)
            v.wait_ge(s["wexp"], 1)
            v.wait_ge(s["con_in"], 16)
            wl(v.reciprocal(WSM[:, 14:15], WSM[:, 12:13]))
            wl(v.tensor_scalar(WSM[:, 16:20], WSM[:, 8:12], WSM[:, 14:15], None, ALU.mult))
            wl(v.max(MX8[:, :], WSM[:, 16:24]))
            wl(v.max_index(WIX[:, :], MX8[:, :], WSM[:, 16:24]))
            wl(v.tensor_copy(WSM[:, 15:16], WIX[:, 0:1]))
            wl(v.tensor_scalar(WSM[:, 28:32], con_("iota", 4), WSM[:, 15:16], None, ALU.is_equal))
            wl(v.tensor_tensor(WSM[:, 32:36], WSM[:, 28:32], WSM[:, 16:20], ALU.subtract))
            v.tensor_tensor(WSM[:, 24:28], WSM[:, 32:36], WSM[:, 16:20], ALU.add).then_inc(s["w_soft"], 1)
            v.wait_ge(s["wmx_rows"], 1)
            v.tensor_reduce(WRW[0:1, :], PS[0:1, 0, 0:256].rearrange("p (a b) -> p a b", a=2), AX.X, ALU.max).then_inc(s["wmx_row"], 1)
            v.wait_ge(s["wmx_bc"], 1)
            nq = 0

            def ql(ins):
                nonlocal nq
                nq += 1
                ins.then_inc(s["q_chain"], 1)
                v.wait_ge(s["q_chain"], nq)

            ql(v.tensor_scalar(QS[:, 0:2], PS[:, 1, 0:2], 1.0 / 127.0, None, ALU.mult))
            v.reciprocal(QS[:, 2:4], QS[:, 0:2]).then_inc(s["q_sc"], 1)
            ql(v.reciprocal(QS[:, 4:7], par_("sc", 0, 3)))
            ql(v.tensor_tensor(QS[:, 8:10], QS[:, 0:2], par_("sc", 0, 2), ALU.mult))
            ql(v.reciprocal(QS[:, 12:14], QS[:, 8:10]))
            ql(v.tensor_tensor(QS[:, 14:16], par_("cb", 0, 2), QS[:, 12:14], ALU.mult))
            ql(v.tensor_scalar(QS[:, 14:16], QS[:, 14:16], -2.0 ** 31, 2.0 ** 31, ALU.max, ALU.min))
            ql(v.tensor_scalar(QS[:, 16:18], QS[:, 14:16], MAGIC, -MAGIC, ALU.add, ALU.add))
            ql(v.tensor_tensor(QS[:, 18:20], QS[:, 14:16], QS[:, 14:16], ALU.mult))
            ql(v.tensor_scalar(QS[:, 18:20], QS[:, 18:20], 2.0 ** 44, None, ALU.is_lt))
            ql(v.tensor_tensor(QS[:, 16:18], QS[:, 16:18], QS[:, 14:16], ALU.subtract))
            ql(v.tensor_tensor(QS[:, 16:18], QS[:, 16:18], QS[:, 18:20], ALU.mult))
            ql(v.tensor_tensor(QS[:, 16:18], QS[:, 16:18], QS[:, 14:16], ALU.add))
            ql(v.tensor_tensor(QS[:, 10:12], QS[:, 16:18], QS[:, 8:10], ALU.mult))

            v.wait_ge(s["c2_done"], 2)
            v.tensor_copy(rows(Y2P, 1, 1, 1), grid(bank(5))).then_inc(s["y2_ready"], 1)
            v.wait_ge(s["y2_ready"], 2)
            v.wait_ge(s["w_a_in"], 16)
            with v.Fori(0, 3) as dh:
                done = 0
                for p, units in enumerate(PLAN):
                    v.wait_ge(s["ring_free"], dh * GROUPS + (8 + p - RG + 1))
                    mine = [(cg, u) for cg, u in enumerate(units) if not on_scalar(u[0], cg)]
                    for cg, (c8, dws) in sorted(mine, key=lambda m: -len(m[1][1])):
                        ins = v.tensor_scalar(grid(RING[:, 4 * ((8 + p) % RG) + cg, :]), window(dh, dws[0]),
                                              WA2[:, ds(dh * 96 + (32 * dws[0] + 8 * cg + c8), 1)], None, ALU.max)
                        ins.then_inc(s["dve_unit" if len(dws) == 1 else "pair_part"], 1)
                    for cg, (c8, dws) in mine:
                        if len(dws) == 2:
                            done += 1
                            v.wait_ge(s["pair_part"], dh * PAIRS + done)
                            unit = grid(RING[:, 4 * ((8 + p) % RG) + cg, :])
                            v.scalar_tensor_tensor(unit, window(dh, dws[1]),
                                                   WA2[:, ds(dh * 96 + (32 * dws[1] + 8 * cg + c8), 1)], unit,
                                                   ALU.max, ALU.add).then_inc(s["dve_unit"], 1)
            for h in range(2):
                v.wait_ge(s["perm_done"], h + 1)
                v.tensor_tensor(half(XC, h), bank(4 + h), half(XN, h), ALU.add).then_inc(s["x1_tmp"], 1)
                v.wait_ge(s["x1_tmp"], h + 1)
                v.scalar_tensor_tensor(half(X1, h), half(XC, h), 0.0, half(X, h), ALU.max, ALU.add).then_inc(s["x1_ready"], 1)
            v.wait_ge(s["x1_ready"], 2)
            norm(1, X1, lambda h: half(H, h))

            def decide(count):
                v.wait_ge(s["row_done"], count)
                row = PS[0:1, 6, 0:NOPS]
                v.tensor_reduce(KMAX[0:1, :], row, AX.X, ALU.max)
                v.drain()
                v.scalar_tensor_tensor(CAND[0:1, :], row, KMAX[0:1, :], NEXT[0:1, :], ALU.is_equal, ALU.mult)
                v.drain()
                v.tensor_reduce(KMAX[0:1, :], CAND[0:1, :], AX.X, ALU.max)
                v.drain()
                v.tensor_copy(KINT[0:1, :], KMAX[0:1, :]).then_inc(s["decided"], 1)
                v.drain()

            def residual():
                v.tensor_tensor(X[:, :], X1[:, :], H[:, :], ALU.add).then_inc(s["x2_ready"], 1)

            decide(1)
            residual()
            code = v.alloc_register("v_code"); na = v.alloc_register("v_na"); nf = v.alloc_register("v_nf")
            v.wait_ge(s["decided"], 1)
            v.load(code, KINT[0:1, 0:1], bass_reorder=False)
            v.reg_mov(code, v.snap(code) & (OPW - 1))
            chosen = v.alloc_register("v_chosen")
            v.reg_mov(chosen, 1)
            v.reg_mov(na, 0); v.reg_mov(nf, 0)
            with active_steps(v, code) as c:
                past()
                look_ahead()
                with v.If((c & 1) > 0):
                    k = v.snap(na, min_val=0, max_val=NB)
                    v.wait_ge(s["att_w"], k * 16 + 16)
                    for b in range(NIMG):
                        q = slice(32 * b, 32 * b + 32)
                        v.tensor_copy(W4B[q, 0:3, q], W4R[q, 0:3, :]).then_inc(s["att_diag"], 1)
                    v.tensor_copy(W4B[0:64, 3, 0:C], W4R[0:64, 3, :]).then_inc(s["wo_diag"], 1)
                    v.wait_ge(s["att_proj"], k * 4 + 4)
                    v.tensor_copy(KEYS[:, :].rearrange("p (h t) -> p h t", h=2), PS[:, 2:4, 0:HT]).then_inc(s["keys_done"], 1)
                    for b in range(2, NIMG):
                        q = slice(32 * b, 32 * b + 32)
                        v.tensor_copy(QZ[q, b, :].rearrange("p (h t) -> p h t", h=2), PS[q, 4:6, 0:HT]).then_inc(s["qz_dve"], 1)
                    v.wait_ge(s["v_proj"], k + 1)
                    v.tensor_copy(VT[0:QT, 0:4, :], PS[0:QT, 6, 0:512].rearrange("p (j m) -> p j m", j=4))
                    v.tensor_copy(VT[0:QT, 4:7, :], PS[0:QT, 7, 0:384].rearrange("p (j m) -> p j m", j=3)).then_inc(s["v_done"], 1)

                    def less_max(b, j):
                        v.wait_ge(s["mrow_done"], k * 4 + (b + 1))
                        tile = SCR[0:QT, NQ * (b % 2) + j, :].rearrange("p (h t) -> p h t", h=2)
                        v.tensor_tensor(tile, tile, PS[0:QT, 4:6, 0:HT], ALU.add).then_inc(s["less_max"], 1)

                    for b in range(NIMG):
                        for j in range(1, NQ):
                            v.wait_ge(s["score_cp"], k * 28 + (NQ * b + j + 1))
                            if j == 1:
                                if b:
                                    v.wait_ge(s["top_tr"], k * 4 + b)
                                before = SCR[0:QT, NQ * (b % 2), :]
                            else:
                                v.wait_ge(s["top_step"], k * 24 + (6 * b + j - 1))
                                before = TOP[0:QT, :]
                            v.tensor_tensor(TOP[0:QT, :], before, SCR[0:QT, NQ * (b % 2) + j, :], ALU.max).then_inc(s["top_step"], 1)
                            if b:
                                less_max(b - 1, j - 1)
                        v.wait_ge(s["top_tr"], k * 4 + (b + 1))
                        v.tensor_reduce(SMX[0:QT, 0:4], PS[0:QT, 2, 0:4 * QT].rearrange("p (j m) -> p j m", j=4), AX.X, ALU.max)
                        v.tensor_reduce(SMX[0:QT, 4:NQ], PS[0:QT, 3, 0:3 * QT].rearrange("p (j m) -> p j m", j=3), AX.X,
                                        ALU.max).then_inc(s["smax_done"], 1)
                        if b:
                            less_max(b - 1, NQ - 1)
                    for j in range(NQ):
                        less_max(NIMG - 1, j)
                    v.wait_ge(s["att_den"], k + 1)
                    v.reciprocal(RSC[:, :], bank(4, QU)).then_inc(s["att_rs"], 1)
                    for h in range(2):
                        v.wait_ge(s["att_num"], k * 2 + (h + 1))
                        v.wait_ge(s["att_bc"], k * 2 + (h + 1))
                        v.tensor_tensor(half(H, h), half(RS, h), bank(2 + h), ALU.mult).then_inc(s["att_h"], 1)
                    v.reg_add(na, na, 1)
                with v.If((c & 2) > 0):
                    k = v.snap(nf, min_val=0, max_val=NB)
                    v.wait_ge(s["ffn_wa"], k * 16 + 16)
                    for b in range(NIMG):
                        q = slice(32 * b, 32 * b + 32)
                        v.tensor_copy(W1B[q, b, :], W1R[q, 0:HID]).then_inc(s["ffn_diag"], 1)
                    v.wait_ge(s["ffn_wb"], k * 16 + 16)
                    for u in range(1, 8, 2):
                        v.wait_ge(s["ffn_h1"], k * 8 + (u + 1))
                        v.tensor_scalar(HIDT[:, u, :], bank(u % 4), B1S, 0.0, ALU.add, ALU.max).then_inc(s["hid_dve"], 1)
                    v.wait_ge(s["ffn_out"], k * 2 + 2)
                    v.tensor_scalar(half(H, 1), bank(5), B2S, None, ALU.add).then_inc(s["ffn_h"], 1)
                    v.reg_add(nf, nf, 1)
                n = v.snap(chosen, min_val=1, max_val=NB)
                decide(n + 1)
                residual()
                v.reg_add(chosen, chosen, 1)
                v.load(code, KINT[0:1, 0:1], bass_reorder=False)
                v.reg_mov(code, v.snap(code) & (OPW - 1))

            norm(2, X, lambda h: half(XN, h))

            def hold(src, recip, low, high, tmp):
                ql(v.tensor_scalar(tmp, src, recip, low, ALU.mult, ALU.max))
                ql(v.tensor_scalar(tmp, tmp, high, MAGIC, ALU.min, ALU.add))

            v.wait_ge(s["pads"], 3)
            for h in range(2):
                v.wait_ge(s["ln_out"], 4 + h + 1)
                hold(half(XN, h), QS[:, 4:5], -128.0, 127.0, half(SD, h))
                v.tensor_scalar(rows(XQP, h, 1, 1), grid(half(SD, h)), -MAGIC, None, ALU.add).then_inc(s["q_xin"], 1)
            for h in range(2):
                v.wait_ge(s["cv_relu"], h + 1)
                hold(half(SQ, h), QS[:, 5:6], 0.0, 255.0, half(XC, h))
                v.tensor_scalar(rows(HQP, h, 1, 1), grid(half(XC, h)), -MAGIC, None, ALU.add).then_inc(s["cv_q"], 1)
            for h in range(2):
                v.wait_ge(s["cv_relu"], 2 + h + 1)
                hold(half(SQ, h), QS[:, 6:7], 0.0, 255.0, half(SD, h))
                ql(v.tensor_scalar(half(RS, h), half(SD, h), -MAGIC, None, ALU.add))
                v.scalar_tensor_tensor(half(X1, h), half(RS, h), par_("sc", 2), half(X, h), ALU.mult, ALU.add).then_inc(s["x3_ready"], 1)
            v.wait_ge(s["x3_ready"], 2)
            v.wait_ge(s["zeroed"], 6)
            norm(3, X1, lambda h: UPZ[:, 2 + h * HT:2 + (h + 1) * HT])
            v.wait_ge(s["ut_done"], 2)
            v.tensor_copy(UT[:, 4:8, :], PS[:, 5, 0:512].rearrange("p (i m) -> p i m", i=4)).then_inc(s["ut_ready"], 1)
            for u in range(1, 64, 2):
                v.wait_ge(s["u_done"], u + 1)
                if u >= 8:
                    v.wait_ge(s["mix_done"], u // 4 - 1)
                v.tensor_copy(UEV[:, u % 8, :], bank(u % 6)).then_inc(s["uev_dve"], 1)
            v.wait_ge(s["mix_done"], 16)
            x3 = X1[:, :].rearrange("p (t a) -> p t a", a=2)
            y = Y1[:, :].rearrange("p (t a) -> p t a", a=2)
            for a2 in range(2):
                v.tensor_tensor(y[:, :, a2], x3[:, :, a2], bank(6 + a2), ALU.add).then_inc(s["y_ready"], 1)

        @block.tensor
        def _(t):
            def mm(out_, lhsT, rhs, start=True, stop=True):
                return t.matmul(out_, lhsT, rhs, start=start, stop=stop, skip_group_check=True)

            def keep_warm(n, src=CON, b=3):
                for _ in range(n):
                    mm(bank(b, QU), src[:, 0:P], src[:, 0:QU])

            def spread(h, to):
                for q in (2 * h, 2 * h + 1):
                    last = mm(PS[:, to + h, QU * (q % 2):QU * (q % 2) + QU], con_("spread", 512)[:, P * q:P * q + P], RSC[:, :])
                return last

            def norm(k, src, ready=None):
                for h in range(2):
                    if k == 0:
                        t.wait_ge(s["x_low_in" if h else "x_in"], 16)
                    if ready:
                        t.wait_ge(s[ready], h + 1)
                    mm(bank(h), con_("bones"), half(src, h)).then_inc(s["ln_mean"], 1)
                keep_warm(WARM["means"])
                for q in range(4):
                    t.wait_ge(s["ln_sq"], 2 * k + q // 2 + 1)
                    last = mm(PS[32 * q:32 * q + 32, 2, 0:QU], con_("vsel", C), quarter(SQ, q))
                last.then_inc(s["ln_var"], 1)
                keep_warm(WARM["deviations"])
                t.wait_ge(s["ln_rs"], k + 1)
                for h in range(2):
                    spread(h, 0).then_inc(s["ln_bc"], 1)

            t.wait_ge(s["idle_src"], 1)
            keep_warm(WARM["inputs"], XC)
            t.wait_ge(s["con_head"], 16)
            norm(0, X)
            t.wait_ge(s["wa1_in"], 32)
            for h in range(2):
                t.wait_ge(s["ln_out"], h + 1)
                mm(bank(4 + h), WS1[:, :], half(XN, h)).then_inc(s["c1_done"], 1)

            def group(c8s, slot):
                for h in range(2):
                    for cg in range(4):
                        last = mm(PS[32 * cg:32 * cg + 32, 6 + h, 0:HT], SEL[on_scalar(c8s[cg], cg)][:, c8s[cg], :],
                                  half(RING[:, 4 * slot + cg, :], h), start=False, stop=False)
                return last

            t.wait_ge(s["con_in"], 16)
            t.wait_ge(s["y1_ready"], 2)
            for h in range(2):
                mm(bank(6 + h), con_("corr"), half(Y1, h))
            for g in range(8):
                t.wait_ge(s["dve_unit"], DVE_BY[g + 1])
                t.wait_ge(s["act_unit"], ACT_BY[g + 1])
                last = group([g] * 4, g % RG)
                last.then_inc(s["ring_free"], 1)
            mm(PS[0:1, 5, 500:501], CON[:, 0:1], CON[:, 0:1]).then_inc(s["adder_done"], 1)
            t.wait_ge(s["ws2_in"], 16)
            for h in range(2):
                for tap in range(9):
                    if h == 0 and tap in (0, 6):
                        t.wait_ge(s["h1_ready"], tap // 6 + 1)
                    if h and tap == 2:
                        t.wait_ge(s["wmx_part"], 2)
                        for i in range(2):
                            last = mm(PS[0:1, 0, 128 * i:128 * i + 128], WMX[:, i:i + 1], con_("ident"))
                        last.then_inc(s["wmx_rows"], 1)
                    if h and tap == 5:
                        t.wait_ge(s["wmx_row"], 1)
                        mm(PS[:, 1, 0:2], con_("ones", P, 1), WRW[0:1, :]).then_inc(s["wmx_bc"], 1)
                    last = mm(grid(bank(4 + h)), WS2[:, tap, :], rows(H1P, h, tap // 3, tap % 3), tap == 0, tap == 8)
                last.then_inc(s["c2_done"], 1)

            t.wait_ge(s["y2_ready"], 2)
            for h in range(2):
                mm(grid(bank(6 + h)), con_("zero"), rows(Y2P, h, 1, 1))
            with t.Fori(0, 3) as dh:
                for p, units in enumerate(PLAN):
                    t.wait_ge(s["dve_unit"], dh * DVE_ROW[GROUPS] + (DVE_BY[8] + DVE_ROW[p + 1]))
                    t.wait_ge(s["act_unit"], dh * ACT_ROW[GROUPS] + (ACT_BY[8] + ACT_ROW[p + 1]))
                    group([c8 for c8, _ in units], (8 + p) % RG).then_inc(s["ring_free"], 1)
            t.wait_ge(s["xs9_ready"], 1)
            for h in range(2):
                last = mm(bank(6 + h), con_("corr"), half(XS9, h), start=False, stop=False)
            last.then_inc(s["adder_done"], 1)
            for h in range(2):
                t.wait_ge(s["h2_ready"], h + 1)
                mm(bank(4 + h), con_("perm"), half(SQ, h)).then_inc(s["perm_done"], 1)
            norm(1, X1, "x1_ready")
            t.wait_ge(s["ln_out"], 4)

            def token_row():
                mm(PS[0:1, 6, 0:32], H[:, 0:1], con_("ident", 32)).then_inc(s["row_done"], 1)
                keep_warm(WARM["choice"])

            token_row()
            t.wait_ge(s["decided"], 1)
            code = t.alloc_register("t_code"); na = t.alloc_register("t_na"); nf = t.alloc_register("t_nf")
            t.load(code, KINT[0:1, 0:1], bass_reorder=False)
            t.reg_mov(code, t.snap(code) & (OPW - 1))
            t.reg_mov(na, 0); t.reg_mov(nf, 0)
            chosen = t.alloc_register("t_chosen")
            t.reg_mov(chosen, 1)
            with active_steps(t, code) as c:
                keep_warm(WARM["weights"])
                with t.If((c & 1) > 0):
                    k = t.snap(na, min_val=0, max_val=NB)
                    t.wait_ge(s["zeroed"], 4)
                    t.wait_ge(s["att_diag"], k * 4 + 4)
                    for i, b0 in ((0, 4), (1, 2)):
                        for h in range(2):
                            mm(bank(b0 + h), W4B[:, i, :], half(H, h)).then_inc(s["att_proj"], 1)
                    for j in range(NQ):
                        last = mm(PS[0:QT, 6 + j // 4, P * (j % 4):P * (j % 4) + P], H[:, QT * j:QT * j + QT], W4B[:, 2, :])
                    last.then_inc(s["v_proj"], 1)
                    t.wait_ge(s["keys_done"], k + 1)

                    def scores(b, j):
                        u, pr = NQ * b + j, score_banks(b, j)
                        if j == 0:
                            t.wait_ge(s["qz_act" if b < 2 else "qz_dve"], k * 2 + (b % 2 + 1))
                        if b and j < 2:
                            t.wait_ge(s["score_cp"], k * 28 + (u if j else u - 1))
                        elif j > 2 or (b == 0 and j == 2):
                            t.wait_ge(s["score_cp"], k * 28 + (u - 1))
                        for h in range(2):
                            last = mm(PS[0:QT, pr + h, 0:HT], KEYS[:, QT * j:QT * j + QT], half(QZ[:, b, :], h))
                        last.then_inc(s["st_done"], 1)

                    def maxima_transposed(b):
                        t.wait_ge(s["top_step"], k * 24 + (6 * b + 6))
                        for j in range(NQ):
                            last = mm(PS[0:QT, 2 + j // 4, QT * (j % 4):QT * (j % 4) + QT], TOP[0:QT, QT * j:QT * j + QT],
                                      con_("ident", QT, QT))
                        last.then_inc(s["top_tr"], 1)

                    def maxima_spread(b):
                        t.wait_ge(s["smax_done"], k * 4 + (b + 1))
                        if b:
                            t.wait_ge(s["less_max"], k * 28 + NQ * b)
                        else:
                            t.wait_ge(s["qz_act"], k * 2 + 2)
                            t.wait_ge(s["qz_dve"], k * 2 + 2)
                        for lo in (0, 112, 224, 336, 392, 448, 560, 672):
                            j, h = lo // QT, lo // HT
                            n = min(QT * (j + 1), HT if lo < HT else T) - lo
                            last = mm(PS[0:QT, 4 + h, lo - HT * h:lo - HT * h + n], SMX[0:QT, j:j + 1].to_broadcast([QT, QT]),
                                      con_("nident", QT, QT)[:, lo - QT * j:lo - QT * j + n])
                        last.then_inc(s["mrow_done"], 1)

                    def weigh(b, pair):
                        t.wait_ge(s["exp_done"], k * 28 + (NQ * b + min(2 * pair + 2, NQ)))
                        if pair == 0:
                            if b:
                                t.wait_ge(s["ae_done"], k * 4 + b)
                            else:
                                t.wait_ge(s["v_done"], k + 1)
                        for h in range(2):
                            for w in range(2):
                                for e in range(2):
                                    j = 2 * pair + e
                                    if j < NQ:
                                        q = 64 * w + 32 * e
                                        last = mm(PS[q:q + 32, 6 + h, 0:HT],
                                                  con_("ones", C, QT) if w else VT[0:QT, j, 32 * b:32 * b + 32],
                                                  half(SCR[0:QT, NQ * (b % 2) + j, :], h), pair == 0, j + 2 >= NQ)
                        last.then_inc(s["pv_done"], 1)

                    for b in range(NIMG):
                        for j in range(NQ):
                            scores(b, j)
                            if b >= 1 and j == 0:
                                if b >= 2:
                                    weigh(b - 2, 2)
                                maxima_transposed(b - 1)
                            if b >= 1 and j == 1:
                                if b >= 2:
                                    weigh(b - 2, 3)
                                maxima_spread(b - 1)
                            if b >= 1 and j in (5, 6):
                                weigh(b - 1, j - 5)
                    maxima_transposed(NIMG - 1)
                    weigh(NIMG - 2, 2)
                    maxima_spread(NIMG - 1)
                    weigh(NIMG - 2, 3)
                    keep_warm(WARM["exponentials"], b=0)
                    for pair in range(4):
                        weigh(NIMG - 1, pair)
                    t.wait_ge(s["wo_diag"], k + 1)
                    keep_warm(WARM["sums"], b=0)
                    t.wait_ge(s["ae_done"], k * 4 + 4)
                    for b in range(NIMG):
                        for q in range(4):
                            last = mm(PS[32 * q:32 * q + 32, 4, 0:QU], con_("dsel")[:, 32 * b:32 * b + 32], quarter(AE[b], q),
                                      b == 0, b == 3)
                    last.then_inc(s["att_den"], 1)
                    for h in range(2):
                        for b in range(NIMG):
                            last = mm(PS[32 * b:32 * b + 32, h, 0:HT], W4B[:, 3, 0:C], half(AE[b], h))
                        last.then_inc(s["att_wo"], 1)
                    t.wait_ge(s["att_rs"], k + 1)
                    for h in range(2):
                        spread(h, 2).then_inc(s["att_bc"], 1)
                    t.wait_ge(s["att_h"], k * 2 + 2)
                    t.reg_add(na, na, 1)
                with t.If((c & 2) > 0):
                    k = t.snap(nf, min_val=0, max_val=NB)
                    t.wait_ge(s["zeroed"], 4)
                    for h in range(2):
                        for b in range(NIMG):
                            u = 4 * h + b
                            if h == 0:
                                t.wait_ge(s["ffn_diag"], k * 4 + (b + 1))
                            if u >= 4:
                                t.wait_ge(s["hid_act" if u % 2 == 0 else "hid_dve"], k * 4 + (u - 4) // 2 + 1)
                            mm(bank(u % 4), W1B[:, b, :], half(H, h)).then_inc(s["ffn_h1"], 1)
                    for h in range(2):
                        t.wait_ge(s["hid_act"], k * 4 + 2 * h + 2)
                        t.wait_ge(s["hid_dve"], k * 4 + 2 * h + 2)
                        if h == 0:
                            t.wait_ge(s["ffn_wb"], k * 16 + 16)
                        for b in range(NIMG):
                            last = mm(PS[32 * b:32 * b + 32, 4 + h, 0:HT], W2S[:, 0:C], HIDT[:, 4 * h + b, :])
                        last.then_inc(s["ffn_out"], 1)
                    t.wait_ge(s["ffn_h"], k * 2 + 2)
                    t.reg_add(nf, nf, 1)
                token_row()
                n = t.snap(chosen, min_val=1, max_val=NB)
                t.wait_ge(s["decided"], n + 1)
                t.reg_add(chosen, chosen, 1)
                t.load(code, KINT[0:1, 0:1], bass_reorder=False)
                t.reg_mov(code, t.snap(code) & (OPW - 1))

            n = t.snap(chosen, min_val=1, max_val=NB + 1)
            t.wait_ge(s["x2_ready"], n)
            norm(2, X)
            t.wait_ge(s["cq_done"], 2)
            for i, (w, src) in enumerate(((CQ1, XQP), (CQ2, HQP))):
                for h in range(2):
                    for tap in range(9):
                        if h == 0 and tap in (0, 6):
                            t.wait_ge(s["cv_q" if i else "q_xin"], tap // 6 + 1)
                        last = mm(grid(bank(4 + h)), w[:, P * tap:P * tap + P], rows(src, h, tap // 3, tap % 3), tap == 0, tap == 8)
                    last.then_inc(s["cc_done"], 1)
            norm(3, X1, "x3_ready")
            t.wait_ge(s["ln_out"], 8)

            def direct(a2):
                for n, (lo, hi, sgm) in enumerate(SEGS):
                    for lag in range(3):
                        c0 = 2 + a2 - lag + 2 * lo
                        last = mm(PS[:, 6 + a2, lo:hi], MUB[:, 3 * sgm + lag, :], UPZ[:, c0:c0 + 2 * (hi - lo) - 1:2],
                                  start=(n == 0 and lag == 0), stop=False)
                return last

            t.wait_ge(s["d_ready"], 4)
            direct(0)
            t.wait_ge(s["urv_ready"], 2)
            for c in range(2):
                for i in range(4):
                    a0 = 1024 - 255 - c - 256 * i
                    last = mm(PS[:, 4 + c, P * i:P * i + P], URV[:, a0:a0 + 255:2], con_("ident"))
                last.then_inc(s["ut_done"], 1)
            direct(1).then_inc(s["ar_done"], 1)
            t.wait_ge(s["ut_ready"], 2)
            t.wait_ge(s["strip_in"], 32)

            def filtered(u):
                grp, b = u // 4, u % 4
                g, a2, odd = grp // 4, (grp // 2) % 2, grp % 2
                c = a2 ^ odd
                if u >= 6:
                    t.wait_ge(s["uev_act" if u % 2 == 0 else "uev_dve"], (u - 6) // 2 + 1)
                for i in range(4):
                    n = NPH - P * i
                    for kk in range(4):
                        k = 4 * g + kk
                        if not odd:
                            m = HE[:, k, 0:n]
                        else:
                            m = HO[:, k, 1:1 + n] if a2 else HO[:, k, 0:n]
                        last = mm(PS[32 * kk:32 * kk + 32, u % 6, P * i:NPH], UT[:, 4 * c + i, 32 * b:32 * b + 32], m,
                                  i == 0, i == 3)
                last.then_inc(s["u_done"], 1)

            def mixed(grp):
                g, a2, odd = grp // 4, (grp // 2) % 2, grp % 2
                t.wait_ge(s["uev_act"], 2 * grp + 2)
                t.wait_ge(s["uev_dve"], 2 * grp + 2)
                for lo, hi, sgm in SEGS:
                    for b in range(4):
                        last = mm(PS[32 * b:32 * b + 32, 6 + a2, lo:hi], ASEG[:, odd, sgm, 32 * g:32 * g + 32],
                                  UEV[:, (4 * grp + b) % 8, lo:hi], False, False)
                last.then_inc(s["mix_done"], 1)

            for grp in range(16):
                for b in range(4):
                    filtered(4 * grp + b)
                if grp:
                    mixed(grp - 1)
            mixed(15)


def _constants():
    import numpy as np

    con = np.zeros((P, CC["n"]), np.float32)
    p = np.arange(P)
    con[:, CC["ident"]:CC["ident"] + P] = np.eye(P)
    con[:, CC["nident"]:CC["nident"] + P] = -np.eye(P)
    con[:, CC["bones"]:CC["bones"] + P] = (p[:, None] // 32 == p[None, :] // 32) / 32.0
    for c8 in range(8):
        for b in range(4):
            con[32 * b:32 * b + 32, CC["sel1"] + 32 * c8 + 8 * b + c8] = 1.0
            con[32 * b:32 * b + 32, CC["sel2"] + 32 * c8 + 8 * b + c8] = 2.0
    for r in range(P):
        cg, b, c8 = r // 32, (r // 8) % 4, r % 8
        if not on_scalar(c8, cg):
            con[32 * b:32 * b + 32, CC["corr"] + r] = -1.0
            con[r, CC["dmask"]] = 1.0
        con[r, CC["perm"] + 32 * b + 8 * cg + c8] = 1.0
    con[:, CC["ones"]:CC["ones"] + P] = 1.0
    for b in range(NIMG):
        con[[64, 96], CC["dsel"] + 40 * b:CC["dsel"] + 40 * b + 8] = 1.0
        con[32 * b:32 * b + 32, CC["vsel"] + 8 * b:CC["vsel"] + 8 * b + 8] = 1.0 / 32.0
        for q in range(4):
            a = CC["spread"] + P * q + 32 * b
            con[32 * q + 8 * b, a:a + 32] = 1.0
    con[:, CC["eps5"]] = 1e-5
    con[:, CC["eps6"]] = 1e-6
    con[:, CC["iota"]:CC["iota"] + 4] = np.arange(4)
    con[:, CC["opw"]:CC["opw"] + NOPS] = OPW * (NOPS - np.arange(NOPS))
    con[:, CC["blk4"]:CC["blk4"] + NB] = 4.0 * (NB - np.arange(NB))
    return con


def _diag(w):
    import numpy as np

    z = np.zeros((NIMG, C, w.shape[1], NIMG, C), w.dtype)
    for b in range(NIMG):
        z[b, :, :, b, :] = w
    return z.reshape(P, w.shape[1], P)


def _layout(i):
    import numpy as np

    co_of_r = np.array([8 * (r // 32) + r % 8 for r in range(P)])
    img_of_r = np.array([(r // 8) % 4 for r in range(P)])
    co_of_bc = np.tile(np.arange(C), NIMG)
    par = np.zeros((P, PC["n"]), np.float32)
    for k in range(2):
        for col, name in (("g", "gamma"), ("be", "beta"), ("mu", "mean"), ("va", "var")):
            par[:, PC[col] + k] = i[f"L0_conv_bn{k + 1}_{name}"][co_of_r]
        par[:, PC["cb"] + k] = i[f"L1_conv_b{k + 1}"][co_of_bc]
    for k, name in enumerate(("s_in", "s_a1", "s_a2")):
        par[:, PC["sc"] + k] = i[f"L1_conv_{name}"][0]
    par[:, PC["lw"]:PC["lw"] + 4] = i["L1_ffn_log_weights"]
    par[:, PC["gu"]:PC["gu"] + 4] = i["L1_ffn_gumbel"]
    par[:, PC["sg"]:PC["sg"] + 4] = np.repeat(i["L1_ffn_sigma"].reshape(4, 4).T, C, axis=0)
    ws2 = i["L0_conv_w_shift2"].reshape(C, C, 9).transpose(1, 2, 0)
    ws2r = np.zeros((P, 9, P), np.float32)
    for r in range(P):
        ws2r[r, :, 32 * img_of_r[r]:32 * img_of_r[r] + 32] = ws2[co_of_r[r]]
    wa2 = i["L0_conv_w_add2"].reshape(C, C, 9)
    phi = i["L1_ffn_phi"][:T]
    phe = np.zeros((NK, LE), np.float32)
    pho = np.zeros((NK, LO), np.float32)
    phe[:, 127:] = phi[0::2].T
    pho[:, 128:] = phi[1::2].T

    def mst(m):
        return m.reshape(4, 4, 4, C, C).transpose(2, 3, 0, 1, 4).reshape(P, 4, P)

    def conv(w):
        return _diag(w.reshape(C, C, 9).transpose(1, 2, 0)).reshape(P, 9 * P)

    return {
        "x": i["x"].reshape(P, T), "par": par, "con": _constants(),
        "ws1": _diag(i["L0_conv_w_shift1"].reshape(C, 1, C).transpose(2, 1, 0)).reshape(P, P),
        "wa1c": np.tile(i["L0_conv_w_add1"].reshape(C, C).T, (NIMG, 1)),
        "wa1r": i["L0_conv_w_add1"].reshape(C, C)[co_of_r],
        "ws2": ws2r,
        "wa2c": np.tile(wa2.transpose(1, 2, 0).reshape(C, 9 * C), (NIMG, 1)),
        "wa2r": wa2.reshape(C, 9 * C)[co_of_r],
        "amt": i["L0_ffn_attn_mask"].T.reshape(1, -1),
        "fmt": i["L0_ffn_ffn_mask"].T.reshape(1, -1),
        "fwa": np.concatenate((i["L0_ffn_ffn_w1"].reshape(-1, C, HID), i["L0_ffn_ffn_b2"].reshape(-1, C, 1)), 2),
        "fwb": np.concatenate((i["L0_ffn_ffn_w2"].reshape(-1, HID, C), i["L0_ffn_ffn_b1"].reshape(-1, HID, 1)), 2),
        "aw": np.concatenate([i[f"L0_ffn_{n}"].reshape(-1, C, C) for n in ("wq", "wk", "wv", "wo")], 2),
        "cw1": conv(i["L1_conv_w1"]), "cw2": conv(i["L1_conv_w2"]), "phe": phe, "pho": pho,
        "mpp": mst(i["L1_ffn_M_phi_plus"]), "mpm": mst(i["L1_ffn_M_phi_minus"]),
        "mu": i["L1_ffn_M_u"].transpose(2, 0, 1, 3).reshape(C, 4, 96),
    }


def kernel(**inputs):
    import numpy as np
    import concourse.bacc as bacc
    from concourse.bass_utils import run_bass_kernel_spmd

    arrays = {k: np.ascontiguousarray(v) for k, v in _layout({k: np.asarray(v) for k, v in inputs.items()}).items()}
    nc = bacc.Bacc("TRN2", target_bir_lowering=False, num_devices=1)
    args = [nc.dram_tensor(f"in_{n}", a.shape, mybir.dt.from_np(a.dtype), kind="ExternalInput").ap() for n, a in arrays.items()]
    out = nc.dram_tensor("out_y", (P, T), F32, kind="ExternalOutput").ap()
    build(nc, *args, out)
    r = run_bass_kernel_spmd(nc, [{f"in_{n}": a for n, a in arrays.items()}], core_ids=[0])
    return r.results[0]["out_y"].reshape(NIMG, C, SIDE, SIDE)
```
